# Optimizing a Trainium2 kernel written in Bass

```python
import numpy as np
import jax
import jax.numpy as jnp

def _softmax(x, axis=-1):
    return jax.nn.softmax(x, axis=axis)

def _gelu(x):
    return jax.nn.gelu(x, approximate=True)

def _silu(x):
    return jax.nn.silu(x)

def _sigmoid(x):
    return jax.nn.sigmoid(x)

def _layernorm(x, axis=-1, eps=1e-05):
    m = jnp.mean(x, axis=axis, keepdims=True)
    v = jnp.var(x, axis=axis, keepdims=True)
    return (x - m) / jnp.sqrt(v + eps)

def _scatter_add(tgt, idx, src, axis=0):
    return tgt.at[idx].add(src)

def _segment_sum(src, seg, n):
    return jax.ops.segment_sum(src, seg, n)
kernel_name = 'mk_gps_d1_gnn_r8_c8615a'

def setup_inputs(seed: int=0):
    np.random.seed(seed)
    _w = jnp.asarray

    def _rec_inputs():
        import jax
        import jax.numpy as jnp
        _gk = jax.random.key(seed)
        x = -0.0003713 + 1 * jax.random.normal(jax.random.fold_in(_gk, 1), (6250, 256), jnp.float32)
        _s = jax.random.randint(jax.random.fold_in(_gk, 2), (100000,), 0, 6250, jnp.int32)
        _d = jax.random.randint(jax.random.fold_in(_gk, 3), (100000,), 0, 6250, jnp.int32)
        _loop = jnp.arange(6250, dtype=jnp.int32)
        src = jnp.concatenate([_s, _d, _loop])
        dst = jnp.concatenate([_d, _s, _loop])
        _o = jnp.argsort(dst, stable=True)
        src = src[_o]
        dst = dst[_o]
        edge_attr_64 = 0.000189758 + 1.00013 * jax.random.normal(jax.random.fold_in(_gk, 12), (206250, 64), jnp.float32)
        return (x, src, dst, edge_attr_64)
    x, src, dst, edge_attr_64 = _rec_inputs()

    def _L0_gnn_setup():
        import jax, jax.numpy as jnp
        import numpy as np
        N_NODES = 6250
        N_EDGES = 100000
        NODE_IN = 256
        EDGE_OUT = 64
        GLOBAL_IN = 128
        NODE_OUT = 256
        HIDDEN = 512
        N_GRAPHS = 64
        key = jax.random.key(seed)
        ks = jax.random.split(key, 8)
        x = jax.random.normal(ks[0], (N_NODES, NODE_IN), dtype=jnp.float32)
        edge_index = jax.random.randint(ks[1], (2, N_EDGES), 0, N_NODES, dtype=jnp.int64)
        edge_attr = jax.random.normal(ks[2], (N_EDGES, EDGE_OUT), dtype=jnp.float32)
        u = jax.random.normal(ks[3], (N_GRAPHS, GLOBAL_IN), dtype=jnp.float32)
        batch = jnp.sort(jax.random.randint(ks[4], (N_NODES,), 0, N_GRAPHS, dtype=jnp.int64))
        in_dim = NODE_IN + EDGE_OUT + GLOBAL_IN
        b1s = 1.0 / np.sqrt(in_dim)
        b2s = 1.0 / np.sqrt(HIDDEN)
        W1 = jax.random.uniform(ks[5], (in_dim, HIDDEN), dtype=jnp.float32, minval=-b1s, maxval=b1s)
        b1 = jnp.zeros((HIDDEN,), dtype=jnp.float32)
        W2 = jax.random.uniform(ks[6], (HIDDEN, NODE_OUT), dtype=jnp.float32, minval=-b2s, maxval=b2s)
        b2 = jnp.zeros((NODE_OUT,), dtype=jnp.float32)
        return {'x': x, 'edge_index': edge_index, 'edge_attr': edge_attr, 'u': u, 'batch': batch, 'W1': W1, 'b1': b1, 'W2': W2, 'b2': b2}
    _L0_gnn_all = _L0_gnn_setup()
    _L0_gnn_in = {k: v for k, v in _L0_gnn_all.items() if k in ('u', 'W1', 'b1', 'W2', 'b2')}
    del _L0_gnn_all

    def _L0_mix_setup():
        import jax, jax.numpy as jnp
        import numpy as np
        import math
        EMBED = 256
        HEADS = 4
        HEAD_DIM = EMBED // HEADS
        OUT_DIM = 256
        LN_EPS = 1e-05

        def _qkv_init(key):
            spread = math.sqrt(3.0 / EMBED)
            gain, delta = (0.01, 0.01)
            w = jax.random.uniform(key, (EMBED, EMBED), minval=-spread, maxval=spread) * gain
            return w + delta * jnp.eye(EMBED, dtype=w.dtype)

        def _layer_norm(x, g, b):
            mu = jnp.mean(x, axis=-1, keepdims=True)
            var = jnp.mean(jnp.square(x - mu), axis=-1, keepdims=True)
            return (x - mu) * jax.lax.rsqrt(var + LN_EPS) * g + b

        def _split_heads(x, B, S):
            return x.reshape(B, S, HEADS, HEAD_DIM).transpose(0, 2, 1, 3)
        key = jax.random.key(seed)
        ks = jax.random.split(key, 6)
        seq = jax.random.normal(ks[0], (4, 1024, EMBED), dtype=jnp.float32)
        wq = _qkv_init(ks[1])
        wk = _qkv_init(ks[2])
        wv = _qkv_init(ks[3])
        bound = 1.0 / math.sqrt(EMBED)
        wo = jax.random.uniform(ks[4], (OUT_DIM, EMBED), minval=-bound, maxval=bound)
        bo = jax.random.uniform(ks[5], (OUT_DIM,), minval=-bound, maxval=bound)
        ln_k_g = jnp.ones((HEAD_DIM,), jnp.float32)
        ln_k_b = jnp.zeros((HEAD_DIM,), jnp.float32)
        ln_v_g = jnp.ones((HEAD_DIM,), jnp.float32)
        ln_v_b = jnp.zeros((HEAD_DIM,), jnp.float32)
        return {'seq': seq, 'wq': wq, 'wk': wk, 'wv': wv, 'wo': wo, 'bo': bo, 'ln_k_g': ln_k_g, 'ln_k_b': ln_k_b, 'ln_v_g': ln_v_g, 'ln_v_b': ln_v_b}
    _L0_mix_all = _L0_mix_setup()
    _L0_mix_in = {k: v for k, v in _L0_mix_all.items() if k in ('wq', 'wk', 'wv', 'wo', 'bo', 'ln_k_g', 'ln_k_b', 'ln_v_g', 'ln_v_b')}
    del _L0_mix_all

    def _L0_ffn_setup():
        import jax, jax.numpy as jnp
        import numpy as np
        E = 8
        K = 2
        D = 256
        H = 512
        DOUT = 256
        EPS = 1e-05
        key = jax.random.key(seed)
        ks = jax.random.split(key, 9)
        s = 0.02
        return {'x': jax.random.normal(ks[0], (4, 1024, D), jnp.float32), 'gamma': 1.0 + 0.05 * jax.random.normal(ks[1], (D,), jnp.float32), 'beta': 0.05 * jax.random.normal(ks[2], (D,), jnp.float32), 'Wr': 0.01 * jax.random.normal(ks[3], (D, E), jnp.float32), 'br': jnp.zeros((E,), jnp.float32), 'W1': s * jax.random.normal(ks[4], (E, D, H), jnp.float32), 'b1': s * jax.random.normal(ks[5], (E, H), jnp.float32), 'W2': s * jax.random.normal(ks[6], (E, H, DOUT), jnp.float32), 'b2': s * jax.random.normal(ks[7], (E, DOUT), jnp.float32)}
    _L0_ffn_all = _L0_ffn_setup()
    _L0_ffn_in = {k: v for k, v in _L0_ffn_all.items() if k in ('gamma', 'beta', 'Wr', 'br', 'W1', 'b1', 'W2', 'b2')}
    del _L0_ffn_all
    return {'x': x, 'src': src, 'dst': dst, 'edge_attr_64': edge_attr_64, 'L0_gnn_u': _L0_gnn_in['u'], 'L0_gnn_W1': _L0_gnn_in['W1'], 'L0_gnn_b1': _L0_gnn_in['b1'], 'L0_gnn_W2': _L0_gnn_in['W2'], 'L0_gnn_b2': _L0_gnn_in['b2'], 'L0_mix_wq': _L0_mix_in['wq'], 'L0_mix_wk': _L0_mix_in['wk'], 'L0_mix_wv': _L0_mix_in['wv'], 'L0_mix_wo': _L0_mix_in['wo'], 'L0_mix_bo': _L0_mix_in['bo'], 'L0_mix_ln_k_g': _L0_mix_in['ln_k_g'], 'L0_mix_ln_k_b': _L0_mix_in['ln_k_b'], 'L0_mix_ln_v_g': _L0_mix_in['ln_v_g'], 'L0_mix_ln_v_b': _L0_mix_in['ln_v_b'], 'L0_ffn_gamma': _L0_ffn_in['gamma'], 'L0_ffn_beta': _L0_ffn_in['beta'], 'L0_ffn_Wr': _L0_ffn_in['Wr'], 'L0_ffn_br': _L0_ffn_in['br'], 'L0_ffn_W1': _L0_ffn_in['W1'], 'L0_ffn_b1': _L0_ffn_in['b1'], 'L0_ffn_W2': _L0_ffn_in['W2'], 'L0_ffn_b2': _L0_ffn_in['b2']}

def reference(x, src, dst, edge_attr_64, L0_gnn_u, L0_gnn_W1, L0_gnn_b1, L0_gnn_W2, L0_gnn_b2, L0_mix_wq, L0_mix_wk, L0_mix_wv, L0_mix_wo, L0_mix_bo, L0_mix_ln_k_g, L0_mix_ln_k_b, L0_mix_ln_v_g, L0_mix_ln_v_b, L0_ffn_gamma, L0_ffn_beta, L0_ffn_Wr, L0_ffn_br, L0_ffn_W1, L0_ffn_b1, L0_ffn_W2, L0_ffn_b2):
    import jax
    import jax.numpy as jnp

    def _L0_gnn_ref(x, edge_index, edge_attr, u, batch, W1, b1, W2, b2):
        import jax, jax.numpy as jnp
        import numpy as np
        N_NODES = 6250
        N_EDGES = 100000
        NODE_IN = 256
        EDGE_OUT = 64
        GLOBAL_IN = 128
        NODE_OUT = 256
        HIDDEN = 512
        N_GRAPHS = 64
        n = x.shape[0]
        src = edge_index[0]
        sums = jax.ops.segment_sum(edge_attr, src, num_segments=n)
        counts = jax.ops.segment_sum(jnp.ones((edge_attr.shape[0],), edge_attr.dtype), src, num_segments=n)
        edge_attr_agg = sums / jnp.maximum(counts, 1.0)[:, None]
        u_expanded = u[batch]
        combined = jnp.concatenate([x, edge_attr_agg, u_expanded], axis=1)
        h = jax.nn.relu(combined @ W1 + b1)
        return h @ W2 + b2

    def _L0_mix_ref(seq, wq, wk, wv, wo, bo, ln_k_g, ln_k_b, ln_v_g, ln_v_b):
        import jax, jax.numpy as jnp
        import numpy as np
        import math
        EMBED = 256
        HEADS = 4
        HEAD_DIM = EMBED // HEADS
        OUT_DIM = 256
        LN_EPS = 1e-05

        def _qkv_init(key):
            spread = math.sqrt(3.0 / EMBED)
            gain, delta = (0.01, 0.01)
            w = jax.random.uniform(key, (EMBED, EMBED), minval=-spread, maxval=spread) * gain
            return w + delta * jnp.eye(EMBED, dtype=w.dtype)

        def _layer_norm(x, g, b):
            mu = jnp.mean(x, axis=-1, keepdims=True)
            var = jnp.mean(jnp.square(x - mu), axis=-1, keepdims=True)
            return (x - mu) * jax.lax.rsqrt(var + LN_EPS) * g + b

        def _split_heads(x, B, S):
            return x.reshape(B, S, HEADS, HEAD_DIM).transpose(0, 2, 1, 3)
        B, S, _ = seq.shape
        q = _split_heads(seq @ wq.T, B, S)
        k = _split_heads(seq @ wk.T, B, S)
        v = _split_heads(seq @ wv.T, B, S)
        k = _layer_norm(k, ln_k_g, ln_k_b)
        v = _layer_norm(v, ln_v_g, ln_v_b)
        kv = jnp.einsum('bhsd,bhse->bhde', k, v) / S
        ga = jnp.einsum('bhsd,bhde->bhse', q, kv)
        ga = ga.transpose(0, 2, 1, 3).reshape(B, S, EMBED)
        return ga @ wo.T + bo

    def _L0_ffn_ref(x, gamma, beta, Wr, br, W1, b1, W2, b2):
        import jax, jax.numpy as jnp
        import numpy as np
        E = 8
        K = 2
        D = 256
        H = 512
        DOUT = 256
        EPS = 1e-05
        mu = jnp.mean(x, axis=-1, keepdims=True)
        var = jnp.mean(jnp.square(x - mu), axis=-1, keepdims=True)
        xn = (x - mu) * jax.lax.rsqrt(var + EPS) * gamma + beta
        logits = jnp.einsum('bsd,de->bse', xn, Wr) + br
        top_vals, top_idx = jax.lax.top_k(logits, K)
        w = jax.nn.softmax(top_vals, axis=-1)
        w_full = jnp.einsum('bsk,bske->bse', w, jax.nn.one_hot(top_idx, E, dtype=w.dtype))
        y = jnp.zeros(x.shape[:-1] + (DOUT,), x.dtype)
        for e in range(E):
            h = jax.nn.gelu(jnp.einsum('bsd,dh->bsh', xn, W1[e]) + b1[e], approximate=False)
            y_e = jnp.einsum('bsh,hd->bsd', h, W2[e]) + b2[e]
            y = y + y_e * w_full[..., e, None]
        return y
    edge_index = jnp.stack([src, dst])
    batch0 = jnp.zeros((6250,), jnp.int32)
    xn = _layernorm(x, axis=-1)
    x = x + _L0_gnn_ref(xn, edge_index, edge_attr_64, L0_gnn_u, batch0, L0_gnn_W1, L0_gnn_b1, L0_gnn_W2, L0_gnn_b2) + _L0_mix_ref(xn[None], L0_mix_wq, L0_mix_wk, L0_mix_wv, L0_mix_wo, L0_mix_bo, L0_mix_ln_k_g, L0_mix_ln_k_b, L0_mix_ln_v_g, L0_mix_ln_v_b)[0]
    x = x + _L0_ffn_ref(_layernorm(x, axis=-1)[None], L0_ffn_gamma, L0_ffn_beta, L0_ffn_Wr, L0_ffn_br, L0_ffn_W1, L0_ffn_b1, L0_ffn_W2, L0_ffn_b2)[0]
    return x

_drawn_inputs = setup_inputs


def setup_inputs(seed=0):
    import zlib

    import numpy as np

    out = dict(_drawn_inputs(seed))
    spreads = {'L0_gnn_b1': (0.0, 0.338),
     'L0_gnn_b2': (0.0, 0.1),
     'L0_mix_ln_k_g': (1.0, 0.6),
     'L0_mix_ln_k_b': (0.0, 0.8),
     'L0_mix_ln_v_g': (1.0, 0.6),
     'L0_mix_ln_v_b': (0.0, 0.8),
     'L0_ffn_br': (0.0, 0.1)}
    factors = {'edge_attr_64': 3.52,
     'L0_mix_wq': 8.0,
     'L0_mix_wk': 8.0,
     'L0_mix_wv': 8.0,
     'L0_mix_wo': 8.0,
     'L0_ffn_gamma': 6.365,
     'L0_ffn_beta': 5.206,
     'L0_ffn_b1': 34.071,
     'L0_ffn_b2': 4.371,
     'L0_mix_bo': 3.693}
    for name, (base, spread) in spreads.items():
        noise = np.random.default_rng([zlib.crc32(name.encode()), seed]).standard_normal(out[name].shape)
        drawn = base * np.exp(spread * noise) if base else spread * noise
        out[name] = jnp.asarray(drawn.astype(out[name].dtype))
    for name, factor in factors.items():
        out[name] = (out[name] * factor).astype(out[name].dtype)
    return out
```

```python
from contextlib import ExitStack, contextmanager

import concourse.bass as bass
from concourse import mybir

ALU = mybir.AluOpType
ACT = mybir.ActivationFunctionType
AX_X = mybir.AxisListType.X
F32 = mybir.dt.float32
BF16 = mybir.dt.bfloat16
I32 = mybir.dt.int32
U32 = mybir.dt.uint32

N = 6250
D = 256
EA = 64
HID = 512
HEADS, HD = 4, 64
NE = 8
EPS = 1e-5

P = 125
NT = N // P
KC = D // 128
HC = HID // 128

E = 206250
EC = E // P
SEGS = 10
SC = EC // SEGS
STEPS = 5
SLOTS = 3
CH = SC // (STEPS * SLOTS)
NB = 25
BN = N // NB
UR = 256
GROUPS = 11
NU = 2 * GROUPS * STEPS
assert (SC * P + NB * (UR - 1)) // UR <= NU
SEG_ROWS = NU * UR
ROW = EA + 2
AGG = 2 * (EA + 1)
CREDIT = GROUPS
STEP_OFF = -(-2 * GROUPS // 4) * 4
PREFIX_STEP = 3
PREFIX = 1
OH = 256
FILLS = 30


K = 2
TR = 128
ET = (N * K + NE * (TR - 1)) // TR + 1
ET += ET % 2
MOVE = 5
BIG = 3.0e38


class Steps:

    def __init__(self, eng, sem):
        self.eng, self.sem, self.base, self.k = eng, sem, 0, 0

    def did(self, ins):
        ins.then_inc(self.sem, 1)
        self.k += 1

    def wait(self):
        self.eng.wait_ge(self.sem, self.base + self.k)

    @contextmanager
    def loop(self, start, end, per):
        with self.eng.Fori(start, end) as i:
            base, k = self.base, self.k
            self.base, self.k = base + k + (i - start) * per, 0
            yield i
            assert self.k == per, (self.k, per)
            self.base, self.k = base, k + (end - start) * per


def build(nc, x, src, edge_attr, gnn_u, gnn_W1, gnn_b1, gnn_W2, gnn_b2,
          wq, wk, wv, wo, bo, k_g, k_b, v_g, v_b, gamma, beta, Wr, br, W1, b1, W2, b2,
          out, buckets, x1, sorted_y, expert_out):
    with ExitStack() as ctx:
        def sb(name, shape, dt=F32):
            return ctx.enter_context(nc.sbuf_tensor(name, shape, dt))

        def psum(name, shape, dt=F32):
            return ctx.enter_context(nc.psum_tensor(name, shape, dt))

        def sem(name):
            return ctx.enter_context(nc.semaphore(name))

        x_or_xnT = sb("x_or_xnT", [128, NT * D])
        xs = x_or_xnT[0:P, :].rearrange("p (j d) -> p j d", d=D)
        xnT = x_or_xnT[:, :].rearrange("p (j c n) -> p j c n", c=KC, n=128)[:, :, :, 0:P]
        agg = sb("agg", [P, NB + 1, AGG])
        arena = sb("arena", [128, 19000])
        arena2 = sb("arena2", [128, 8000])

        def carver(store, at=0):
            at = [at]
            return lambda shape, dt=F32: carve(store, at, shape, dt)

        def carve(store, at, shape, dt):
            size = 1
            for n in shape[1:]:
                size *= n
            words = size if dt != BF16 else (size + 1) // 2
            view = store[0:shape[0], at[0]:at[0] + words]
            at[0] += words
            assert at[0] <= store.shape[1], at[0]
            if dt != F32:
                view = view.bitcast(dt)[:, 0:size]
            names = " ".join("abcd"[:len(shape) - 1])
            return view.rearrange(f"p ({names}) -> p {names}",
                                  **{n: m for n, m in zip("abcd", shape[1:])}) if len(shape) > 2 else view

        part = carver(arena)
        part2 = carver(arena2)

        w_kv = part2([128, KC, 2 * D])
        w_q = part2([128, KC, D])
        w_oT = part2([128, KC, D])
        w1x = sb("w1x", [128, KC, HID])
        w1e = sb("w1e", [EA, HID])
        w1u = sb("w1u", [128, HID])
        w2 = sb("w2", [128, HC, D])
        u_col = sb("u_col", [128, 1])
        b1_row = sb("b1_row", [1, HID])
        h_bias = sb("h_bias", [128, HC])
        bias_rows = sb("bias_rows", [1, 2, D])
        gkv = sb("gkv", [P, 2, HD])
        bkv = sb("bkv", [P, 2, HD])
        mix_w = part2([128, KC, D])
        kv_sb = part2([128, KC, 128])
        kvo = part2([128, KC, D])
        ident = sb("ident", [128, 128])
        ones = sb("ones", [P, P])
        below = sb("below", [P, P])
        node_iota = sb("node_iota", [128, OH], BF16)
        bucket_iota = sb("bucket_iota", [P, NB], BF16)
        unit_start = sb("unit_start", [1, NU])
        seg_start = sb("seg_start", [P, SEGS])
        spare = sb("spare", [1, 16])
        eps_col = sb("eps_col", [P, 1])
        zeros = sb("zeros", [128, SEG_ROWS * ROW // 128 // FILLS])
        pos = part([P, EC], I32)
        local = part([P, EC], BF16)
        mask = part([P, NB, SC], BF16)
        count = part([P, NB, SC])
        filled = mask[:, :, :].rearrange("p b t -> p (b t)")[0:1, 0:NU * NB].rearrange("p (u b) -> p u b", b=NB)
        kq = sb("kq", [P, SC], I32)
        kf = sb("kf", [P, 4, SC])
        hist = sb("hist", [P, NB])
        rk = sb("rk", [P, 8, NB])
        rk_i = sb("rk_i", [P, NB], I32)
        ustart_f = sb("ustart_f", [1, NU])
        agg_off = sb("agg_off", [1, SEGS * STEPS * STEP_OFF], I32)
        stage = part([P, SLOTS, CH, EA])
        rows = part([P, SLOTS, CH, ROW])
        rows_at = sb("rows_at", [P, SLOTS, CH], I32)
        unit = part([128, GROUPS, 4, ROW])
        unit_hi = unit.rearrange("p k j f -> p (k j f)").bitcast(BF16)\
            .rearrange("p (k j f h) -> p k j f h", k=GROUPS, j=4, h=2)[:, :, :, :, 1]
        rest = part([128, 3, 4, ROW])
        rest_hi = rest.rearrange("p k j f -> p (k j f)").bitcast(BF16)\
            .rearrange("p (k j f h) -> p k j f h", k=3, j=4, h=2)[:, :, :, :, 1]
        rest_lo = part([128, 3, 4, ROW], BF16)
        raw = part([128, 3, KC, D])
        onehot = raw.rearrange("p n c d -> p (n c d)").bitcast(BF16).rearrange("p (k j n) -> p k j n", k=3, j=4)
        xt = part2([P, 2, D])
        xn = part2([P, 2, D])
        xnT_t = part2([128, 2, KC, P])
        stats = sb("stats", [P, NT, 6])
        mv = sb("mv", [P, NT, 2])
        sd = sb("sd", [P, NT])
        rstd = sb("rstd", [P, NT])
        sq = part2([P, 2 * D])
        ss = sb("ss", [P, 8])
        hsd = sb("hsd", [P, 8])
        hrs = sb("hrs", [P, 8])
        kvn = part2([P, 2, 2 * D])
        csum = sb("csum", [128, KC, 8])

        part2 = carver(arena2)
        logits = part2([P, NT, NE])
        W1_all = arena[:, 0:NE * KC * HID]
        W2_all = arena[:, NE * KC * HID:NE * (KC * HID + HC * D)]
        x1t = part2([P, 2, 2, D])
        cnt = sb("cnt", [P, 2])
        rcnt = sb("rcnt", [P, 2])
        aggn = part2([P, 2, EA])
        aggT = part2([EA, 2, P])
        hT = part2([128, HC, 2, P])
        st = sb("st", [P, 2, 6])
        mv2 = sb("mv2", [P, 2, 2])
        sd2 = sb("sd2", [P, 2])
        rs2 = sb("rs2", [P, 2])
        y1 = part2([P, 2, D])
        y2 = part2([P, 2, D])
        ynT = part2([128, 2, KC, P])
        w_r = sb("w_r", [128, KC, NE])
        br_row = sb("br_row", [1, NE])
        gb_rows = sb("gb_rows", [1, 2, D])
        gb_col = sb("gb_col", [128, 2, KC])

        part2 = carver(arena2, NT * NE)
        best = part2([P, NE, K * NT])
        at = part2([P, NE, K * NT])
        left = part2([P, NT, NE])
        tmp = part2([P, NT, NE])
        top = part2([P, 2, 4, NT])
        b1_rows = arena2[:, arena2.shape[1] - NE * HID:]
        assert NT * NE + 2 * NE * K * NT + 2 * NT * NE + 8 * NT <= arena2.shape[1] - NE * HID
        b2_rows = arena[:, NE * (KC * HID + HC * D):NE * (KC * HID + HC * D) + NE * D]
        expert_iota = sb("expert_iota", [P, NE])
        tile_start = sb("tile_start", [1, ET])
        part4 = carver(agg[:, :, :].rearrange("p b f -> p (b f)"))
        send = part4([P, MOVE, D])
        send_at = sb("send_at", [P, MOVE, K], I32)
        place = part4([P, K, NT], I32)
        weight = part4([P, K, NT])
        ended = part4([1, ET, NE])
        expert_f = part4([1, ET])
        expert = part4([1, ET], I32)
        part3 = carver(x_or_xnT)
        row_in = part3([128, 2, D])
        zT = part3([128, 2, KC, TR])
        hb = part3([128, 2, HID])
        hg = part3([128, 2, HID])
        hgT = part3([128, 2, HC, TR])
        y_out = part3([128, 2, D])
        fetched = part3([P, MOVE, K, D])
        res = part3([P, MOVE, D])

        ps_rank = psum("ps_rank", [128, 512])
        ps_t = psum("ps_t", [128, 512])
        ps_kv = psum("ps_kv", [128, 512])
        ps_acc = [psum(f"ps_acc{c}", [128, 512]) for c in range(KC)]
        ps_y = (ps_kv, ps_rank)
        ps_g = [psum(f"ps_g{k}", [128, 512]) for k in range(3)]

        s_src = sem("s_src")
        s_x = sem("s_x")
        s_w = sem("s_w")
        s_prefill = sem("s_prefill")
        s_stage = [sem(f"s_stage{k}") for k in range(SLOTS)]
        s_scat = [sem(f"s_scat{k}") for k in range(SLOTS)]
        s_copied = sem("s_copied")
        s_meta = sem("s_meta")
        s_const = sem("s_const")
        s_cst2 = sem("s_cst2")
        s_unit = [sem(f"s_unit{k}") for k in range(GROUPS)]
        s_hist = sem("s_hist")
        s_prefix = sem("s_prefix")
        s_rank = sem("s_rank")
        s_onehot = sem("s_onehot")
        s_group = sem("s_group")
        s_added = sem("s_added")
        s_dve = sem("s_dve")
        s_act = sem("s_act")
        s_stats = sem("s_stats")
        s_sd = sem("s_sd")
        s_wT = sem("s_wT")
        s_wTc = sem("s_wTc")
        s_wkv = sem("s_wkv")
        s_xn = sem("s_xn")
        s_xt = sem("s_xt")
        s_xtc = sem("s_xtc")
        s_kvp = sem("s_kvp")
        s_sq = sem("s_sq")
        s_ss = sem("s_ss")
        s_hsd = sem("s_hsd")
        s_kvn = sem("s_kvn")
        s_kvacc = sem("s_kvacc")
        s_kvsb = sem("s_kvsb")
        s_kvo = sem("s_kvo")
        s_kvoc = sem("s_kvoc")
        s_mixw = sem("s_mixw")
        s_mixwc = sem("s_mixwc")
        s_x2 = sem("s_x2")
        s_mix = sem("s_mix")
        s_mixed = sem("s_mixed")
        s_hb = sem("s_hb")
        s_hbc = sem("s_hbc")
        s_out = sem("s_out")
        s_gw = sem("s_gw")
        s_gb = sem("s_gb")
        s_gbc = sem("s_gbc")
        s_we = sem("s_we")
        s_x1in = [sem(f"s_x1in{a}") for a in range(2)]
        s_x1out = sem("s_x1out")
        s_aggn = sem("s_aggn")
        s_aggt = sem("s_aggt")
        s_aggtc = sem("s_aggtc")
        s_h = sem("s_h")
        s_relu = sem("s_relu")
        s_o = sem("s_o")
        s_x1done = sem("s_x1done")
        s_mv2 = sem("s_mv2")
        s_sd2 = sem("s_sd2")
        s_yn = sem("s_yn")
        s_keep = sem("s_keep")
        s_yt = sem("s_yt")
        s_ytc = sem("s_ytc")
        s_lg = sem("s_lg")
        s_lgc = sem("s_lgc")
        s_xt2 = [sem(f"s_xt2{a}") for a in range(2)]
        s_x1 = sem("s_x1")
        s_sortfill = sem("s_sortfill")
        s_b1 = sem("s_b1")
        s_chist = sem("s_chist")
        s_cprefix = sem("s_cprefix")
        s_diff = sem("s_diff")
        s_exp = sem("s_exp")
        s_place = sem("s_place")
        s_staged = sem("s_staged")
        s_sent = [sem(f"s_sent{m}") for m in range(MOVE)]
        s_rowin = [sem(f"s_rowin{a}") for a in range(2)]
        s_zt = sem("s_zt")
        s_ztc = sem("s_ztc")
        s_eh = sem("s_eh")
        s_ehb = sem("s_ehb")
        s_gelu = sem("s_gelu")
        s_gt = sem("s_gt")
        s_gtc = sem("s_gtc")
        s_ey = sem("s_ey")
        s_eyb = sem("s_eyb")
        s_eout = [sem(f"s_eout{a}") for a in range(2)]
        s_cat = sem("s_cat")
        s_fetch = [sem(f"s_fetch{m}") for m in range(MOVE)]
        s_res = [sem(f"s_res{m}") for m in range(MOVE)]
        s_comb = sem("s_comb")
        s_final = [sem(f"s_final{m}") for m in range(MOVE)]

        ea_v = edge_attr.rearrange("(p t) f -> p (t f)", p=P)
        buck_fill = buckets.rearrange("(s p q) f -> s p (q f)", s=SEGS, p=128)
        buck_units = buckets.rearrange("(g u p j) f -> g p u (j f)", u=2, p=128, j=2)
        ZW = SEG_ROWS * ROW // 128 // FILLS
        SFILLS = 64
        SW = ET * D // SFILLS
        assert SW * SFILLS == ET * D and SW <= ZW
        NCONST = 12

        block = ctx.enter_context(nc.Block())

        def wait_apart(eng, sem, value):
            if not isinstance(value, int):
                value = eng.to_reg(value)
            eng.wait_ge(s_const, NCONST)
            eng.wait_ge(sem, value)

        def after(eng, sem, value):
            if not (isinstance(value, int) and value <= 0):
                eng.wait_ge(sem, value)

        def pairwise(eng, step, last):
            for a in range(2):
                step(a, a, 0)
            with eng.Fori(1, last // 2) as i:
                for a in range(2):
                    step(2 * i + a, a, i)

        @block.sync
        def _(sp):
            def load_chunk(k, col):
                src_cols = ea_v[:, bass.ds(col * EA, CH * EA)]
                dst = stage[:, k].rearrange("p c f -> p (c f)")
                sp.dma_start(dst[0:112, :], src_cols[0:112, :]).then_inc(s_stage[k], 16)
                sp.dma_start(dst[112:P, :], src_cols[112:P, :]).then_inc(s_stage[k], 16)

            def prefill(s):
                if not isinstance(s, int) or s > 0:
                    sp.wait_ge(s_prefill, s * (FILLS * 16))
                for q in range(FILLS):
                    sp.dma_start(buck_fill[bass.ds(s, 1), :, q * ZW:(q + 1) * ZW].rearrange("s p q -> (s p) q"),
                                 zeros[:, :]).then_inc(s_prefill, 16)

            def load_unit(g, k):
                sp.wait_ge(s_group, g + 1)
                sp.dma_start(unit[:, k].rearrange("p (u j) f -> p u (j f)", u=2),
                             buck_units[bass.ds(g, 1)].rearrange("g p u q -> (g p) u q")).then_inc(s_unit[k], 16)

            sp.dma_start(pos[:, :], src.rearrange("(p t) -> p t", p=P)).then_inc(s_src, 16)
            for k in range(SLOTS):
                load_chunk(k, k * CH)
            sp.wait_ge(s_const, 1)
            prefill(0)
            for a in range(5):
                sp.dma_start(xs[:, 10 * a:10 * a + 10, :],
                             x.rearrange("(t p) d -> p t d", p=P)[:, 10 * a:10 * a + 10, :]).then_inc(s_x, 16)

            def load(dst, src_ap):
                sp.dma_start(dst, src_ap).then_inc(s_w, 16)
            for n, w in enumerate((wk, wv, wo)):
                load(raw[:, n], w.rearrange("(c p) i -> p c i", p=128))
            load(w_q[:, :, :], wq.rearrange("(c p) i -> p c i", p=128))
            load(w1x[:, :, :], gnn_W1[0:D, :].rearrange("(c p) h -> p c h", p=128))
            load(w1e[:, :], gnn_W1[D:D + EA, :])
            load(w1u[:, :], gnn_W1[D + EA:, :])
            load(w2[:, :, :], gnn_W2.rearrange("(c p) d -> p c d", p=128))
            load(u_col[:, :], gnn_u[0, :].rearrange("(p a) -> p a", a=1))
            load(b1_row[:, :], gnn_b1.rearrange("(a d) -> a d", a=1))
            load(bias_rows[0:1, 0, :], bo.rearrange("(a d) -> a d", a=1))
            load(bias_rows[0:1, 1, :], gnn_b2.rearrange("(a d) -> a d", a=1))
            load(gkv[:, 0, :], k_g.rearrange("(a d) -> a d", a=1).to_broadcast([P, HD]))
            load(gkv[:, 1, :], v_g.rearrange("(a d) -> a d", a=1).to_broadcast([P, HD]))
            load(bkv[:, 0, :], k_b.rearrange("(a d) -> a d", a=1).to_broadcast([P, HD]))
            load(bkv[:, 1, :], v_b.rearrange("(a d) -> a d", a=1).to_broadcast([P, HD]))

            x_tiles = x.rearrange("(j p) d -> j p d", p=P)
            x1_tiles = x1.rearrange("(j p) d -> j p d", p=P)

            def load_g(dst, src_ap):
                sp.dma_start(dst, src_ap).then_inc(s_gw, 16)
            load_g(w_r[:, :, :], Wr.rearrange("(c p) e -> p c e", p=128))
            load_g(br_row[:, :], br.rearrange("(a e) -> a e", a=1))
            load_g(gb_rows[0:1, 0, :], gamma.rearrange("(a d) -> a d", a=1))
            load_g(gb_rows[0:1, 1, :], beta.rearrange("(a d) -> a d", a=1))

            def step(s, i, units, last=False, mix2=False):
                j = (s - SEGS // 2) * (2 * STEPS) + i * 2
                if mix2:
                    for a in range(2):
                        sp.wait_ge(s_x1, (j + 1) * 16)
                        sp.dma_start(xt[:, a, :], x_tiles[bass.ds(j + a, 1)].rearrange("a p d -> (a p) d"))\
                            .then_inc(s_xt2[a], 16)
                if not last:
                    for k in range(SLOTS):
                        sp.wait_ge(s_copied, s * (STEPS * SLOTS) + i * SLOTS + k + 1)
                        load_chunk(k, s * SC + (i * SLOTS + SLOTS + k) * CH)
                if units:
                    for k in range(GROUPS):
                        load_unit((s - 1) * (STEPS * GROUPS) + i * GROUPS + k, k)
                if mix2:
                    for a in range(2):
                        sp.wait_ge(s_mixed, j + a + 2)
                        sp.dma_start(x1_tiles[bass.ds(j + a, 1)].rearrange("a p d -> (a p) d"), xt[:, a, :])\
                            .then_inc(s_x1, 16)

            def scattered(s):
                for k in range(SLOTS):
                    value = (s + 1) * (STEPS * CH * 16)
                    if isinstance(s, int):
                        sp.wait_ge(s_scat[k], value)
                    else:
                        wait_apart(sp, s_scat[k], value)

            prefill(1)
            with sp.Fori(0, STEPS) as i:
                step(0, i, False)
            for first, end in ((1, SEGS // 2), (SEGS // 2, SEGS - 1)):
                with sp.Fori(first, end) as s:
                    prefill(s + 1)
                    scattered(s - 1)
                    with sp.Fori(0, STEPS) as i:
                        step(s, i, True, mix2=first > 1)
            scattered(SEGS - 2)
            with sp.Fori(0, STEPS - 1) as i:
                step(SEGS - 1, i, True, mix2=True)
            step(SEGS - 1, STEPS - 1, True, last=True, mix2=True)
            scattered(SEGS - 1)
            with sp.Fori(0, STEPS) as i:
                step(SEGS, i, True, last=True)
            sp.wait_ge(s_x1, (NT + 1) * 16)
            x1_pairs = x1.rearrange("(b t p) d -> b p t d", p=P, t=2)

            def load_x1(b, a):
                sp.dma_start(x1t[:, a], x1_pairs[bass.ds(b, 1)].rearrange("b p t d -> (b p) t d")).then_inc(s_x1in[a], 16)

            def store_x1(b, a):
                sp.wait_ge(s_x1done, b + 1)
                sp.dma_start(x1_pairs[bass.ds(b, 1)].rearrange("b p t d -> (b p) t d"), x1t[:, a]).then_inc(s_x1out, 16)
                sp.wait_ge(s_x1out, (b + 1) * 16)
                wait_apart(sp, s_mv2, b * 2 + 2)

            load_x1(0, 0)
            load_x1(1, 1)
            sp.wait_ge(s_added, 2 + SEGS * STEPS * GROUPS)
            for c in range(KC):
                sp.dma_start(W1_all.rearrange("p (e c h) -> p e c h", c=KC, h=HID)[:, :, c, :],
                             W1.rearrange("e (c p) h -> p e c h", p=128)[:, :, c, :]).then_inc(s_we, 16)
            for c in range(HC):
                sp.dma_start(W2_all.rearrange("p (e c d) -> p e c d", c=HC, d=D)[:, :, c, :],
                             W2.rearrange("e (c p) d -> p e c d", p=128)[:, :, c, :]).then_inc(s_we, 16)
            sp.dma_start(b2_rows, b2.rearrange("(a e) d -> a (e d)", a=1).to_broadcast([128, NE * D])).then_inc(s_we, 16)
            for q in range(SFILLS):
                sp.dma_start(sorted_y.rearrange("(p q) d -> p (q d)", p=128)[:, q * SW:(q + 1) * SW],
                             zeros[:, 0:SW]).then_inc(s_sortfill, 16)
            with sp.Fori(0, NB // 2 - 1) as i:
                for a in range(2):
                    store_x1(2 * i + a, a)
                    load_x1(2 * i + a + 2, a)
            for a in range(2):
                store_x1(NB - 3 + a, a)
                if a == 0:
                    load_x1(NB - 1, 0)
            store_x1(NB - 1, 0)
            sp.wait_ge(s_lgc, NT + 1)
            sp.dma_start(b1_rows, b1.rearrange("(a e) h -> a (e h)", a=1).to_broadcast([128, NE * HID])).then_inc(s_b1, 16)
            for m in range(MOVE):
                sp.wait_ge(s_sent[m], NT // MOVE * K * 16)
            row_tiles = sorted_y.rearrange("(r p) d -> r p d", p=TR)
            out_tiles = expert_out.rearrange("(r p) d -> r p d", p=TR)

            def load_rows(r, a):
                sp.dma_start(row_in[:, a, :], row_tiles[bass.ds(r, 1)].rearrange("a p d -> (a p) d"))\
                    .then_inc(s_rowin[a], 16)

            def store_rows(r, a):
                sp.wait_ge(s_eyb, r + 1)
                sp.dma_start(out_tiles[bass.ds(r, 1)].rearrange("a p d -> (a p) d"), y_out[:, a, :])\
                    .then_inc(s_eout[a], 16)

            def expert_rows(r, a, i):
                sp.wait_ge(s_zt, r + 1)
                load_rows(r + 2, a)
                store_rows(r, a)

            for a in range(2):
                load_rows(a, a)
            pairwise(sp, expert_rows, ET - 2)
            for a in range(2):
                store_rows(ET - 2 + a, a)

            def combine(i):
                for m in range(MOVE):
                    after(sp, s_final[m], i * 16)
                    sp.dma_start(res[:, m, :], x1_tiles[bass.ds(i * MOVE + m, 1)].rearrange("a p d -> (a p) d"))\
                        .then_inc(s_res[m], 16)
                for m in range(MOVE):
                    sp.wait_ge(s_comb, i * MOVE + m + 1)
                    sp.dma_start(out_nodes[bass.ds(i * MOVE + m, 1)].rearrange("a p d -> (a p) d"), res[:, m, :])\
                        .then_inc(s_final[m], 16)

            out_nodes = out.rearrange("(j p) d -> j p d", p=P)
            combine(0)
            with sp.Fori(1, NT // MOVE) as i:
                combine(i)
            for m in range(MOVE):
                sp.wait_ge(s_final[m], NT // MOVE * 16)

        @block.gpsimd
        def _(pool):
            pool.memset(zeros[:, :], 0.0).then_inc(s_const, 1)
            for k, (free, n) in enumerate([(s_x1, 16), (s_mixed, 1), (s_ss, 1), (s_mix, 1), (s_xt, 1), (s_kvacc, 1),
                                           (s_ytc, 1), (s_lgc, 1), (s_yt, 1), (s_keep, 1)]):
                pool.memset(spare[0:1, k:k + 1], 0.0).then_inc(free, n)
            pool.memset(ident[:, :], 0.0).then_inc(s_cst2, 1)
            pool.memset(below[:, :], 0.0).then_inc(s_cst2, 1)
            pool.memset(eps_col[:, :], EPS).then_inc(s_const, 1)
            pool.memset(ones[:, :], 1.0).then_inc(s_const, 1)
            pool.memset(rows[:, :, :, :], 1.0).then_inc(s_const, 1)
            pool.iota(node_iota[:, :], [[1, OH]], base=0, channel_multiplier=0,
                      allow_small_or_imprecise_dtypes=True).then_inc(s_const, 1)
            pool.iota(bucket_iota[:, :], [[1, NB]], base=0, channel_multiplier=0,
                      allow_small_or_imprecise_dtypes=True).then_inc(s_const, 1)
            pool.iota(unit_start[:, :], [[UR, NU]], base=0, channel_multiplier=0,
                      allow_small_or_imprecise_dtypes=True).then_inc(s_const, 1)
            pool.iota(expert_iota[:, :], [[1, NE]], base=0, channel_multiplier=0,
                      allow_small_or_imprecise_dtypes=True).then_inc(s_const, 1)
            pool.iota(tile_start[:, :], [[TR, ET]], base=0, channel_multiplier=0,
                      allow_small_or_imprecise_dtypes=True).then_inc(s_const, 1)
            pool.iota(rk_i[:, 0:SEGS], [[SEG_ROWS // 128, SEGS]], base=0, channel_multiplier=0).then_inc(s_cst2, 1)
            pool.wait_ge(s_cst2, 3)
            pool.affine_select(out=ident[:, :], in_=ident[:, :], compare_op=ALU.not_equal, fill=1.0,
                               base=0, pattern=[[-1, 128]], channel_multiplier=1).then_inc(s_const, 1)
            pool.affine_select(out=below[:, :], in_=below[:, :], compare_op=ALU.is_ge, fill=1.0,
                               base=0, pattern=[[-1, P]], channel_multiplier=1).then_inc(s_const, 1)
            pool.tensor_scalar(seg_start[:, :], rk_i[:, 0:SEGS], 128.0, 0.0, ALU.mult, ALU.add).then_inc(s_const, 1)
            with pool.Fori(0, SEGS) as s:
                wait_apart(pool, s_prefill, (s + 1) * (FILLS * 16))
                with pool.Fori(0, STEPS) as i:
                    for k in range(SLOTS):
                        c = s * (STEPS * SLOTS) + i * SLOTS + k
                        pool.wait_ge(s_copied, c + 1)
                        wait_apart(pool, s_meta, (c + 1) * 2)
                        for e in range(CH):
                            pool.indirect_dma_start(buckets[:, :], bass.IndirectOffsetOnAxis(rows_at[:, k, e:e + 1], 0),
                                                    rows[:, k, e, :], None).then_inc(s_scat[k], 16)

            pool.wait_ge(s_sortfill, SFILLS * 16)

            def dispatch(i):
                for m in range(MOVE):
                    wait_apart(pool, s_staged, (i * MOVE + m + 1) * 2)
                    for k in range(K):
                        pool.indirect_dma_start(sorted_y[:, :], bass.IndirectOffsetOnAxis(send_at[:, m, k:k + 1], 0),
                                                send[:, m, :], None).then_inc(s_sent[m], 16)

            with pool.Fori(0, NT // MOVE) as i:
                dispatch(i)
            for a in range(2):
                pool.wait_ge(s_eout[a], ET // 2 * 16)

            def fetch(i):
                for m in range(MOVE):
                    if not isinstance(i, int):
                        wait_apart(pool, s_comb, (i - 1) * MOVE + m + 1)
                    wait_apart(pool, s_cat, i * MOVE + m + 1)
                    for k in range(K):
                        pool.indirect_dma_start(fetched[:, m, k, :], None, expert_out[:, :],
                                                bass.IndirectOffsetOnAxis(send_at[:, m, k:k + 1], 0)).then_inc(s_fetch[m], 16)

            fetch(0)
            with pool.Fori(1, NT // MOVE) as i:
                fetch(i)

        @block.scalar
        def _(act):
            did = Steps(act, s_act)
            act.wait_ge(s_const, NCONST)
            for n in range(3):
                act.wait_ge(s_wT, n + 1)
                dst = (w_kv[:, :, 0:D], w_kv[:, :, D:2 * D], w_oT[:, :, :])[n]
                nc.scalar.copy(dst, ps_t[:, :].rearrange("p (c d) -> p c d", c=KC)).then_inc(s_wTc, 1)

            def chunk(s, i, k):
                c = s * (STEPS * SLOTS) + i * SLOTS + k
                n = s * STEPS + i
                act.wait_ge(s_stage[k], (n + 1) * 32)
                after(act, s_scat[k], n * (CH * 16))
                nc.scalar.copy(rows[:, k, :, 0:EA], stage[:, k, :, :]).then_inc(s_copied, 1)
                col = s * SC + (i * SLOTS + k) * CH
                nc.scalar.copy(rows[:, k, :, EA + 1:ROW],
                               local[:, bass.ds(col, CH)].rearrange("p (c a) -> p c a", a=1)).then_inc(s_meta, 1)
                nc.scalar.copy(rows_at[:, k, :], pos[:, bass.ds(col, CH)]).then_inc(s_meta, 1)

            def pass1(j, a):
                act.wait_ge(s_xt, j + 2)
                pt = ps_t[:, 0:KC * P].rearrange("p (c n) -> p c n", c=KC)
                nc.scalar.copy(xnT_t[:, a], pt).then_inc(s_xtc, 1)
                nc.scalar.copy(xnT[:, bass.ds(j, 1)].rearrange("p a c n -> p (a c) n"), pt).then_inc(s_xtc, 1)
                act.wait_ge(s_kvp, j + 1)
                act.wait_ge(s_ss, j + 1)
                nc.scalar.activation(sq[:, :], ps_kv[0:P, :], ACT.Square).then_inc(s_sq, 1)
                act.wait_ge(s_ss, j + 2)
                nc.scalar.activation(hsd[:, :], ss[:, :], ACT.Sqrt, bias=eps_col[:, :], scale=1.0 / HD).then_inc(s_hsd, 1)

            def pass2(j, a):
                act.wait_ge(s_mix, j + 1)
                nc.scalar.copy(xnT_t[:, a], xnT[:, bass.ds(j, 1)].rearrange("p a c n -> p (a c) n")).then_inc(s_x2, 1)

            def step(s, i, mix, rank_first=False):
                for k in range(SLOTS):
                    chunk(s, i, k)
                for a in range(2):
                    if mix == 1:
                        pass1(s * (2 * STEPS) + i * 2 + a, a)
                    else:
                        pass2((s - SEGS // 2) * (2 * STEPS) + i * 2 + a, a)

            act.wait_ge(s_stats, 1)
            nc.scalar.activation(sd[:, :], mv[:, :, 1], ACT.Sqrt, bias=eps_col[:, :]).then_inc(s_sd, 1)
            act.wait_ge(s_hb, 1)
            nc.scalar.activation(h_bias[:, :], ps_kv[:, 0:HC], ACT.Copy).then_inc(s_hbc, 1)
            act.wait_ge(s_rank, 1)
            step(0, 0, 1)
            with act.Fori(1, STEPS) as i:
                step(0, i, 1)
            with act.Fori(1, SEGS // 2) as s:
                act.wait_ge(s_rank, s + 1)
                with act.Fori(0, STEPS) as i:
                    step(s, i, 1)
            for c in range(KC):
                act.wait_ge(s_kvo, KC)
                nc.scalar.copy(kvo[:, c, :], ps_t[:, c * D:(c + 1) * D]).then_inc(s_kvoc, 1)
            for c in range(KC):
                act.wait_ge(s_mixw, KC)
                nc.scalar.copy(mix_w[:, c, :], ps_kv[:, c * D:(c + 1) * D]).then_inc(s_mixwc, 1)
            with act.Fori(SEGS // 2, SEGS) as s:
                act.wait_ge(s_rank, s + 1)
                with act.Fori(0, STEPS) as i:
                    step(s, i, 2)
            act.wait_ge(s_gb, 1)
            nc.scalar.copy(gb_col[:, :, :], ps_t[:, 0:2 * KC].rearrange("p (n c) -> p n c", n=2)).then_inc(s_gbc, 1)

            def network(b):
                act.wait_ge(s_aggt, b + 1)
                nc.scalar.copy(aggT[:, :, :], ps_rank[0:EA, 0:2 * P].rearrange("p (t n) -> p t n", t=2)).then_inc(s_aggtc, 1)
                for hc in range(HC):
                    act.wait_ge(s_h, b * 2 + hc // 2 + 1)
                    act_in = ps_acc[hc // 2][:, (hc % 2) * BN:(hc % 2 + 1) * BN]
                    nc.scalar.activation(hT[:, hc].rearrange("p t n -> p (t n)"), act_in, ACT.Relu,
                                         bias=h_bias[:, hc:hc + 1]).then_inc(s_relu, 1)
                for r in range(2):
                    act.wait_ge(s_mv2, b * 2 + r + 1)
                    nc.scalar.activation(sd2[:, :], mv2[:, :, 1], ACT.Sqrt, bias=eps_col[:, :]).then_inc(s_sd2, 1)

            def router(b):
                act.wait_ge(s_yn, b * 2 + 2)
                nc.scalar.copy(xs[:, bass.ds(b * 2, 2), :], y2[:, :, :]).then_inc(s_keep, 1)
                for a in range(2):
                    act.wait_ge(s_yt, b * 2 + a + 2)
                    for c in range(KC):
                        nc.scalar.activation(ynT[:, a, c, :], ps_t[:, c * P:(c + 1) * P], ACT.Identity,
                                             scale=gb_col[:, 0, c:c + 1], bias=gb_col[:, 1, c:c + 1]).then_inc(s_ytc, 1)
                    act.wait_ge(s_lg, b * 2 + a + 1)
                    nc.scalar.copy(logits[:, bass.ds(b * 2 + a, 1), :].rearrange("p a e -> p (a e)"),
                                   ps_kv[0:P, 0:NE]).then_inc(s_lgc, 1)

            network(0)
            with act.Fori(1, NB) as b:
                network(b)
                router(b - 1)
            router(NB - 1)
            act.wait_ge(s_diff, 1)
            nc.scalar.activation(top[:, 1, 1, :], top[:, 1, 0, :], ACT.Exp).then_inc(s_exp, 1)

            def stage_rows(i):
                for m in range(MOVE):
                    after(act, s_sent[m], i * (K * 16))
                    t = i * MOVE + m
                    nc.scalar.copy(send[:, m, :], xs[:, bass.ds(t, 1), :].rearrange("p a d -> p (a d)")).then_inc(s_staged, 1)
                    nc.scalar.copy(send_at[:, m, :], place[:, :, bass.ds(t, 1)].rearrange("p k a -> p (k a)")).then_inc(s_staged, 1)

            act.wait_ge(s_place, 1)
            stage_rows(0)
            with act.Fori(1, NT // MOVE) as i:
                stage_rows(i)

            def scale_rows(r, a):
                act.wait_ge(s_zt, r + 1)
                after(act, s_eh, r - 1)
                for c in range(KC):
                    nc.scalar.activation(zT[:, a, c, :], ps_t[:, c * TR:(c + 1) * TR], ACT.Identity,
                                         scale=gb_col[:, 0, c:c + 1], bias=gb_col[:, 1, c:c + 1]).then_inc(s_ztc, 1)

            def gelu(r, a):
                act.wait_ge(s_ehb, r + 1)
                after(act, s_gt, r - 1)
                nc.scalar.activation(hg[:, a, :], hb[:, a, :], ACT.Gelu).then_inc(s_gelu, 1)

            def expert_tile(r, a, i):
                gelu(r + 1, 1 - a)
                scale_rows(r + 2, a)

            for m in range(MOVE):
                act.wait_ge(s_sent[m], NT // MOVE * K * 16)
            scale_rows(0, 0)
            scale_rows(1, 1)
            gelu(0, 0)
            pairwise(act, expert_tile, ET - 2)
            gelu(ET - 1, 1)

            def place_back(i):
                for m in range(MOVE):
                    after(act, s_fetch[m], i * (K * 16))
                    nc.scalar.copy(send_at[:, m, :],
                                   place[:, :, bass.ds(i * MOVE + m, 1)].rearrange("p k a -> p (k a)")).then_inc(s_cat, 1)

            place_back(0)
            with act.Fori(1, NT // MOVE) as i:
                place_back(i)

        @block.vector
        def _(dve):
            did = Steps(dve, s_dve)
            v = nc.vector

            def rank_stages(s):
                cols = pos[:, bass.ds(s * SC, SC)]
                did.did(v.tensor_scalar(kq[:, :], cols, 1.0 / BN, None, ALU.mult))
                yield
                did.wait()
                did.did(v.scalar_tensor_tensor(kf[:, 0], kq[:, :], -float(BN), cols, ALU.mult, ALU.add))
                yield
                did.wait()
                did.did(v.tensor_scalar(kf[:, 1], kf[:, 0], 0.0, None, ALU.is_lt))
                yield
                did.wait()
                did.did(v.scalar_tensor_tensor(kf[:, 2], kf[:, 1], float(BN), kf[:, 0], ALU.mult, ALU.add))
                did.did(v.scalar_tensor_tensor(kf[:, 3], kf[:, 1], -1.0, kq[:, :], ALU.mult, ALU.add))
                yield
                did.wait()
                did.did(v.tensor_scalar(kf[:, 0], kf[:, 2], float(BN), None, ALU.is_ge))
                yield
                did.wait()
                did.did(v.scalar_tensor_tensor(local[:, bass.ds(s * SC, SC)], kf[:, 0], -float(BN), kf[:, 2],
                                               ALU.mult, ALU.add))
                did.did(v.tensor_tensor(kf[:, 1], kf[:, 3], kf[:, 0], ALU.add))
                yield
                did.wait()
                did.did(v.tensor_tensor(mask[:, :, :], kf[:, 1:2, :].to_broadcast([P, NB, SC]),
                                        bucket_iota[:, :].unsqueeze(2).to_broadcast([P, NB, SC]), ALU.is_equal))
                yield
                did.wait()
                v.tensor_reduce(hist[:, :], mask[:, :, :], AX_X, ALU.add).then_inc(s_hist, 1)
                yield
                flat = mask[:, :, :].rearrange("p b t -> p (b t)")
                did.did(v.tensor_tensor_scan(count[:, :, :].rearrange("p b t -> p (b t)"), flat, flat, 0.0,
                                             ALU.add, ALU.max))
                yield PREFIX
                dve.wait_ge(s_prefix, s + 1)
                lanes_before, total = ps_rank[0:P, 0:NB], ps_rank[0:P, NB:2 * NB]
                did.did(v.tensor_scalar(rk_i[:, :], total, float(UR - 1), None, ALU.add))
                yield
                did.wait()
                did.did(v.tensor_scalar(rk_i[:, :], rk_i[:, :], 8, 8, ALU.logical_shift_right, ALU.logical_shift_left))
                yield
                did.wait()
                did.did(v.tensor_copy(rk[:, 0], rk_i[:, :]))
                did.did(v.tensor_tensor_scan(rk[:, 1], hist[:, :], hist[:, :], 0.0, ALU.add, ALU.max))
                yield
                did.wait()
                did.did(v.tensor_tensor_scan(rk[:, 2], rk[:, 0], rk[:, 0], 0.0, ALU.add, ALU.max))
                did.did(v.scalar_tensor_tensor(rk[:, 3], hist[:, :], seg_start[:, bass.ds(s, 1)], rk[:, 1],
                                               ALU.add, ALU.subtract))
                did.did(v.scalar_tensor_tensor(rk[:, 4], lanes_before, -1.0, rk[:, 0], ALU.add, ALU.subtract))
                yield
                did.wait()
                did.did(v.tensor_tensor(rk[:, 5], rk[:, 2], rk[:, 3], ALU.add))
                yield
                did.wait()
                did.did(v.tensor_tensor(rk[:, 6], rk[:, 5], rk[:, 4], ALU.add))
                yield
                did.wait()
                did.did(v.tensor_tensor(count[:, :, :], count[:, :, :],
                                        rk[:, 6, :].unsqueeze(2).to_broadcast([P, NB, SC]), ALU.add))
                yield
                did.wait()
                did.did(v.tensor_tensor(count[:, :, :], count[:, :, :], mask[:, :, :], ALU.mult))
                yield
                did.wait()
                did.did(v.tensor_tensor(filled[:, :, :], rk[0:1, 2:3, :].to_broadcast([1, NU, NB]),
                                        unit_start[:, :].unsqueeze(2).to_broadcast([1, NU, NB]), ALU.is_le))
                yield
                did.wait()
                did.did(v.tensor_reduce(ustart_f[:, :], filled[:, :, :], AX_X, ALU.add))
                with nc.allow_low_precision(reason="whole numbers below 2^24"):
                    did.did(v.tensor_reduce(pos[:, bass.ds(s * SC, SC)], count[:, :, :].rearrange("p b t -> p t b"),
                                            AX_X, ALU.add))
                yield
                did.wait()
                v.tensor_scalar(agg_off[:, bass.ds(s * (STEPS * STEP_OFF), STEPS * STEP_OFF)]
                                .rearrange("p (i u) -> p i u", i=STEPS)[:, :, 0:2 * GROUPS],
                                ustart_f[:, :].rearrange("p (i u) -> p i u", i=STEPS), float(AGG), None,
                                ALU.mult).then_inc(s_rank, 1)
                if isinstance(s, int):
                    dve.wait_ge(s_rank, s + 1)
                else:
                    wait_apart(dve, s_rank, s + 1)

            def rank(s):
                for _ in rank_stages(s):
                    pass

            RANK = 24

            def one_hots(g, k):
                dve.wait_ge(s_unit[k], (g[1] + 1) * 16)
                dve.wait_ge(s_group, g[0] + 10)
                did.did(v.tensor_tensor(rest[:, k % 3], unit[:, k], unit_hi[:, k], ALU.subtract))
                for t in range(4):
                    v.tensor_scalar(onehot[:, k % 3, t, :], node_iota[:, :], unit[:, k, t, EA + 1:ROW], None,
                                    ALU.is_equal)
                did.wait()
                v.tensor_tensor(rest_lo[:, k % 3], rest[:, k % 3], rest_hi[:, k % 3], ALU.subtract)\
                    .then_inc(s_onehot, 1)

            aggf = agg[:, :, :].rearrange("p b f -> p (b f)")

            def slots_of(n):
                _, offs = nc.values_load_multi_w_load_instructions(
                    agg_off[0:1, bass.ds(n * STEP_OFF, STEP_OFF)], engines=(mybir.EngineType.DVE,),
                    min_val=0, max_val=NB * AGG, skip_runtime_bounds_check_because="rank() writes only slots' offsets")
                return offs

            def add_units(g, k, offs):
                dve.wait_ge(s_group, g + CREDIT + 1)
                dve.wait_ge(s_added, g + 2)
                for u in range(2):
                    slot = aggf[:, bass.ds(offs[2 * k + u], AGG)]
                    add = v.tensor_tensor(slot, slot, ps_g[k % 3][0:P, u * AGG:(u + 1) * AGG], ALU.add)
                    if u == 0:
                        did.did(add)
                        did.wait()
                add.then_inc(s_added, 1)

            def mix_stages(j, a):
                def normalise():
                    dve.wait_ge(s_xt, j + 1)
                    v.tensor_scalar(xn[:, a], xs[:, bass.ds(j, 1), :].rearrange("p a d -> p (a d)"),
                                    mv[:, bass.ds(j, 1), 0], rstd[:, bass.ds(j, 1)],
                                    ALU.subtract, ALU.mult).then_inc(s_xn, 1)

                def squares():
                    dve.wait_ge(s_sq, j + 1)
                    v.tensor_reduce(ss[:, :], sq[:, :].rearrange("p (h d) -> p h d", d=HD), AX_X, ALU.add)\
                        .then_inc(s_ss, 1)

                def kv():
                    dve.wait_ge(s_hsd, j + 1)
                    did.did(v.reciprocal(hrs[:, :], hsd[:, :]))
                    did.wait()
                    dve.wait_ge(s_kvacc, j + 1)
                    dst = kvn[:, a].rearrange("p (h d) -> p h d", d=HD)
                    did.did(v.tensor_tensor(dst, ps_kv[0:P, :].rearrange("p (h d) -> p h d", d=HD),
                                            hrs[:, :].unsqueeze(2).to_broadcast([P, 8, HD]), ALU.mult))
                    did.wait()
                    for n in range(2):
                        half = kvn[:, a, n * D:(n + 1) * D].rearrange("p (h d) -> p h d", d=HD)
                        did.did(v.tensor_tensor(half, half, gkv[:, n:n + 1, :].to_broadcast([P, HEADS, HD]), ALU.mult))
                    did.wait()
                    for n in range(2):
                        half = kvn[:, a, n * D:(n + 1) * D].rearrange("p (h d) -> p h d", d=HD)
                        last = v.tensor_tensor(half, half, bkv[:, n:n + 1, :].to_broadcast([P, HEADS, HD]), ALU.add)
                    last.then_inc(s_kvn, 1)

                return {0: normalise, 2: squares, 3: kv}

            def mix2(j, a, n):
                dve.wait_ge(s_mix, j + 2)
                dve.wait_ge(s_xt2[a], (n + 1) * 16)
                v.tensor_tensor(xt[:, a], xt[:, a], ps_kv[0:P, a * D:(a + 1) * D], ALU.add).then_inc(s_mixed, 1)

            def step(s, i, mix, groups, ranking=None):
                if mix == 1:
                    j = s * (2 * STEPS) + i * 2
                    todo = mix_stages(j, 0)
                    todo.update({k + 5: f for k, f in mix_stages(j + 1, 1).items()})
                elif mix == 2:
                    j = (s - SEGS // 2) * (2 * STEPS) + i * 2
                    n2 = (s - SEGS // 2) * STEPS + i
                    todo = {2: lambda: mix2(j, 0, n2), 7: lambda: mix2(j + 1, 1, n2)}
                else:
                    todo = {}
                n = (s - 1) * STEPS + i
                for k in range(GROUPS):
                    if groups:
                        one_hots((n * GROUPS + k, n), k)
                        if k == 0:
                            offs = slots_of(n)
                        else:
                            add_units(n * GROUPS + k - 1, k - 1, offs)
                    if k in todo:
                        todo[k]()
                    if ranking is not None and k not in todo:
                        ranking(i)
                if groups:
                    add_units(n * GROUPS + GROUPS - 1, GROUPS - 1, offs)

            def segment(s, mix, groups):
                stages = rank_stages(s + 1)
                at_prefix = []

                def ranking(i):
                    if at_prefix and i < PREFIX_STEP:
                        return
                    if next(stages, None) is PREFIX:
                        at_prefix.append(True)

                for i in range(STEPS):
                    step(s, i, mix, groups, ranking)
                    if i == PREFIX_STEP - 1:
                        assert at_prefix
                assert next(stages, PREFIX + 1) == PREFIX + 1

            G_STEP = 2 * GROUPS
            M_STEP = 2 * 4

            did.did(v.memset(agg_off[:, :], 0))
            v.memset(agg[:, 0:1, :], 0.0).then_inc(s_added, 2)
            v.memset(agg[:, 1:, :], 0.0).then_inc(s_group, CREDIT)
            dve.wait_ge(s_const, NCONST)
            dve.wait_ge(s_src, 16)
            rank(0)
            dve.wait_ge(s_wTc, 2)
            for c in range(KC):
                wc = w_kv[:, c].rearrange("p (h d) -> p h d", d=HD)
                did.did(v.tensor_reduce(csum[:, c], wc, AX_X, ALU.add))
            did.wait()
            did.did(v.tensor_scalar(csum[:, :, :], csum[:, :, :], 1.0 / HD, None, ALU.mult))
            did.wait()
            for c in range(KC):
                wc = w_kv[:, c].rearrange("p (h d) -> p h d", d=HD)
                last = v.tensor_tensor(wc, wc, csum[:, c].unsqueeze(2).to_broadcast([128, 8, HD]), ALU.subtract)
                last.then_inc(s_wkv, 1)
            dve.wait_ge(s_x, 80)
            with did.loop(0, NT, 1) as j:
                did.did(v.bn_stats(stats[:, bass.ds(j, 1), :].rearrange("p a d -> p (a d)"),
                                   xs[:, bass.ds(j, 1), :].rearrange("p a d -> p (a d)")))
            did.wait()
            did.did(v.tensor_tensor(mv[:, :, 0], stats[:, :, 1], stats[:, :, 4], ALU.add))
            did.did(v.tensor_tensor(mv[:, :, 1], stats[:, :, 1], stats[:, :, 4], ALU.subtract))
            did.did(v.tensor_tensor(rstd[:, :], stats[:, :, 2], stats[:, :, 5], ALU.add))
            did.wait()
            did.did(v.tensor_scalar(mv[:, :, 0], mv[:, :, 0], 0.5, None, ALU.mult))
            did.did(v.tensor_tensor(sd[:, :], mv[:, :, 1], mv[:, :, 1], ALU.mult))
            did.wait()
            did.did(v.tensor_scalar(sd[:, :], sd[:, :], 0.25, None, ALU.mult))
            did.wait()
            v.scalar_tensor_tensor(mv[:, :, 1], rstd[:, :], 1.0 / D, sd[:, :], ALU.mult, ALU.add).then_inc(s_stats, 1)
            dve.wait_ge(s_sd, 1)
            did.did(v.reciprocal(rstd[:, :], sd[:, :]))
            did.wait()
            segment(0, 1, False)
            with did.loop(1, SEGS // 2, RANK + STEPS * (M_STEP + G_STEP)) as s:
                segment(s, 1, True)
            dve.wait_ge(s_kvacc, NT + 1)
            did.did(v.memset(kv_sb[:, :, :], 0.0))
            did.wait()
            for c in range(KC):
                for h in range(2):
                    r = slice(64 * h, 64 * h + 64)
                    last = v.tensor_scalar(kv_sb[r, c, r], ps_acc[c][r, r], 1.0 / N, None, ALU.mult)
                    last.then_inc(s_kvsb, 1)
            with did.loop(SEGS // 2, SEGS - 1, RANK + STEPS * G_STEP) as s:
                segment(s, 2, True)
            with did.loop(0, STEPS, G_STEP) as i:
                step(SEGS - 1, i, 2, True)
            with did.loop(0, STEPS, G_STEP) as i:
                step(SEGS, i, 0, True)

            def network(b, a):
                sums = agg[:, bass.ds(b, 1), :].rearrange("p b (h f) -> p (b h) f", h=2)
                did.did(v.tensor_scalar(cnt[:, :], sums[:, :, EA], 1.0, None, ALU.max))
                did.wait()
                did.did(v.reciprocal(rcnt[:, :], cnt[:, :]))
                did.wait()
                if not (isinstance(b, int) and b == 0):
                    dve.wait_ge(s_aggt, b)
                v.tensor_tensor(aggn[:, :, :], sums[:, :, 0:EA], rcnt[:, :].unsqueeze(2).to_broadcast([P, 2, EA]),
                                ALU.mult).then_inc(s_aggn, 1)

            def norms(b, a, n):
                dve.wait_ge(s_x1in[a], (n + 1) * 16)
                dve.wait_ge(s_o, b + 1)
                v.tensor_tensor(x1t[:, a], x1t[:, a], ps_g[0][0:P, :].rearrange("p (t d) -> p t d", t=2),
                                ALU.add).then_inc(s_x1done, 1)
                dve.wait_ge(s_x1done, b + 1)
                for r in range(2):
                    src_t = x1t[:, a] if r == 0 else y1[:, :, :]
                    for q in range(2):
                        did.did(v.bn_stats(st[:, q, :], src_t[:, q, :]))
                    wait_apart(dve, did.sem, did.base + did.k)
                    for q in range(2):
                        last = v.bn_aggr(mv2[:, q, :], st[:, q, :])
                        last.then_inc(s_dve, 1) if q == 0 else last.then_inc(s_mv2, 1)
                    did.k += 1
                    did.wait()
                    dve.wait_ge(s_sd2, b * 2 + r + 1)
                    did.did(v.reciprocal(rs2[:, :], sd2[:, :]))
                    did.wait()
                    for q in range(2):
                        dst = (y1, y2)[r][:, q, :]
                        if r == 1 and q == 0:
                            dve.wait_ge(s_yt, b * 2 + 1)
                            dve.wait_ge(s_keep, b + 1)
                        last = v.tensor_scalar(dst, src_t[:, q, :], mv2[:, q, 0:1], rs2[:, q:q + 1],
                                               ALU.subtract, ALU.mult)
                        if r == 0:
                            did.did(last)
                        else:
                            last.then_inc(s_yn, 1)
                    if r == 0:
                        did.wait()

            NORMS = 2 + 1 + 1 + 2 + 2 + 1 + 1
            network(0, 0)
            with did.loop(0, NB // 2, 2 * (2 + NORMS)) as i:
                for a in range(2):
                    network(2 * i + a + 1, a)
                    norms(2 * i + a, a, i)
            norms(NB - 1, 0, NB // 2)

            dve.wait_ge(s_lgc, NT + 1)
            dve.wait_ge(s_x1out, NB * 16)
            dve.wait_ge(s_keep, NB + 1)
            did.wait()
            experts = expert_iota[:, :].unsqueeze(1).to_broadcast([P, NT, NE])
            for k in range(K):
                vals = (logits, left)[k]
                did.did(v.tensor_reduce(top[:, k, 0, :], vals[:, :, :], AX_X, ALU.max))
                did.wait()
                did.did(v.tensor_tensor(tmp[:, :, :], vals[:, :, :],
                                        top[:, k, 0, :].unsqueeze(2).to_broadcast([P, NT, NE]), ALU.is_equal))
                did.wait()
                did.did(v.scalar_tensor_tensor(tmp[:, :, :], tmp[:, :, :], -float(NE), experts, ALU.mult, ALU.add))
                did.wait()
                did.did(v.tensor_reduce(top[:, k, 1, :], tmp[:, :, :], AX_X, ALU.min))
                did.wait()
                did.did(v.tensor_scalar(top[:, k, 1, :], top[:, k, 1, :], float(NE), None, ALU.add))
                did.wait()
                did.did(v.tensor_tensor(best[:, :, k * NT:(k + 1) * NT].rearrange("p e t -> p t e"),
                                        top[:, k, 1, :].unsqueeze(2).to_broadcast([P, NT, NE]), experts, ALU.is_equal))
                did.wait()
                if k == 0:
                    did.did(v.scalar_tensor_tensor(left[:, :, :],
                                                   best[:, :, 0:NT].rearrange("p e t -> p t e"), -BIG,
                                                   logits[:, :, :], ALU.mult, ALU.add))
                    did.wait()
            v.tensor_tensor(top[:, 1, 0, :], top[:, 1, 0, :], top[:, 0, 0, :], ALU.subtract).then_inc(s_diff, 1)
            v.tensor_reduce(hist[:, 0:NE], best[:, :, :], AX_X, ALU.add).then_inc(s_chist, 1)
            flat = best[:, :, :].rearrange("p e t -> p (e t)")
            did.did(v.tensor_tensor_scan(at[:, :, :].rearrange("p e t -> p (e t)"), flat, flat, 0.0, ALU.add, ALU.max))
            dve.wait_ge(s_exp, 1)
            did.did(v.tensor_scalar(top[:, 0, 2, :], top[:, 1, 1, :], 1.0, None, ALU.add))
            did.wait()
            did.did(v.reciprocal(weight[:, 0, :], top[:, 0, 2, :]))
            did.wait()
            did.did(v.tensor_tensor(weight[:, 1, :], weight[:, 0, :], top[:, 1, 1, :], ALU.mult))
            dve.wait_ge(s_chist, 1)
            dve.wait_ge(s_cprefix, 1)
            lanes_before, total = ps_rank[0:P, 0:NE], ps_rank[0:P, NE:2 * NE]
            did.did(v.tensor_scalar(rk_i[:, 0:NE], total, float(TR - 1), None, ALU.add))
            did.wait()
            did.did(v.tensor_scalar(rk_i[:, 0:NE], rk_i[:, 0:NE], 7, 7, ALU.logical_shift_right, ALU.logical_shift_left))
            did.wait()
            did.did(v.tensor_copy(rk[:, 0, 0:NE], rk_i[:, 0:NE]))
            did.did(v.tensor_tensor_scan(rk[:, 1, 0:NE], hist[:, 0:NE], hist[:, 0:NE], 0.0, ALU.add, ALU.max))
            did.wait()
            did.did(v.tensor_tensor_scan(rk[:, 2, 0:NE], rk[:, 0, 0:NE], rk[:, 0, 0:NE], 0.0, ALU.add, ALU.max))
            did.did(v.tensor_tensor(rk[:, 3, 0:NE], hist[:, 0:NE], rk[:, 1, 0:NE], ALU.subtract))
            did.did(v.scalar_tensor_tensor(rk[:, 4, 0:NE], lanes_before, -1.0, rk[:, 0, 0:NE], ALU.add, ALU.subtract))
            did.wait()
            did.did(v.tensor_tensor(rk[:, 5, 0:NE], rk[:, 2, 0:NE], rk[:, 3, 0:NE], ALU.add))
            did.did(v.tensor_tensor(ended[:, :, :], rk[0:1, 2:3, 0:NE].to_broadcast([1, ET, NE]),
                                    tile_start[:, :].unsqueeze(2).to_broadcast([1, ET, NE]), ALU.is_le))
            did.wait()
            did.did(v.tensor_tensor(rk[:, 6, 0:NE], rk[:, 5, 0:NE], rk[:, 4, 0:NE], ALU.add))
            did.did(v.tensor_reduce(expert_f[:, :], ended[:, :, :], AX_X, ALU.add))
            did.wait()
            did.did(v.tensor_scalar(expert[:, :], expert_f[:, :], float(NE - 1), None, ALU.min))
            did.did(v.tensor_tensor(at[:, :, :], at[:, :, :],
                                    rk[:, 6, 0:NE].unsqueeze(2).to_broadcast([P, NE, K * NT]), ALU.add))
            did.wait()
            did.did(v.tensor_tensor(at[:, :, :], at[:, :, :], best[:, :, :], ALU.mult))
            did.wait()
            with nc.allow_low_precision(reason="whole numbers below 2^24"):
                v.tensor_reduce(place[:, :, :].rearrange("p k t -> p (k t)"), at[:, :, :].rearrange("p e t -> p t e"),
                                AX_X, ALU.add).then_inc(s_place, 1)

            def which(r):
                return v.value_load(expert[0:1, bass.ds(r, 1)], min_val=0, max_val=NE - 1)

            def add_b1(r, a):
                e = which(r)
                dve.wait_ge(s_eh, r + 1)
                after(dve, s_gelu, r - 1)
                v.tensor_tensor(hb[:, a, :], ps_acc[a][:, :], b1_rows[:, bass.ds(e * HID, HID)], ALU.add).then_inc(s_ehb, 1)

            def keep_gT(r, a):
                dve.wait_ge(s_gt, r + 1)
                after(dve, s_ey, r - 1)
                v.tensor_copy(hgT[:, a].rearrange("p c n -> p (c n)"), ps_g[a][:, :]).then_inc(s_gtc, 1)

            def add_b2(r, a, i):
                e = which(r)
                dve.wait_ge(s_ey, r + 1)
                after(dve, s_eout[a], i * 16)
                v.tensor_tensor(y_out[:, a, :], ps_y[a][:, 0:D], b2_rows[:, bass.ds(e * D, D)], ALU.add).then_inc(s_eyb, 1)

            def expert_tile(r, a, i):
                add_b1(r + 1, 1 - a)
                add_b2(r, a, i)
                keep_gT(r + 1, 1 - a)

            dve.wait_ge(s_b1, 16)
            dve.wait_ge(s_we, (KC + HC + 1) * 16)
            add_b1(0, 0)
            keep_gT(0, 0)
            pairwise(dve, expert_tile, ET - 2)
            add_b1(ET - 1, 1)
            add_b2(ET - 2, 0, ET // 2 - 1)
            keep_gT(ET - 1, 1)
            add_b2(ET - 1, 1, ET // 2 - 1)

            with did.loop(0, NT // MOVE, MOVE) as i:
                for m in range(MOVE):
                    t = i * MOVE + m
                    dve.wait_ge(s_res[m], (i + 1) * 16)
                    dve.wait_ge(s_fetch[m], (i + 1) * (K * 16))
                    did.did(v.scalar_tensor_tensor(res[:, m, :], fetched[:, m, 0, :], weight[:, 0, bass.ds(t, 1)],
                                                   res[:, m, :], ALU.mult, ALU.add))
                    did.wait()
                    v.scalar_tensor_tensor(res[:, m, :], fetched[:, m, 1, :], weight[:, 1, bass.ds(t, 1)],
                                           res[:, m, :], ALU.mult, ALU.add).then_inc(s_comb, 1)

        @block.tensor
        def _(pe):
            t = nc.tensor
            pe.wait_ge(s_const, NCONST)

            def rank(s):
                pe.wait_ge(s_hist, s + 1)
                pe.wait_ge(s_rank, s)
                t.matmul(ps_rank[0:P, 0:NB], below[:, :], hist[:, :], start=True, stop=True)
                t.matmul(ps_rank[0:P, NB:2 * NB], ones[:, :], hist[:, :], start=True, stop=True).then_inc(s_prefix, 1)

            def pair(g, k):
                pe.wait_ge(s_onehot, g + 1)
                pe.wait_ge(s_added, g + 1)
                for u in range(2):
                    for half in range(2):
                        o = u * AGG + half * (EA + 1)
                        for j in range(2):
                            for n, rows_of in enumerate((unit_hi[:, k], rest_hi[:, k % 3], rest_lo[:, k % 3])):
                                last = t.matmul(ps_g[k % 3][:, o:o + EA + 1],
                                                onehot[:, k % 3, 2 * u + j, half * P:half * P + 128],
                                                rows_of[:, 2 * u + j, 0:EA + 1],
                                                start=(j == 0 and n == 0), stop=(j == 1 and n == 2))
                last.then_inc(s_group, 1)

            def project(j, a, first=False):
                pe.wait_ge(s_xn, j + 1)
                pe.wait_ge(s_xtc, 2 * j)
                for c in range(KC):
                    last = t.transpose(ps_t[:, c * P:(c + 1) * P], xn[:, a, c * 128:(c + 1) * 128], ident[0:P, 0:P])
                last.then_inc(s_xt, 1)
                pe.wait_ge(s_xtc, 2 * j + 2)
                pe.wait_ge(s_kvn, j)
                for c in range(KC):
                    last = t.matmul(ps_kv[0:P, :], xnT_t[:, a, c, :], w_kv[:, c, :], start=(c == 0), stop=(c == KC - 1))
                last.then_inc(s_kvp, 1)

            def accumulate(j, a, start):
                pe.wait_ge(s_kvn, j + 1)
                for c in range(KC):
                    last = t.matmul(ps_acc[c][:, 0:128], kvn[:, a, D + 128 * c:D + 128 * c + 128],
                                    kvn[:, a, 128 * c:128 * c + 128], start=start, stop=False,
                                    skip_group_check=True)
                last.then_inc(s_kvacc, 1)

            def mix2(j, a):
                pe.wait_ge(s_x2, j + 1)
                pe.wait_ge(s_mixed, j + 1)
                o = ps_kv[0:P, a * D:(a + 1) * D]
                for c in range(KC):
                    t.matmul(o, xnT_t[:, a, c, :], mix_w[:, c, :], start=(c == 0), stop=False)
                for r in range(2):
                    last = t.matmul(o, ones[0:1, :], bias_rows[0:1, r, :], start=False, stop=(r == 1))
                last.then_inc(s_mix, 1)

            def step(s, i, mix, groups, first=False):
                if mix == 1:
                    j = s * (2 * STEPS) + i * 2
                    todo = {0: lambda: project(j, 0), 4: lambda: accumulate(j, 0, first),
                            5: lambda: project(j + 1, 1), 9: lambda: accumulate(j + 1, 1, False)}
                elif mix == 2:
                    j = (s - SEGS // 2) * (2 * STEPS) + i * 2
                    todo = {1: lambda: mix2(j, 0), 6: lambda: mix2(j + 1, 1)}
                else:
                    todo = {}
                n = (s - 1) * STEPS + i
                for k in range(GROUPS):
                    if groups:
                        pair(n * GROUPS + k, k)
                    if k in todo:
                        todo[k]()

            pe.wait_ge(s_w, 16 * 16)
            for n in range(3):
                pe.wait_ge(s_wTc, n)
                for ci in range(KC):
                    for co in range(KC):
                        last = t.transpose(ps_t[:, ci * D + co * 128:ci * D + co * 128 + 128],
                                           raw[:, n, co, ci * 128:(ci + 1) * 128], ident[:, :])
                last.then_inc(s_wT, 1)
            rank(0)
            for c in range(HC):
                o = ps_kv[:, c:c + 1]
                t.matmul(o, w1u[:, c * 128:(c + 1) * 128], u_col[:, :], start=True, stop=False)
                last = t.matmul(o, b1_row[0:1, c * 128:(c + 1) * 128], ones[0:1, 0:1], start=False, stop=True)
            last.then_inc(s_hb, 1)
            pe.wait_ge(s_wkv, 2)
            pe.wait_ge(s_wTc, 3)
            pe.wait_ge(s_hbc, 1)
            step(0, 0, 1, False, first=True)
            with pe.Fori(1, PREFIX_STEP) as i:
                step(0, i, 1, False)
            rank(1)
            with pe.Fori(PREFIX_STEP, STEPS) as i:
                step(0, i, 1, False)
            with pe.Fori(1, SEGS // 2) as s:
                with pe.Fori(0, PREFIX_STEP) as i:
                    step(s, i, 1, True)
                rank(s + 1)
                with pe.Fori(PREFIX_STEP, STEPS) as i:
                    step(s, i, 1, True)
            pe.wait_ge(s_kvsb, 4)
            for c in range(KC):
                t.matmul(ps_t[:, c * D:(c + 1) * D], kv_sb[:, c, :], w_oT[:, c, :], start=True, stop=True)\
                    .then_inc(s_kvo, 1)
            pe.wait_ge(s_kvoc, KC)
            pe.wait_ge(s_kvn, NT)
            for ci in range(KC):
                for c in range(KC):
                    last = t.matmul(ps_kv[:, ci * D:(ci + 1) * D], w_q[:, c, ci * 128:(ci + 1) * 128], kvo[:, c, :],
                                    start=(c == 0), stop=(c == KC - 1))
                last.then_inc(s_mixw, 1)
            pe.wait_ge(s_mixwc, KC)
            with pe.Fori(SEGS // 2, SEGS - 1) as s:
                with pe.Fori(0, PREFIX_STEP) as i:
                    step(s, i, 2, True)
                rank(s + 1)
                with pe.Fori(PREFIX_STEP, STEPS) as i:
                    step(s, i, 2, True)
            with pe.Fori(0, STEPS) as i:
                step(SEGS - 1, i, 2, True)
            with pe.Fori(0, STEPS) as i:
                step(SEGS, i, 0, True)

            pe.wait_ge(s_gw, 4 * 16)
            for n in range(2):
                for c in range(KC):
                    last = t.matmul(ps_t[:, n * KC + c:n * KC + c + 1], gb_rows[0:1, n, c * 128:(c + 1) * 128],
                                    ones[0:1, 0:1], start=True, stop=True)
            last.then_inc(s_gb, 1)
            pe.wait_ge(s_gbc, 1)
            pe.wait_ge(s_mixed, NT + 1)
            pe.wait_ge(s_added, 2 + SEGS * STEPS * GROUPS)

            def network(b):
                wait_apart(pe, s_aggn, b + 1)
                for a in range(2):
                    last = t.transpose(ps_rank[0:EA, a * P:(a + 1) * P], aggn[:, a, :], ident[0:P, 0:P])
                last.then_inc(s_aggt, 1)
                pe.wait_ge(s_aggtc, b + 1)
                for hc in range(HC):
                    if hc % 2 == 0 and not (isinstance(b, int) and b == 0):
                        pe.wait_ge(s_relu, (b - 1) * HC + hc + 2)
                    o = ps_acc[hc // 2][:, (hc % 2) * BN:(hc % 2 + 1) * BN]
                    for c in range(KC):
                        t.matmul(o, w1x[:, c, hc * 128:(hc + 1) * 128], xnT[:, bass.ds(b * 2, 2), c, :],
                                 start=(c == 0), stop=False)
                    last = t.matmul(o, w1e[:, hc * 128:(hc + 1) * 128], aggT[:, :, :].rearrange("p t n -> p (t n)"),
                                    start=False, stop=True)
                    if hc % 2:
                        last.then_inc(s_h, 1)
                if not (isinstance(b, int) and b == 0):
                    pe.wait_ge(s_x1done, b)
                for a in range(2):
                    for hc in range(HC):
                        pe.wait_ge(s_relu, b * HC + hc + 1) if a == 0 else None
                        last = t.matmul(ps_g[0][0:P, a * D:(a + 1) * D], hT[:, hc, a, :], w2[:, hc, :],
                                        start=(hc == 0), stop=(hc == HC - 1))
                last.then_inc(s_o, 1)

            def router(b):
                for a in range(2):
                    pe.wait_ge(s_yn, b * 2 + a + 1)
                    pe.wait_ge(s_ytc, (b * 2 + a) * KC + 1)
                    for c in range(KC):
                        last = t.transpose(ps_t[:, c * P:(c + 1) * P],
                                           y2[:, a, c * 128:(c + 1) * 128],
                                           ident[0:P, 0:P])
                    last.then_inc(s_yt, 1)
                    pe.wait_ge(s_ytc, (b * 2 + a + 1) * KC + 1)
                    pe.wait_ge(s_lgc, b * 2 + a + 1)
                    for c in range(KC):
                        t.matmul(ps_kv[0:P, 0:NE], ynT[:, a, c, :], w_r[:, c, :], start=(c == 0), stop=False)
                    t.matmul(ps_kv[0:P, 0:NE], ones[0:1, :], br_row[:, :], start=False, stop=True).then_inc(s_lg, 1)

            network(0)
            with pe.Fori(1, NB) as b:
                network(b)
                router(b - 1)
            router(NB - 1)

            pe.wait_ge(s_chist, 1)
            t.matmul(ps_rank[0:P, 0:NE], below[:, :], hist[:, 0:NE], start=True, stop=True)
            t.matmul(ps_rank[0:P, NE:2 * NE], ones[:, :], hist[:, 0:NE], start=True, stop=True).then_inc(s_cprefix, 1)

            def which(r):
                return t.value_load(expert[0:1, bass.ds(r, 1)], min_val=0, max_val=NE - 1)

            def rows_T(r, a, i):
                pe.wait_ge(s_rowin[a], (i + 1) * 16)
                after(pe, s_ztc, r * KC)
                for c in range(KC):
                    last = t.transpose(ps_t[:, c * TR:(c + 1) * TR], row_in[:, a, c * 128:(c + 1) * 128], ident[:, :])
                last.then_inc(s_zt, 1)

            def hidden(r, a):
                e = which(r)
                pe.wait_ge(s_ztc, (r + 1) * KC)
                after(pe, s_ehb, r - 1)
                for c in range(KC):
                    last = t.matmul(ps_acc[a][:, :], zT[:, a, c, :], W1_all[:, bass.ds(e * (KC * HID) + c * HID, HID)],
                                    start=(c == 0), stop=(c == KC - 1))
                last.then_inc(s_eh, 1)

            def gelu_T(r, a):
                pe.wait_ge(s_gelu, r + 1)
                after(pe, s_gtc, r - 1)
                for c in range(HC):
                    last = t.transpose(ps_g[a][:, c * TR:(c + 1) * TR], hg[:, a, c * 128:(c + 1) * 128], ident[:, :])
                last.then_inc(s_gt, 1)

            def outputs(r, a):
                e = which(r)
                pe.wait_ge(s_gtc, r + 1)
                after(pe, s_eyb, r - 1)
                for c in range(HC):
                    last = t.matmul(ps_y[a][:, 0:D], hgT[:, a, c, :], W2_all[:, bass.ds(e * (HC * D) + c * D, D)],
                                    start=(c == 0), stop=(c == HC - 1))
                last.then_inc(s_ey, 1)

            def expert_tile(r, a, i):
                hidden(r + 1, 1 - a)
                outputs(r, a)
                rows_T(r + 2, a, i + 1)
                gelu_T(r + 1, 1 - a)

            pe.wait_ge(s_place, 1)
            pe.wait_ge(s_we, (KC + HC + 1) * 16)
            rows_T(0, 0, 0)
            rows_T(1, 1, 0)
            hidden(0, 0)
            gelu_T(0, 0)
            pairwise(pe, expert_tile, ET - 2)
            hidden(ET - 1, 1)
            outputs(ET - 2, 0)
            gelu_T(ET - 1, 1)
            outputs(ET - 1, 1)


_INS = ["x", "src", "edge_attr_64", "L0_gnn_u", "L0_gnn_W1", "L0_gnn_b1", "L0_gnn_W2", "L0_gnn_b2",
        "L0_mix_wq", "L0_mix_wk", "L0_mix_wv", "L0_mix_wo", "L0_mix_bo",
        "L0_mix_ln_k_g", "L0_mix_ln_k_b", "L0_mix_ln_v_g", "L0_mix_ln_v_b",
        "L0_ffn_gamma", "L0_ffn_beta", "L0_ffn_Wr", "L0_ffn_br", "L0_ffn_W1", "L0_ffn_b1", "L0_ffn_W2", "L0_ffn_b2"]


def kernel(**inputs):
    import numpy as _np
    import concourse.bacc as _bacc
    from concourse import mybir as _mybir
    from concourse.bass_utils import run_bass_kernel_spmd as _run

    nc = _bacc.Bacc("TRN2", target_bir_lowering=False, num_devices=1)
    arrays, args = {}, []
    for name in _INS:
        a = _np.ascontiguousarray(inputs[name])
        arrays[f"in_{name}_dram"] = a
        args.append(nc.dram_tensor(f"in_{name}_dram", a.shape, _mybir.dt.from_np(a.dtype), kind="ExternalInput").ap())
    args.append(nc.dram_tensor("out_0_dram", (N, D), F32, kind="ExternalOutput").ap())
    args.append(nc.dram_tensor("buckets", (SEGS * SEG_ROWS, ROW), F32, kind="Internal").ap())
    args.append(nc.dram_tensor("x1", (N, D), F32, kind="Internal").ap())
    args.append(nc.dram_tensor("sorted_y", (ET * TR, D), F32, kind="Internal").ap())
    args.append(nc.dram_tensor("expert_out", (ET * TR, D), F32, kind="Internal").ap())
    build(nc, *args)
    r = _run(nc, [arrays], core_ids=[0])
    return r.results[0]["out_0_dram"]
```

```python
from contextlib import ExitStack, contextmanager

import concourse.bass as bass
from concourse import mybir

ALU = mybir.AluOpType
ACT = mybir.ActivationFunctionType
AX_X = mybir.AxisListType.X
F32 = mybir.dt.float32
BF16 = mybir.dt.bfloat16
I32 = mybir.dt.int32
U32 = mybir.dt.uint32

N = 6250
D = 256
EA = 64
HID = 512
HEADS, HD = 4, 64
NE = 8
EPS = 1e-5

P = 125
NT = N // P
KC = D // 128
HC = HID // 128

E = 206250
EC = E // P
SEGS = 10
SC = EC // SEGS
STEPS = 5
SLOTS = 3
CH = SC // (STEPS * SLOTS)
NB = 25
BN = N // NB
UR = 256
GROUPS = 11
NU = 2 * GROUPS * STEPS
assert (SC * P + NB * (UR - 1)) // UR <= NU
SEG_ROWS = NU * UR
ROW = EA + 2
AGG = 2 * (EA + 1)
RING = 4
LAG = RING - 2
assert GROUPS % RING == RING - 1
BEHIND = STEPS + 1
CREDIT = GROUPS
STEP_OFF = -(-2 * GROUPS // 4) * 4
PREFIX_STEP = 2
PREFIX = 1
OH = 256
FILLS = 2
QW = 15


K = 2
TR = 128
ET = (N * K + NE * (TR - 1)) // TR + 1
ET += ET % 2
MOVE = 5
BIG = 3.0e38


class Steps:

    def __init__(self, eng, sem):
        self.eng, self.sem, self.base, self.k = eng, sem, 0, 0

    def did(self, ins):
        ins.then_inc(self.sem, 1)
        self.k += 1

    def wait(self):
        self.eng.wait_ge(self.sem, self.base + self.k)

    @contextmanager
    def loop(self, start, end, per):
        with self.eng.Fori(start, end) as i:
            base, k = self.base, self.k
            self.base, self.k = base + k + (i - start) * per, 0
            yield i
            assert self.k == per, (self.k, per)
            self.base, self.k = base, k + (end - start) * per


def build(nc, x, src, edge_attr, gnn_u, gnn_W1, gnn_b1, gnn_W2, gnn_b2,
          wq, wk, wv, wo, bo, k_g, k_b, v_g, v_b, gamma, beta, Wr, br, W1, b1, W2, b2,
          out, buckets, x1, sorted_y, expert_out):
    with ExitStack() as ctx:
        def sb(name, shape, dt=F32):
            return ctx.enter_context(nc.sbuf_tensor(name, shape, dt))

        def psum(name, shape, dt=F32):
            return ctx.enter_context(nc.psum_tensor(name, shape, dt))

        def sem(name):
            return ctx.enter_context(nc.semaphore(name))

        x_or_xnT = sb("x_or_xnT", [128, NT * D])
        xs = x_or_xnT[0:P, :].rearrange("p (j d) -> p j d", d=D)
        xnT = x_or_xnT[:, :].rearrange("p (j c n) -> p j c n", c=KC, n=128)[:, :, :, 0:P]
        agg = sb("agg", [P, NB + 1, AGG])
        arena = sb("arena", [128, 19500])
        arena2 = sb("arena2", [128, 8000])

        def carver(store, at=0):
            at = [at]
            return lambda shape, dt=F32: carve(store, at, shape, dt)

        def carve(store, at, shape, dt):
            size = 1
            for n in shape[1:]:
                size *= n
            words = size if dt != BF16 else (size + 1) // 2
            view = store[0:shape[0], at[0]:at[0] + words]
            at[0] += words
            assert at[0] <= store.shape[1], at[0]
            if dt != F32:
                view = view.bitcast(dt)[:, 0:size]
            names = " ".join("abcd"[:len(shape) - 1])
            return view.rearrange(f"p ({names}) -> p {names}",
                                  **{n: m for n, m in zip("abcd", shape[1:])}) if len(shape) > 2 else view

        part = carver(arena)
        part2 = carver(arena2)

        w_kv = part2([128, KC, 2 * D])
        w_q = part2([128, KC, D])
        w_oT = part2([128, KC, D])
        w1x = sb("w1x", [128, KC, HID])
        w1e = sb("w1e", [EA, HID])
        w1u = sb("w1u", [128, HID])
        w2 = sb("w2", [128, HC, D])
        u_col = sb("u_col", [128, 1])
        b1_row = sb("b1_row", [1, HID])
        h_bias = sb("h_bias", [128, HC])
        bias_rows = sb("bias_rows", [1, 2, D])
        k_rows = sb("k_rows", [128, 2, HD])
        kv_cols = sb("kv_cols", [128, 4])
        kv_sums = sb("kv_sums", [128, 2 * KC])
        k_shift = sb("k_shift", [128, KC + 1])
        mix_w = part2([128, KC, D])
        kv_sb = part2([128, KC, 128])
        kvo = part2([128, KC, D])
        ident = sb("ident", [128, 128])
        ones = sb("ones", [P, P])
        below = sb("below", [P, P])
        node_iota = sb("node_iota", [128, OH], BF16)
        bucket_iota = sb("bucket_iota", [P, NB], BF16)
        unit_start = sb("unit_start", [1, NU])
        seg_start = sb("seg_start", [P, SEGS])
        spare = sb("spare", [1, 16])
        eps_col = sb("eps_col", [P, 1])
        eps2_col = sb("eps2_col", [P, 1])
        zeros = sb("zeros", [128, SEG_ROWS * ROW // 128 // (FILLS * QW)])
        pos = part([P, EC], I32)
        local = part([P, EC], BF16)
        mask = part([P, NB, SC], BF16)
        count = part([P, NB, SC])
        filled = mask[:, :, :].rearrange("p b t -> p (b t)")[0:1, 0:NU * NB].rearrange("p (u b) -> p u b", b=NB)
        kq = sb("kq", [P, SC], I32)
        kf = sb("kf", [P, 4, SC])
        hist = sb("hist", [P, NB])
        rk = sb("rk", [P, 8, NB])
        rk_i = sb("rk_i", [P, NB], I32)
        ustart_f = sb("ustart_f", [1, NU])
        agg_off = sb("agg_off", [1, (SEGS * STEPS + 1) * STEP_OFF], I32)
        stage = part([P, SLOTS, CH, EA])
        rows = part([P, SLOTS, CH, ROW])
        rows_at = sb("rows_at", [P, SLOTS, CH], I32)
        unit = part([128, GROUPS, 4, ROW])
        unit_hi = unit.rearrange("p k j f -> p (k j f)").bitcast(BF16)\
            .rearrange("p (k j f h) -> p k j f h", k=GROUPS, j=4, h=2)[:, :, :, :, 1]
        rest = part([128, RING, 4, ROW])
        rest_hi = rest.rearrange("p k j f -> p (k j f)").bitcast(BF16)\
            .rearrange("p (k j f h) -> p k j f h", k=RING, j=4, h=2)[:, :, :, :, 1]
        rest_lo = part([128, RING, 4, ROW], BF16)
        onehot_words = part([128, RING * 4 * OH // 2])
        onehot = onehot_words.bitcast(BF16).rearrange("p (k j n) -> p k j n", k=RING, j=4)
        raw = onehot_words[:, 0:3 * KC * D].rearrange("p (n c d) -> p n c d", n=3, c=KC)
        xt = part2([P, 2, D])
        xn = part2([P, 2, D])
        xnT_t = part2([128, 2, KC, P])
        stats = sb("stats", [P, NT, 6])
        mv = sb("mv", [P, NT, 2])
        sd = sb("sd", [P, NT])
        rstd = sb("rstd", [P, NT])
        sq = part2([P, 2 * D])
        ss = sb("ss", [P, 8])
        hsd = sb("hsd", [P, 8])
        hrs = sb("hrs", [P, 8])
        kvn = part2([P, 2, 2 * D])
        csum = sb("csum", [128, KC, 8])

        part2 = carver(arena2)
        logits = part2([P, NT, NE])
        W1_all = arena[:, 0:NE * KC * HID]
        W2_all = arena[:, NE * KC * HID:NE * (KC * HID + HC * D)]
        x1t = part2([P, 2, 2, D])
        cnt = sb("cnt", [P, 2])
        rcnt = sb("rcnt", [P, 2])
        aggn = part2([P, 2, EA])
        aggT = part2([EA, 2, P])
        hT = part2([128, 2, HC, 2, P])
        st = sb("st", [P, 2, 6])
        mv2 = sb("mv2", [P, 2, 2])
        sd2 = sb("sd2", [P, 2])
        rs2 = sb("rs2", [P, 2])
        y2 = part2([P, 2, 2, D])
        ynT = part2([128, KC, 2, P])
        w_r = sb("w_r", [128, KC, NE])
        br_row = sb("br_row", [1, NE])
        gb_rows = sb("gb_rows", [1, 2, D])
        gb_col = sb("gb_col", [128, 2, KC])

        part2 = carver(arena2, NT * NE)
        best = part2([P, NE, K * NT])
        at = part2([P, NE, K * NT])
        left = part2([P, NT, NE])
        tmp = part2([P, NT, NE])
        top = part2([P, 2, 4, NT])
        b1_rows = arena2[:, arena2.shape[1] - NE * HID:]
        assert NT * NE + 2 * NE * K * NT + 2 * NT * NE + 8 * NT <= arena2.shape[1] - NE * HID
        b2_rows = arena[:, NE * (KC * HID + HC * D):NE * (KC * HID + HC * D) + NE * D]
        expert_iota = sb("expert_iota", [P, NE])
        tile_start = sb("tile_start", [1, ET])
        part4 = carver(agg[:, :, :].rearrange("p b f -> p (b f)"))
        send = part4([P, MOVE, D])
        send_at = sb("send_at", [P, MOVE, K], I32)
        place = part4([P, K, NT], I32)
        weight = part4([P, K, NT])
        ended = part4([1, ET, NE])
        expert_f = part4([1, ET])
        experts3 = part4([1, ET // 2, 4], I32)
        part3 = carver(x_or_xnT)
        row_in = part3([128, 2, D])
        zT = part3([128, 2, KC, TR])
        hb = part3([128, 2, HID])
        hg = part3([128, 2, HID])
        hgT = part3([128, 2, HC, TR])
        y_out = part3([128, 2, D])
        fetched = part3([P, MOVE, K, D])
        res = part3([P, MOVE, D])

        ps_rank = psum("ps_rank", [128, 512])
        ps_t = psum("ps_t", [128, 512])
        ps_kv = psum("ps_kv", [128, 512])
        ps_acc = [psum(f"ps_acc{c}", [128, 512]) for c in range(KC)]
        ps_vk = [ps_acc[0][:, 128 * c:128 * (c + 1)] for c in range(KC)]
        ps_sums = ps_acc[0][:, KC * 128:KC * 128 + 2 * KC]
        ps_y = (ps_kv, ps_rank)
        ps_g = [psum(f"ps_g{k}", [128, 512]) for k in range(RING - 1)] + [ps_acc[1]]

        s_src = sem("s_src")
        s_x = sem("s_x")
        s_w = sem("s_w")
        s_prefill = sem("s_prefill")
        s_stage = [sem(f"s_stage{k}") for k in range(SLOTS)]
        s_scat = [sem(f"s_scat{k}") for k in range(SLOTS)]
        s_copied = sem("s_copied")
        s_meta = sem("s_meta")
        s_const = sem("s_const")
        s_cst2 = sem("s_cst2")
        s_unit = [sem(f"s_unit{k}") for k in range(GROUPS)]
        s_hist = sem("s_hist")
        s_prefix = sem("s_prefix")
        s_rank = sem("s_rank")
        s_onehot = sem("s_onehot")
        s_group = sem("s_group")
        s_added = sem("s_added")
        s_dve = sem("s_dve")
        s_act = sem("s_act")
        s_stats = sem("s_stats")
        s_sd = sem("s_sd")
        s_wT = sem("s_wT")
        s_wTc = sem("s_wTc")
        s_wkv = sem("s_wkv")
        s_xn = sem("s_xn")
        s_xt = sem("s_xt")
        s_xtc = sem("s_xtc")
        s_kvp = sem("s_kvp")
        s_sq = sem("s_sq")
        s_ss = sem("s_ss")
        s_hsd = sem("s_hsd")
        s_kvn = sem("s_kvn")
        s_kvacc = sem("s_kvacc")
        s_kvsb = sem("s_kvsb")
        s_kshift = sem("s_kshift")
        s_krow = sem("s_krow")
        s_kvo = sem("s_kvo")
        s_kvoc = sem("s_kvoc")
        s_mixw = sem("s_mixw")
        s_mixwc = sem("s_mixwc")
        s_x2 = sem("s_x2")
        s_mix = sem("s_mix")
        s_mixed = sem("s_mixed")
        s_hb = sem("s_hb")
        s_hbc = sem("s_hbc")
        s_out = sem("s_out")
        s_gw = sem("s_gw")
        s_gb = sem("s_gb")
        s_gbc = sem("s_gbc")
        s_we = sem("s_we")
        s_x1in = [sem(f"s_x1in{a}") for a in range(2)]
        s_x1out = sem("s_x1out")
        s_aggn = sem("s_aggn")
        s_aggt = sem("s_aggt")
        s_aggtc = sem("s_aggtc")
        s_h = sem("s_h")
        s_relu = sem("s_relu")
        s_o = sem("s_o")
        s_x1done = sem("s_x1done")
        s_mv2 = sem("s_mv2")
        s_sd2 = sem("s_sd2")
        s_yn = sem("s_yn")
        s_keep = sem("s_keep")
        s_yt = sem("s_yt")
        s_ytc = sem("s_ytc")
        s_lg = sem("s_lg")
        s_lgc = sem("s_lgc")
        s_xt2 = [sem(f"s_xt2{a}") for a in range(2)]
        s_x1 = sem("s_x1")
        s_sortfill = sem("s_sortfill")
        s_b1 = sem("s_b1")
        s_chist = sem("s_chist")
        s_cprefix = sem("s_cprefix")
        s_diff = sem("s_diff")
        s_exp = sem("s_exp")
        s_place = sem("s_place")
        s_staged = sem("s_staged")
        s_sent = [sem(f"s_sent{m}") for m in range(MOVE)]
        s_rowin = [sem(f"s_rowin{a}") for a in range(2)]
        s_zt = sem("s_zt")
        s_ztc = sem("s_ztc")
        s_eh = sem("s_eh")
        s_ehb = sem("s_ehb")
        s_gelu = sem("s_gelu")
        s_gt = sem("s_gt")
        s_gtc = sem("s_gtc")
        s_ey = sem("s_ey")
        s_eyb = sem("s_eyb")
        s_eout = [sem(f"s_eout{a}") for a in range(2)]
        s_cat = sem("s_cat")
        s_fetch = [sem(f"s_fetch{m}") for m in range(MOVE)]
        s_res = [sem(f"s_res{m}") for m in range(MOVE)]
        s_comb = sem("s_comb")
        s_final = [sem(f"s_final{m}") for m in range(MOVE)]

        ea_v = edge_attr.rearrange("(p t) f -> p (t f)", p=P)
        buck_fill = buckets.rearrange("(s p q) f -> s p (q f)", s=SEGS, p=128)\
            .rearrange("s p (q w) -> s p q w", q=FILLS * QW)
        buck_units = buckets.rearrange("(g u p j) f -> g p u (j f)", u=2, p=128, j=2)
        ZW = SEG_ROWS * ROW // 128 // (FILLS * QW)
        SFILLS = 64
        SW = ET * D // SFILLS
        assert SW * SFILLS == ET * D and SW <= ZW
        NCONST = 13

        block = ctx.enter_context(nc.Block())

        def wait_apart(eng, sem, value):
            if not isinstance(value, int):
                value = eng.to_reg(value)
            eng.wait_ge(s_const, NCONST)
            eng.wait_ge(sem, value)

        def after(eng, sem, value):
            if not (isinstance(value, int) and value <= 0):
                eng.wait_ge(sem, value)

        def in_turn(eng, step, loop=None):
            for b in range(2):
                step(b, b, 0)
            with (loop or eng.Fori)(1, NB // 2 - 1) as i:
                for a in range(2):
                    step(2 * i + a, a, i)
            for b in range(NB // 2 * 2 - 2, NB):
                step(b, b % 2, b // 2)

        def known_below(b, n):
            return isinstance(b, int) and b < n

        def known_from(b, n):
            return isinstance(b, int) and b >= n

        def experts_of(kind):
            def load(i):
                _, e = nc.values_load_multi_w_load_instructions(
                    experts3[0:1, bass.ds(i, 1), :].rearrange("p i e -> p (i e)"), engines=(kind,), min_val=0,
                    max_val=NE - 1, skip_runtime_bounds_check_because="they are cut off at NE - 1")
                return e
            return load

        def pairwise(eng, step, last, load=lambda i: (None,) * 4):
            e = load(0)
            for a in range(2):
                step(a, a, 0, e[a:])
            with eng.Fori(1, last // 2) as i:
                e = load(i)
                for a in range(2):
                    step(2 * i + a, a, i, e[a:])

        @block.sync
        def _(sp):
            def load_chunk(k, col):
                src_cols = ea_v[:, bass.ds(col * EA, CH * EA)]
                dst = stage[:, k].rearrange("p c f -> p (c f)")
                sp.dma_start(dst[0:112, :], src_cols[0:112, :]).then_inc(s_stage[k], 16)
                sp.dma_start(dst[112:P, :], src_cols[112:P, :]).then_inc(s_stage[k], 16)

            sort_fill = sorted_y.rearrange("(p q) d -> p (q d)", p=128).rearrange("p (q w) -> p q w", w=SW)

            def prefill(s):
                if not isinstance(s, int) or s > 0:
                    sp.wait_ge(s_prefill, s * (FILLS * 16))
                if isinstance(s, int) and s < 2:
                    pass
                else:
                    part_of = SFILLS // (SEGS - 2)
                    sp.dma_start(sort_fill[:, bass.ds((s - 2) * part_of, part_of), :],
                                 zeros[:, 0:SW].unsqueeze(1).to_broadcast([128, part_of, SW])).then_inc(s_sortfill, 16)
                for q in range(FILLS):
                    sp.dma_start(buck_fill[bass.ds(s, 1), :, q * QW:(q + 1) * QW, :].rearrange("s p q w -> (s p) q w"),
                                 zeros[:, :].unsqueeze(1).to_broadcast([128, QW, ZW])).then_inc(s_prefill, 16)

            def load_unit(g, k):
                sp.wait_ge(s_group, g + 1)
                sp.dma_start(unit[:, k].rearrange("p (u j) f -> p u (j f)", u=2),
                             buck_units[bass.ds(g, 1)].rearrange("g p u q -> (g p) u q")).then_inc(s_unit[k], 16)

            sp.dma_start(pos[:, :], src.rearrange("(p t) -> p t", p=P)).then_inc(s_src, 16)
            for k in range(SLOTS):
                load_chunk(k, k * CH)
            sp.wait_ge(s_const, 1)
            prefill(0)
            for a in range(5):
                sp.dma_start(xs[:, 10 * a:10 * a + 10, :],
                             x.rearrange("(t p) d -> p t d", p=P)[:, 10 * a:10 * a + 10, :]).then_inc(s_x, 16)

            def load(dst, src_ap):
                sp.dma_start(dst, src_ap).then_inc(s_w, 16)
            for n, w in enumerate((wk, wv, wo)):
                load(raw[:, n], w.rearrange("(c p) i -> p c i", p=128))
            load(w_q[:, :, :], wq.rearrange("(c p) i -> p c i", p=128))
            load(w1x[:, :, :], gnn_W1[0:D, :].rearrange("(c p) h -> p c h", p=128))
            load(w1e[:, :], gnn_W1[D:D + EA, :])
            load(w1u[:, :], gnn_W1[D + EA:, :])
            load(w2[:, :, :], gnn_W2.rearrange("(c p) d -> p c d", p=128))
            load(u_col[:, :], gnn_u[0, :].rearrange("(p a) -> p a", a=1))
            load(b1_row[:, :], gnn_b1.rearrange("(a d) -> a d", a=1))
            load(bias_rows[0:1, 0, :], bo.rearrange("(a d) -> a d", a=1))
            load(bias_rows[0:1, 1, :], gnn_b2.rearrange("(a d) -> a d", a=1))
            for n, row in enumerate((k_g, k_b)):
                load(k_rows[:, n, :], row.rearrange("(a d) -> a d", a=1).to_broadcast([128, HD]))
            for n, row in enumerate((k_g, k_b, v_g, v_b)):
                for h in range(2):
                    load(kv_cols[h * HD:(h + 1) * HD, n:n + 1], row.rearrange("(p a) -> p a", a=1))

            x_tiles = x.rearrange("(j p) d -> j p d", p=P)
            x1_tiles = x1.rearrange("(j p) d -> j p d", p=P)

            def load_g(dst, src_ap):
                sp.dma_start(dst, src_ap).then_inc(s_gw, 16)
            load_g(w_r[:, :, :], Wr.rearrange("(c p) e -> p c e", p=128))
            load_g(br_row[:, :], br.rearrange("(a e) -> a e", a=1))
            load_g(gb_rows[0:1, 0, :], gamma.rearrange("(a d) -> a d", a=1))
            load_g(gb_rows[0:1, 1, :], beta.rearrange("(a d) -> a d", a=1))

            def step(s, i, units, last=False, mix2=False):
                j = (s - SEGS // 2) * (2 * STEPS) + i * 2
                if mix2:
                    for a in range(2):
                        sp.wait_ge(s_x1, (j + 1) * 16)
                        sp.dma_start(xt[:, a, :], x_tiles[bass.ds(j + a, 1)].rearrange("a p d -> (a p) d"))\
                            .then_inc(s_xt2[a], 16)
                if units:
                    for k in range(GROUPS):
                        load_unit((s * STEPS + i - BEHIND) * GROUPS + k, k)
                if not last:
                    for k in range(SLOTS):
                        sp.wait_ge(s_copied, s * (STEPS * SLOTS) + i * SLOTS + k + 1)
                        load_chunk(k, s * SC + (i * SLOTS + SLOTS + k) * CH)
                if mix2:
                    for a in range(2):
                        sp.wait_ge(s_mixed, j + a + 2)
                        sp.dma_start(x1_tiles[bass.ds(j + a, 1)].rearrange("a p d -> (a p) d"), xt[:, a, :])\
                            .then_inc(s_x1, 16)

            def scattered(s):
                for k in range(SLOTS):
                    value = (s + 1) * (STEPS * CH * 16)
                    if isinstance(s, int):
                        sp.wait_ge(s_scat[k], value)
                    else:
                        wait_apart(sp, s_scat[k], value)

            prefill(1)
            with sp.Fori(0, STEPS) as i:
                step(0, i, False)
            for first, end in ((1, 2), (2, SEGS // 2), (SEGS // 2, SEGS - 1)):
                with sp.Fori(first, end) as s:
                    prefill(s + 1)
                    step(s, 0, first > 1, mix2=first >= SEGS // 2)
                    scattered(s - 1)
                    with sp.Fori(1, STEPS) as i:
                        step(s, i, True, mix2=first >= SEGS // 2)
            step(SEGS - 1, 0, True, mix2=True)
            scattered(SEGS - 2)
            with sp.Fori(1, STEPS - 1) as i:
                step(SEGS - 1, i, True, mix2=True)
            step(SEGS - 1, STEPS - 1, True, last=True, mix2=True)
            step(SEGS, 0, True, last=True)
            scattered(SEGS - 1)
            with sp.Fori(1, BEHIND) as i:
                step(SEGS, i, True, last=True)
            sp.wait_ge(s_x1, (NT + 1) * 16)
            x1_pairs = x1.rearrange("(b t p) d -> b p t d", p=P, t=2)

            def load_x1(b, a):
                sp.dma_start(x1t[:, a], x1_pairs[bass.ds(b, 1)].rearrange("b p t d -> (b p) t d")).then_inc(s_x1in[a], 16)

            def store_x1(b, a):
                sp.wait_ge(s_x1done, b + 1)
                sp.dma_start(x1_pairs[bass.ds(b, 1)].rearrange("b p t d -> (b p) t d"), x1t[:, a]).then_inc(s_x1out, 16)
                sp.wait_ge(s_x1out, (b + 1) * 16)
                wait_apart(sp, s_yn, b + 1)

            load_x1(0, 0)
            load_x1(1, 1)
            sp.wait_ge(s_added, RING - 1 + SEGS * STEPS * GROUPS)
            for c in range(KC):
                sp.dma_start(W1_all.rearrange("p (e c h) -> p e c h", c=KC, h=HID)[:, :, c, :],
                             W1.rearrange("e (c p) h -> p e c h", p=128)[:, :, c, :]).then_inc(s_we, 16)
            for c in range(HC):
                sp.dma_start(W2_all.rearrange("p (e c d) -> p e c d", c=HC, d=D)[:, :, c, :],
                             W2.rearrange("e (c p) d -> p e c d", p=128)[:, :, c, :]).then_inc(s_we, 16)
            sp.dma_start(b2_rows, b2.rearrange("(a e) d -> a (e d)", a=1).to_broadcast([128, NE * D])).then_inc(s_we, 16)
            with sp.Fori(0, NB // 2 - 1) as i:
                for a in range(2):
                    store_x1(2 * i + a, a)
                    load_x1(2 * i + a + 2, a)
            for a in range(2):
                store_x1(NB - 3 + a, a)
                if a == 0:
                    load_x1(NB - 1, 0)
            store_x1(NB - 1, 0)
            sp.wait_ge(s_lgc, NB)
            sp.dma_start(b1_rows, b1.rearrange("(a e) h -> a (e h)", a=1).to_broadcast([128, NE * HID])).then_inc(s_b1, 16)
            for m in range(MOVE):
                sp.wait_ge(s_sent[m], NT // MOVE * K * 16)
            row_tiles = sorted_y.rearrange("(r p) d -> r p d", p=TR)
            out_tiles = expert_out.rearrange("(r p) d -> r p d", p=TR)

            def load_rows(r, a):
                sp.dma_start(row_in[:, a, :], row_tiles[bass.ds(r, 1)].rearrange("a p d -> (a p) d"))\
                    .then_inc(s_rowin[a], 16)

            def store_rows(r, a):
                sp.wait_ge(s_eyb, r + 1)
                sp.dma_start(out_tiles[bass.ds(r, 1)].rearrange("a p d -> (a p) d"), y_out[:, a, :])\
                    .then_inc(s_eout[a], 16)

            def expert_rows(r, a, i, e):
                sp.wait_ge(s_zt, r + 1)
                load_rows(r + 2, a)
                store_rows(r, a)

            for a in range(2):
                load_rows(a, a)
            pairwise(sp, expert_rows, ET - 2)
            for a in range(2):
                store_rows(ET - 2 + a, a)

            def combine(i):
                for m in range(MOVE):
                    after(sp, s_final[m], i * 16)
                    sp.dma_start(res[:, m, :], x1_tiles[bass.ds(i * MOVE + m, 1)].rearrange("a p d -> (a p) d"))\
                        .then_inc(s_res[m], 16)
                for m in range(MOVE):
                    sp.wait_ge(s_comb, i * MOVE + m + 1)
                    sp.dma_start(out_nodes[bass.ds(i * MOVE + m, 1)].rearrange("a p d -> (a p) d"), res[:, m, :])\
                        .then_inc(s_final[m], 16)

            out_nodes = out.rearrange("(j p) d -> j p d", p=P)
            combine(0)
            with sp.Fori(1, NT // MOVE) as i:
                combine(i)
            for m in range(MOVE):
                sp.wait_ge(s_final[m], NT // MOVE * 16)

        @block.gpsimd
        def _(pool):
            pool.memset(zeros[:, :], 0.0).then_inc(s_const, 1)
            for k, (free, n) in enumerate([(s_x1, 16), (s_mixed, 1), (s_ss, 1), (s_mix, 1), (s_xt, 1), (s_kvacc, 1),
                                           (s_added, RING - 1 - LAG)]):
                pool.memset(spare[0:1, k:k + 1], 0.0).then_inc(free, n)
            pool.memset(ident[:, :], 0.0).then_inc(s_cst2, 1)
            pool.memset(below[:, :], 0.0).then_inc(s_cst2, 1)
            pool.memset(eps_col[:, :], EPS).then_inc(s_const, 1)
            pool.memset(eps2_col[:, :], EPS * EPS).then_inc(s_const, 1)
            pool.memset(ones[:, :], 1.0).then_inc(s_const, 1)
            pool.memset(rows[:, :, :, :], 1.0).then_inc(s_const, 1)
            pool.iota(node_iota[:, :], [[1, OH]], base=0, channel_multiplier=0,
                      allow_small_or_imprecise_dtypes=True).then_inc(s_const, 1)
            pool.iota(bucket_iota[:, :], [[1, NB]], base=0, channel_multiplier=0,
                      allow_small_or_imprecise_dtypes=True).then_inc(s_const, 1)
            pool.iota(unit_start[:, :], [[UR, NU]], base=0, channel_multiplier=0,
                      allow_small_or_imprecise_dtypes=True).then_inc(s_const, 1)
            pool.iota(expert_iota[:, :], [[1, NE]], base=0, channel_multiplier=0,
                      allow_small_or_imprecise_dtypes=True).then_inc(s_const, 1)
            pool.iota(tile_start[:, :], [[TR, ET]], base=0, channel_multiplier=0,
                      allow_small_or_imprecise_dtypes=True).then_inc(s_const, 1)
            pool.iota(rk_i[:, 0:SEGS], [[SEG_ROWS // 128, SEGS]], base=0, channel_multiplier=0).then_inc(s_cst2, 1)
            pool.wait_ge(s_cst2, 3)
            pool.affine_select(out=ident[:, :], in_=ident[:, :], compare_op=ALU.not_equal, fill=1.0,
                               base=0, pattern=[[-1, 128]], channel_multiplier=1).then_inc(s_const, 1)
            pool.affine_select(out=below[:, :], in_=below[:, :], compare_op=ALU.is_ge, fill=1.0,
                               base=0, pattern=[[-1, P]], channel_multiplier=1).then_inc(s_const, 1)
            pool.tensor_scalar(seg_start[:, :], rk_i[:, 0:SEGS], 128.0, 0.0, ALU.mult, ALU.add).then_inc(s_const, 1)
            with pool.Fori(0, SEGS) as s:
                wait_apart(pool, s_prefill, (s + 1) * (FILLS * 16))
                with pool.Fori(0, STEPS) as i:
                    for k in range(SLOTS):
                        c = s * (STEPS * SLOTS) + i * SLOTS + k
                        pool.wait_ge(s_copied, c + 1)
                        wait_apart(pool, s_meta, (c + 1) * 2)
                        for e in range(CH):
                            pool.indirect_dma_start(buckets[:, :], bass.IndirectOffsetOnAxis(rows_at[:, k, e:e + 1], 0),
                                                    rows[:, k, e, :], None).then_inc(s_scat[k], 16)

            pool.wait_ge(s_sortfill, (SEGS - 2) * 16)

            def dispatch(i):
                for m in range(MOVE):
                    wait_apart(pool, s_staged, (i * MOVE + m + 1) * 2)
                    for k in range(K):
                        pool.indirect_dma_start(sorted_y[:, :], bass.IndirectOffsetOnAxis(send_at[:, m, k:k + 1], 0),
                                                send[:, m, :], None).then_inc(s_sent[m], 16)

            with pool.Fori(0, NT // MOVE) as i:
                dispatch(i)
            for a in range(2):
                pool.wait_ge(s_eout[a], ET // 2 * 16)

            def fetch(i):
                for m in range(MOVE):
                    if not isinstance(i, int):
                        wait_apart(pool, s_comb, (i - 1) * MOVE + m + 1)
                    wait_apart(pool, s_cat, i * MOVE + m + 1)
                    for k in range(K):
                        pool.indirect_dma_start(fetched[:, m, k, :], None, expert_out[:, :],
                                                bass.IndirectOffsetOnAxis(send_at[:, m, k:k + 1], 0)).then_inc(s_fetch[m], 16)

            fetch(0)
            with pool.Fori(1, NT // MOVE) as i:
                fetch(i)

        @block.scalar
        def _(act):
            did = Steps(act, s_act)
            act.wait_ge(s_const, NCONST)

            def chunk(s, i, k):
                c = s * (STEPS * SLOTS) + i * SLOTS + k
                n = s * STEPS + i
                act.wait_ge(s_stage[k], (n + 1) * 32)
                after(act, s_scat[k], n * (CH * 16))
                nc.scalar.copy(rows[:, k, :, 0:EA], stage[:, k, :, :]).then_inc(s_copied, 1)
                col = s * SC + (i * SLOTS + k) * CH
                nc.scalar.copy(rows[:, k, :, EA + 1:ROW],
                               local[:, bass.ds(col, CH)].rearrange("p (c a) -> p c a", a=1)).then_inc(s_meta, 1)
                nc.scalar.copy(rows_at[:, k, :], pos[:, bass.ds(col, CH)]).then_inc(s_meta, 1)

            def pass1(j, a):
                act.wait_ge(s_xt, j + 2)
                pt = ps_t[:, 0:KC * P].rearrange("p (c n) -> p c n", c=KC)
                nc.scalar.copy(xnT_t[:, a], pt).then_inc(s_xtc, 1)
                nc.scalar.copy(xnT[:, bass.ds(j, 1)].rearrange("p a c n -> p (a c) n"), pt).then_inc(s_xtc, 1)
                act.wait_ge(s_kvp, j + 1)
                act.wait_ge(s_ss, j + 1)
                nc.scalar.activation(sq[:, :], ps_kv[0:P, :], ACT.Square).then_inc(s_sq, 1)
                act.wait_ge(s_ss, j + 2)
                nc.scalar.activation(hsd[:, :], ss[:, :], ACT.Sqrt, bias=eps_col[:, :], scale=1.0 / HD).then_inc(s_hsd, 1)

            def pass2(j, a):
                act.wait_ge(s_mix, j + 1)
                nc.scalar.copy(xnT_t[:, a], xnT[:, bass.ds(j, 1)].rearrange("p a c n -> p (a c) n")).then_inc(s_x2, 1)

            def step(s, i, mix, rank_first=False):
                for k in range(SLOTS):
                    chunk(s, i, k)
                for a in range(2):
                    if mix == 1:
                        pass1(s * (2 * STEPS) + i * 2 + a, a)
                    else:
                        pass2((s - SEGS // 2) * (2 * STEPS) + i * 2 + a, a)

            act.wait_ge(s_rank, 1)
            for k in range(SLOTS):
                chunk(0, 0, k)
            for n in range(3):
                act.wait_ge(s_wT, n + 1)
                dst = (w_kv[:, :, 0:D], w_kv[:, :, D:2 * D], w_oT[:, :, :])[n]
                nc.scalar.copy(dst, ps_t[:, :].rearrange("p (c d) -> p c d", c=KC)).then_inc(s_wTc, 1)
            for k in range(SLOTS):
                chunk(0, 1, k)
            act.wait_ge(s_stats, 1)
            nc.scalar.activation(sd[:, :], mv[:, :, 1], ACT.Sqrt, bias=eps_col[:, :]).then_inc(s_sd, 1)
            act.wait_ge(s_hb, 1)
            nc.scalar.activation(h_bias[:, :], ps_kv[:, 0:HC], ACT.Copy).then_inc(s_hbc, 1)
            for j in range(4):
                pass1(j, j % 2)
            with act.Fori(2, STEPS) as i:
                step(0, i, 1)
            with act.Fori(1, SEGS // 2) as s:
                act.wait_ge(s_rank, s + 1)
                with act.Fori(0, STEPS) as i:
                    step(s, i, 1)
            for c in range(KC):
                act.wait_ge(s_kvo, KC)
                nc.scalar.copy(kvo[:, c, :], ps_t[:, c * D:(c + 1) * D]).then_inc(s_kvoc, 1)
            for c in range(KC):
                act.wait_ge(s_mixw, KC)
                nc.scalar.copy(mix_w[:, c, :], ps_kv[:, c * D:(c + 1) * D]).then_inc(s_mixwc, 1)
            with act.Fori(SEGS // 2, SEGS) as s:
                act.wait_ge(s_rank, s + 1)
                with act.Fori(0, STEPS) as i:
                    step(s, i, 2)
            act.wait_ge(s_gb, 1)
            nc.scalar.copy(gb_col[:, :, :], ps_t[:, 0:2 * KC].rearrange("p (n c) -> p n c", n=2)).then_inc(s_gbc, 1)

            def keep_agg(b):
                act.wait_ge(s_aggt, b + 1)
                nc.scalar.copy(aggT[:, :, :], ps_rank[0:EA, 0:2 * P].rearrange("p (t n) -> p t n", t=2)).then_inc(s_aggtc, 1)

            def relu(b, a):
                after(act, s_o, b - 1)
                for hc in range(HC):
                    if hc % 2 == 0:
                        act.wait_ge(s_h, b * 2 + hc // 2 + 1)
                    nc.scalar.activation(hT[:, a, hc].rearrange("p t n -> p (t n)"),
                                         ps_acc[hc // 2][:, (hc % 2) * BN:(hc % 2 + 1) * BN], ACT.Relu,
                                         bias=h_bias[:, hc:hc + 1]).then_inc(s_relu, 1)

            def keep_y(b, a):
                act.wait_ge(s_yn, b + 1)
                nc.scalar.copy(xs[:, bass.ds(b * 2, 2), :], y2[:, a]).then_inc(s_keep, 1)
                after(act, s_lg, b)
                act.wait_ge(s_yt, b + 1)
                for c in range(KC):
                    nc.scalar.activation(ynT[:, c].rearrange("p t n -> p (t n)"), ps_t[:, c * BN:(c + 1) * BN],
                                         ACT.Identity, scale=gb_col[:, 0, c:c + 1],
                                         bias=gb_col[:, 1, c:c + 1]).then_inc(s_ytc, 1)

            def keep_logits(b):
                act.wait_ge(s_lg, b + 1)
                nc.scalar.copy(logits[:, bass.ds(b * 2, 2), :],
                               ps_kv[0:P, 0:2 * NE].rearrange("p (t e) -> p t e", t=2)).then_inc(s_lgc, 1)

            def bucket(b, a, i):
                if not known_from(b, NB - 1):
                    relu(b + 1, 1 - a)
                if not known_below(b, 2):
                    keep_logits(b - 2)
                if not known_from(b, NB - 2):
                    keep_agg(b + 2)
                if not known_below(b, 1):
                    keep_y(b - 1, 1 - a)
                act.wait_ge(s_mv2, b + 1)
                nc.scalar.activation(sd2[:, :], mv2[:, :, 1], ACT.Sqrt, bias=eps2_col[:, :], scale=1.0 + EPS).then_inc(s_sd2, 1)

            keep_agg(0)
            relu(0, 0)
            keep_agg(1)
            in_turn(act, bucket)
            keep_logits(NB - 2)
            keep_y(NB - 1, (NB - 1) % 2)
            keep_logits(NB - 1)
            act.wait_ge(s_diff, 1)
            nc.scalar.activation(top[:, 1, 1, :], top[:, 1, 0, :], ACT.Exp).then_inc(s_exp, 1)

            def stage_rows(i):
                for m in range(MOVE):
                    after(act, s_sent[m], i * (K * 16))
                    t = i * MOVE + m
                    nc.scalar.copy(send[:, m, :], xs[:, bass.ds(t, 1), :].rearrange("p a d -> p (a d)")).then_inc(s_staged, 1)
                    nc.scalar.copy(send_at[:, m, :], place[:, :, bass.ds(t, 1)].rearrange("p k a -> p (k a)")).then_inc(s_staged, 1)

            act.wait_ge(s_place, 1)
            stage_rows(0)
            with act.Fori(1, NT // MOVE) as i:
                stage_rows(i)

            def scale_rows(r, a):
                act.wait_ge(s_zt, r + 1)
                after(act, s_eh, r - 1)
                for c in range(KC):
                    nc.scalar.activation(zT[:, a, c, :], ps_t[:, c * TR:(c + 1) * TR], ACT.Identity,
                                         scale=gb_col[:, 0, c:c + 1], bias=gb_col[:, 1, c:c + 1]).then_inc(s_ztc, 1)

            def gelu(r, a):
                act.wait_ge(s_ehb, r + 1)
                after(act, s_gt, r - 1)
                nc.scalar.activation(hg[:, a, :], hb[:, a, :], ACT.Gelu).then_inc(s_gelu, 1)

            def expert_tile(r, a, i, e):
                gelu(r + 1, 1 - a)
                scale_rows(r + 2, a)

            for m in range(MOVE):
                act.wait_ge(s_sent[m], NT // MOVE * K * 16)
            scale_rows(0, 0)
            scale_rows(1, 1)
            gelu(0, 0)
            pairwise(act, expert_tile, ET - 2)
            gelu(ET - 1, 1)

            def place_back(i):
                for m in range(MOVE):
                    after(act, s_fetch[m], i * (K * 16))
                    nc.scalar.copy(send_at[:, m, :],
                                   place[:, :, bass.ds(i * MOVE + m, 1)].rearrange("p k a -> p (k a)")).then_inc(s_cat, 1)

            place_back(0)
            with act.Fori(1, NT // MOVE) as i:
                place_back(i)

        @block.vector
        def _(dve):
            did = Steps(dve, s_dve)
            v = nc.vector

            def rank_stages(s):
                cols = pos[:, bass.ds(s * SC, SC)]
                did.did(v.tensor_scalar(kq[:, :], cols, 1.0 / BN, None, ALU.mult))
                yield
                did.wait()
                did.did(v.scalar_tensor_tensor(kf[:, 0], kq[:, :], -float(BN), cols, ALU.mult, ALU.add))
                yield
                did.wait()
                did.did(v.tensor_scalar(kf[:, 1], kf[:, 0], 0.0, None, ALU.is_lt))
                yield
                did.wait()
                did.did(v.scalar_tensor_tensor(kf[:, 2], kf[:, 1], float(BN), kf[:, 0], ALU.mult, ALU.add))
                did.did(v.scalar_tensor_tensor(kf[:, 3], kf[:, 1], -1.0, kq[:, :], ALU.mult, ALU.add))
                yield
                did.wait()
                did.did(v.tensor_scalar(kf[:, 0], kf[:, 2], float(BN), None, ALU.is_ge))
                yield
                did.wait()
                did.did(v.scalar_tensor_tensor(local[:, bass.ds(s * SC, SC)], kf[:, 0], -float(BN), kf[:, 2],
                                               ALU.mult, ALU.add))
                did.did(v.tensor_tensor(kf[:, 1], kf[:, 3], kf[:, 0], ALU.add))
                yield
                did.wait()
                did.did(v.tensor_tensor(mask[:, :, :], kf[:, 1:2, :].to_broadcast([P, NB, SC]),
                                        bucket_iota[:, :].unsqueeze(2).to_broadcast([P, NB, SC]), ALU.is_equal))
                yield
                did.wait()
                flat = mask[:, :, :].rearrange("p b t -> p (b t)")
                did.did(v.tensor_tensor_scan(count[:, :, :].rearrange("p b t -> p (b t)"), flat, flat, 0.0,
                                             ALU.add, ALU.max))
                yield
                did.wait()
                up_to = count[:, :, SC - 1]
                did.did(v.tensor_copy(hist[:, 0:1], up_to[:, 0:1]))
                v.tensor_tensor(hist[:, 1:], up_to[:, 1:], up_to[:, 0:NB - 1], ALU.subtract).then_inc(s_hist, 1)
                yield PREFIX
                dve.wait_ge(s_prefix, s + 1)
                lanes_before, total = ps_rank[0:P, 0:NB], ps_rank[0:P, NB:2 * NB]
                did.did(v.tensor_scalar(rk_i[:, :], total, float(UR - 1), None, ALU.add))
                did.did(v.scalar_tensor_tensor(rk[:, 3], hist[:, :], seg_start[:, bass.ds(s, 1)], up_to,
                                               ALU.add, ALU.subtract))
                yield
                did.wait()
                did.did(v.tensor_scalar(rk_i[:, :], rk_i[:, :], 8, 8, ALU.logical_shift_right, ALU.logical_shift_left))
                yield
                did.wait()
                did.did(v.tensor_copy(rk[:, 0], rk_i[:, :]))
                yield
                did.wait()
                did.did(v.tensor_tensor_scan(rk[:, 2], rk[:, 0], rk[:, 0], 0.0, ALU.add, ALU.max))
                did.did(v.scalar_tensor_tensor(rk[:, 4], lanes_before, -1.0, rk[:, 0], ALU.add, ALU.subtract))
                yield
                did.wait()
                did.did(v.tensor_tensor(rk[:, 5], rk[:, 2], rk[:, 3], ALU.add))
                yield
                did.wait()
                did.did(v.tensor_tensor(rk[:, 6], rk[:, 5], rk[:, 4], ALU.add))
                yield
                did.wait()
                did.did(v.tensor_tensor(count[:, :, :], count[:, :, :],
                                        rk[:, 6, :].unsqueeze(2).to_broadcast([P, NB, SC]), ALU.add))
                yield
                did.wait()
                did.did(v.tensor_tensor(count[:, :, :], count[:, :, :], mask[:, :, :], ALU.mult))
                yield
                did.wait()
                did.did(v.tensor_tensor(filled[:, :, :], rk[0:1, 2:3, :].to_broadcast([1, NU, NB]),
                                        unit_start[:, :].unsqueeze(2).to_broadcast([1, NU, NB]), ALU.is_le))
                yield
                did.wait()
                did.did(v.tensor_reduce(ustart_f[:, :], filled[:, :, :], AX_X, ALU.add))
                with nc.allow_low_precision(reason="whole numbers below 2^24"):
                    did.did(v.tensor_reduce(pos[:, bass.ds(s * SC, SC)], count[:, :, :].rearrange("p b t -> p t b"),
                                            AX_X, ALU.add))
                yield
                did.wait()
                started = ustart_f[:, :].rearrange("p (i u) -> p i u", i=STEPS)
                late = 2 * LAG
                did.did(v.tensor_scalar(agg_off[:, bass.ds((s * STEPS + 1) * STEP_OFF, STEPS * STEP_OFF)]
                                        .rearrange("p (i u) -> p i u", i=STEPS)[:, :, 0:late],
                                        started[:, :, 2 * GROUPS - late:], float(AGG), None, ALU.mult))
                v.tensor_scalar(agg_off[:, bass.ds(s * (STEPS * STEP_OFF), STEPS * STEP_OFF)]
                                .rearrange("p (i u) -> p i u", i=STEPS)[:, :, late:2 * GROUPS],
                                started[:, :, 0:2 * GROUPS - late], float(AGG), None, ALU.mult).then_inc(s_rank, 1)
                if isinstance(s, int):
                    dve.wait_ge(s_rank, s + 1)
                else:
                    wait_apart(dve, s_rank, s + 1)

            def rank(s):
                for _ in rank_stages(s):
                    pass

            RANK = 25

            def pair(n, k, offs):
                g = n * GROUPS + k
                dve.wait_ge(s_unit[k], (n + 1) * 16)
                dve.wait_ge(s_group, g + CREDIT - 2)
                did.did(v.tensor_tensor(rest[:, k % RING], unit[:, k], unit_hi[:, k], ALU.subtract))
                for t in range(3):
                    v.tensor_scalar(onehot[:, k % RING, t, :], node_iota[:, :], unit[:, k, t, EA + 1:ROW], None,
                                    ALU.is_equal)
                add_unit(g - LAG, (k - LAG) % GROUPS, 0, offs[2 * k])
                v.tensor_scalar(onehot[:, k % RING, 3, :], node_iota[:, :], unit[:, k, 3, EA + 1:ROW], None,
                                ALU.is_equal)
                did.wait()
                v.tensor_tensor(rest_lo[:, k % RING], rest[:, k % RING], rest_hi[:, k % RING], ALU.subtract)\
                    .then_inc(s_onehot, 1)
                add_unit(g - LAG, (k - LAG) % GROUPS, 1, offs[2 * k + 1])

            aggf = agg[:, :, :].rearrange("p b f -> p (b f)")

            def slots_of(n):
                _, offs = nc.values_load_multi_w_load_instructions(
                    agg_off[0:1, bass.ds(n * STEP_OFF, STEP_OFF)], engines=(mybir.EngineType.DVE,),
                    min_val=0, max_val=NB * AGG, skip_runtime_bounds_check_because="rank() writes only slots' offsets")
                return offs

            def add_unit(g, k, u, off):
                if u == 0:
                    dve.wait_ge(s_group, g + CREDIT + 1)
                    dve.wait_ge(s_added, g + RING - 1)
                slot = aggf[:, bass.ds(off, AGG)]
                add = v.tensor_tensor(slot, slot, ps_g[k % RING][0:P, u * AGG:(u + 1) * AGG], ALU.add)
                if u == 0:
                    did.did(add)
                else:
                    add.then_inc(s_added, 1)

            def mix_stages(j, a):
                def normalise():
                    dve.wait_ge(s_xt, j + 1)
                    v.tensor_scalar(xn[:, a], xs[:, bass.ds(j, 1), :].rearrange("p a d -> p (a d)"),
                                    mv[:, bass.ds(j, 1), 0], rstd[:, bass.ds(j, 1)],
                                    ALU.subtract, ALU.mult).then_inc(s_xn, 1)

                def squares():
                    dve.wait_ge(s_sq, j + 1)
                    v.tensor_reduce(ss[:, :], sq[:, :].rearrange("p (h d) -> p h d", d=HD), AX_X, ALU.add)\
                        .then_inc(s_ss, 1)

                def kv():
                    dve.wait_ge(s_hsd, j + 1)
                    did.did(v.reciprocal(hrs[:, :], hsd[:, :]))
                    did.wait()
                    dve.wait_ge(s_kvacc, j + 1)
                    dst = kvn[:, a].rearrange("p (h d) -> p h d", d=HD)
                    v.tensor_tensor(dst, ps_kv[0:P, :].rearrange("p (h d) -> p h d", d=HD),
                                    hrs[:, :].unsqueeze(2).to_broadcast([P, 8, HD]), ALU.mult).then_inc(s_kvn, 1)

                return {0: normalise, 3: squares, 4: kv}

            def mix2(j, a, n):
                dve.wait_ge(s_mix, j + 2)
                dve.wait_ge(s_xt2[a], (n + 1) * 16)
                v.tensor_tensor(xt[:, a], xt[:, a], ps_kv[0:P, a * D:(a + 1) * D], ALU.add).then_inc(s_mixed, 1)

            def step(s, i, mix, groups, ranking=None):
                if mix == 1:
                    j = s * (2 * STEPS) + i * 2
                    todo = mix_stages(j, 0)
                    todo.update({k + 5: f for k, f in mix_stages(j + 1, 1).items()})
                elif mix == 2:
                    j = (s - SEGS // 2) * (2 * STEPS) + i * 2
                    n2 = (s - SEGS // 2) * STEPS + i
                    todo = {2: lambda: mix2(j, 0, n2), 7: lambda: mix2(j + 1, 1, n2)}
                else:
                    todo = {}
                n = s * STEPS + i - BEHIND
                for k in range(GROUPS):
                    if groups:
                        if k == 0:
                            offs = slots_of(n)
                        pair(n, k, offs)
                    if k in todo:
                        todo[k]()
                    if ranking is not None:
                        ranking(i)

            def segment(s, mix, groups):
                stages = rank_stages(s + 1)
                at_prefix = []

                def ranking(i):
                    if at_prefix and i < PREFIX_STEP:
                        return
                    if next(stages, None) is PREFIX:
                        at_prefix.append(True)

                for i in range(STEPS):
                    step(s, i, mix, groups and not (isinstance(s, int) and s * STEPS + i < BEHIND), ranking)
                    if i == PREFIX_STEP - 1:
                        assert at_prefix
                assert next(stages, PREFIX + 1) == PREFIX + 1

            G_STEP = 2 * GROUPS
            M_STEP = 2

            did.did(v.memset(agg_off[:, :], NB * AGG))
            did.did(v.memset(agg[:, 0:1, :], 0.0))
            v.memset(agg[:, 1:, :], 0.0).then_inc(s_group, CREDIT)
            for k in range(GROUPS - LAG, GROUPS):
                did.did(v.memset(ps_g[k % RING][:, :], 0.0))
            dve.wait_ge(s_const, NCONST)
            dve.wait_ge(s_src, 16)
            rank(0)
            dve.wait_ge(s_x, 80)
            with did.loop(0, NT, 1) as j:
                did.did(v.bn_stats(stats[:, bass.ds(j, 1), :].rearrange("p a d -> p (a d)"),
                                   xs[:, bass.ds(j, 1), :].rearrange("p a d -> p (a d)")))
            did.wait()
            did.did(v.tensor_tensor(mv[:, :, 0], stats[:, :, 1], stats[:, :, 4], ALU.add))
            did.did(v.tensor_tensor(mv[:, :, 1], stats[:, :, 1], stats[:, :, 4], ALU.subtract))
            did.did(v.tensor_tensor(rstd[:, :], stats[:, :, 2], stats[:, :, 5], ALU.add))
            did.wait()
            did.did(v.tensor_scalar(mv[:, :, 0], mv[:, :, 0], 0.5, None, ALU.mult))
            did.did(v.tensor_tensor(sd[:, :], mv[:, :, 1], mv[:, :, 1], ALU.mult))
            did.wait()
            did.did(v.tensor_scalar(sd[:, :], sd[:, :], 0.25, None, ALU.mult))
            did.wait()
            v.scalar_tensor_tensor(mv[:, :, 1], rstd[:, :], 1.0 / D, sd[:, :], ALU.mult, ALU.add).then_inc(s_stats, 1)
            dve.wait_ge(s_wTc, 2)
            for c in range(KC):
                wc = w_kv[:, c].rearrange("p (h d) -> p h d", d=HD)
                did.did(v.tensor_reduce(csum[:, c], wc, AX_X, ALU.add))
            did.wait()
            did.did(v.tensor_scalar(csum[:, :, :], csum[:, :, :], 1.0 / HD, None, ALU.mult))
            did.wait()
            for c in range(KC):
                wc = w_kv[:, c].rearrange("p (h d) -> p h d", d=HD)
                last = v.tensor_tensor(wc, wc, csum[:, c].unsqueeze(2).to_broadcast([128, 8, HD]), ALU.subtract)
                last.then_inc(s_wkv, 1)
            dve.wait_ge(s_sd, 1)
            did.did(v.reciprocal(rstd[:, :], sd[:, :]))
            did.wait()
            segment(0, 1, False)
            segment(1, 1, True)
            with did.loop(2, SEGS // 2, RANK + STEPS * (M_STEP + G_STEP)) as s:
                segment(s, 1, True)
            dve.wait_ge(s_kvacc, NT + 1)
            did.did(v.memset(kv_sb[:, :, :], 0.0))
            did.wait()
            did.did(v.tensor_copy(kv_sums[:, :], ps_sums))
            did.did(v.tensor_scalar(k_shift[:, KC:], kv_cols[:, 1:2], float(N), None, ALU.mult))
            did.wait()
            for c in range(KC):
                did.did(v.scalar_tensor_tensor(k_shift[:, c:c + 1], kv_sums[:, c:c + 1], kv_cols[:, 0:1],
                                               k_shift[:, KC:], ALU.mult, ALU.add))
            did.wait()
            v.tensor_copy(kvo[:, 0, :].rearrange("p (c n) -> p c n", c=KC),
                          k_shift[:, 0:KC].unsqueeze(2).to_broadcast([128, KC, 128])).then_inc(s_kshift, 1)
            blocks = [(c, slice(HD * h, HD * h + HD)) for c in range(KC) for h in range(2)]
            for c, r in blocks:
                did.did(v.tensor_tensor(kv_sb[r, c, r], ps_vk[c][r, r], k_rows[r, 0, :], ALU.mult))
            did.wait()
            for c, r in blocks:
                did.did(v.scalar_tensor_tensor(kv_sb[r, c, r], k_rows[r, 1, :], kv_sums[r, KC + c:KC + c + 1],
                                               kv_sb[r, c, r], ALU.mult, ALU.add))
            did.wait()
            for c, r in blocks:
                did.did(v.tensor_scalar(kv_sb[r, c, r], kv_sb[r, c, r], kv_cols[r, 2:3], None, ALU.mult))
            did.wait()
            dve.wait_ge(s_krow, 1)
            for c, r in blocks:
                did.did(v.scalar_tensor_tensor(kv_sb[r, c, r], ps_t[r, c * 128 + r.start:c * 128 + r.stop],
                                               kv_cols[r, 3:4], kv_sb[r, c, r], ALU.mult, ALU.add))
            did.wait()
            for c, r in blocks:
                v.tensor_scalar(kv_sb[r, c, r], kv_sb[r, c, r], 1.0 / N, None, ALU.mult).then_inc(s_kvsb, 1)
            with did.loop(SEGS // 2, SEGS - 1, RANK + STEPS * G_STEP) as s:
                segment(s, 2, True)
            with did.loop(0, STEPS, G_STEP) as i:
                step(SEGS - 1, i, 2, True)
            with did.loop(0, BEHIND, G_STEP) as i:
                step(SEGS, i, 0, True)
            offs = slots_of(SEGS * STEPS)
            for k in range(LAG):
                for u in range(2):
                    add_unit(SEGS * STEPS * GROUPS + k - LAG, GROUPS + k - LAG, u, offs[2 * k + u])
                    did.wait()
            dve.wait_ge(s_added, RING - 1 + SEGS * STEPS * GROUPS)

            def network(b):
                sums = agg[:, bass.ds(b, 1), :].rearrange("p b (h f) -> p (b h) f", h=2)
                did.did(v.tensor_scalar(cnt[:, :], sums[:, :, EA], 1.0, None, ALU.max))
                did.wait()
                did.did(v.reciprocal(rcnt[:, :], cnt[:, :]))
                did.wait()
                after(dve, s_aggt, b)
                v.tensor_tensor(aggn[:, :, :], sums[:, :, 0:EA], rcnt[:, :].unsqueeze(2).to_broadcast([P, 2, EA]),
                                ALU.mult).then_inc(s_aggn, 1)

            def bucket(b, a, i):
                dve.wait_ge(s_x1in[a], (i + 1) * 16)
                dve.wait_ge(s_o, b + 1)
                v.tensor_tensor(x1t[:, a], x1t[:, a], ps_g[0][0:P, :].rearrange("p (t d) -> p t d", t=2),
                                ALU.add).then_inc(s_x1done, 1)
                dve.wait_ge(s_x1done, b + 1)
                for q in range(2):
                    did.did(v.bn_stats(st[:, q, :], x1t[:, a, q, :]))
                wait_apart(dve, did.sem, did.base + did.k)
                did.did(v.bn_aggr(mv2[:, 0, :], st[:, 0, :]))
                v.bn_aggr(mv2[:, 1, :], st[:, 1, :]).then_inc(s_mv2, 1)
                if not known_from(b, NB - 3):
                    network(b + 3)
                dve.wait_ge(s_mv2, b + 1)
                dve.wait_ge(s_sd2, b + 1)
                did.did(v.reciprocal(rs2[:, :], sd2[:, :]))
                did.wait()
                after(dve, s_yt, b - 1)
                after(dve, s_keep, b - 1)
                for q in range(2):
                    end = v.tensor_scalar(y2[:, a, q, :], x1t[:, a, q, :], mv2[:, q, 0:1], rs2[:, q:q + 1],
                                          ALU.subtract, ALU.mult)
                end.then_inc(s_yn, 1)

            for b in range(3):
                network(b)
            in_turn(dve, bucket, lambda start, end: did.loop(start, end, 2 * (4 + 2)))
            did.wait()

            dve.wait_ge(s_lgc, NB)
            dve.wait_ge(s_x1out, NB * 16)
            dve.wait_ge(s_keep, NB)
            did.wait()
            experts = expert_iota[:, :].unsqueeze(1).to_broadcast([P, NT, NE])
            for k in range(K):
                vals = (logits, left)[k]
                did.did(v.tensor_reduce(top[:, k, 0, :], vals[:, :, :], AX_X, ALU.max))
                did.wait()
                did.did(v.tensor_tensor(tmp[:, :, :], vals[:, :, :],
                                        top[:, k, 0, :].unsqueeze(2).to_broadcast([P, NT, NE]), ALU.is_equal))
                did.wait()
                did.did(v.scalar_tensor_tensor(tmp[:, :, :], tmp[:, :, :], -float(NE), experts, ALU.mult, ALU.add))
                did.wait()
                did.did(v.tensor_reduce(top[:, k, 1, :], tmp[:, :, :], AX_X, ALU.min))
                did.wait()
                did.did(v.tensor_scalar(top[:, k, 1, :], top[:, k, 1, :], float(NE), None, ALU.add))
                did.wait()
                did.did(v.tensor_tensor(best[:, :, k * NT:(k + 1) * NT].rearrange("p e t -> p t e"),
                                        top[:, k, 1, :].unsqueeze(2).to_broadcast([P, NT, NE]), experts, ALU.is_equal))
                did.wait()
                if k == 0:
                    did.did(v.scalar_tensor_tensor(left[:, :, :],
                                                   best[:, :, 0:NT].rearrange("p e t -> p t e"), -BIG,
                                                   logits[:, :, :], ALU.mult, ALU.add))
                    did.wait()
            v.tensor_tensor(top[:, 1, 0, :], top[:, 1, 0, :], top[:, 0, 0, :], ALU.subtract).then_inc(s_diff, 1)
            v.tensor_reduce(hist[:, 0:NE], best[:, :, :], AX_X, ALU.add).then_inc(s_chist, 1)
            flat = best[:, :, :].rearrange("p e t -> p (e t)")
            did.did(v.tensor_tensor_scan(at[:, :, :].rearrange("p e t -> p (e t)"), flat, flat, 0.0, ALU.add, ALU.max))
            dve.wait_ge(s_exp, 1)
            did.did(v.tensor_scalar(top[:, 0, 2, :], top[:, 1, 1, :], 1.0, None, ALU.add))
            did.wait()
            did.did(v.reciprocal(weight[:, 0, :], top[:, 0, 2, :]))
            did.wait()
            did.did(v.tensor_tensor(weight[:, 1, :], weight[:, 0, :], top[:, 1, 1, :], ALU.mult))
            did.did(v.memset(experts3[:, :, :], 0))
            dve.wait_ge(s_chist, 1)
            dve.wait_ge(s_cprefix, 1)
            lanes_before, total = ps_rank[0:P, 0:NE], ps_rank[0:P, NE:2 * NE]
            did.did(v.tensor_scalar(rk_i[:, 0:NE], total, float(TR - 1), None, ALU.add))
            did.wait()
            did.did(v.tensor_scalar(rk_i[:, 0:NE], rk_i[:, 0:NE], 7, 7, ALU.logical_shift_right, ALU.logical_shift_left))
            did.wait()
            did.did(v.tensor_copy(rk[:, 0, 0:NE], rk_i[:, 0:NE]))
            did.did(v.tensor_tensor_scan(rk[:, 1, 0:NE], hist[:, 0:NE], hist[:, 0:NE], 0.0, ALU.add, ALU.max))
            did.wait()
            did.did(v.tensor_tensor_scan(rk[:, 2, 0:NE], rk[:, 0, 0:NE], rk[:, 0, 0:NE], 0.0, ALU.add, ALU.max))
            did.did(v.tensor_tensor(rk[:, 3, 0:NE], hist[:, 0:NE], rk[:, 1, 0:NE], ALU.subtract))
            did.did(v.scalar_tensor_tensor(rk[:, 4, 0:NE], lanes_before, -1.0, rk[:, 0, 0:NE], ALU.add, ALU.subtract))
            did.wait()
            did.did(v.tensor_tensor(rk[:, 5, 0:NE], rk[:, 2, 0:NE], rk[:, 3, 0:NE], ALU.add))
            did.did(v.tensor_tensor(ended[:, :, :], rk[0:1, 2:3, 0:NE].to_broadcast([1, ET, NE]),
                                    tile_start[:, :].unsqueeze(2).to_broadcast([1, ET, NE]), ALU.is_le))
            did.wait()
            did.did(v.tensor_tensor(rk[:, 6, 0:NE], rk[:, 5, 0:NE], rk[:, 4, 0:NE], ALU.add))
            did.did(v.tensor_reduce(expert_f[:, :], ended[:, :, :], AX_X, ALU.add))
            did.wait()
            pairs_f = expert_f[:, :].rearrange("p (i a) -> p i a", a=2)
            did.did(v.tensor_scalar(experts3[:, :, 0:2], pairs_f, float(NE - 1), None, ALU.min))
            did.did(v.tensor_scalar(experts3[:, 0:ET // 2 - 1, 2:3], pairs_f[:, 1:, 0:1], float(NE - 1), None, ALU.min))
            did.did(v.tensor_tensor(at[:, :, :], at[:, :, :],
                                    rk[:, 6, 0:NE].unsqueeze(2).to_broadcast([P, NE, K * NT]), ALU.add))
            did.wait()
            did.did(v.tensor_tensor(at[:, :, :], at[:, :, :], best[:, :, :], ALU.mult))
            did.wait()
            with nc.allow_low_precision(reason="whole numbers below 2^24"):
                v.tensor_reduce(place[:, :, :].rearrange("p k t -> p (k t)"), at[:, :, :].rearrange("p e t -> p t e"),
                                AX_X, ALU.add).then_inc(s_place, 1)

            def add_b1(r, a, e):
                dve.wait_ge(s_eh, r + 1)
                after(dve, s_gelu, r - 1)
                v.tensor_tensor(hb[:, a, :], ps_acc[a][:, :], b1_rows[:, bass.ds(e * HID, HID)], ALU.add).then_inc(s_ehb, 1)

            def keep_gT(r, a):
                dve.wait_ge(s_gt, r + 1)
                after(dve, s_ey, r - 1)
                v.tensor_copy(hgT[:, a].rearrange("p c n -> p (c n)"), ps_g[a][:, :]).then_inc(s_gtc, 1)

            def add_b2(r, a, i, e):
                dve.wait_ge(s_ey, r + 1)
                after(dve, s_eout[a], i * 16)
                v.tensor_tensor(y_out[:, a, :], ps_y[a][:, 0:D], b2_rows[:, bass.ds(e * D, D)], ALU.add).then_inc(s_eyb, 1)

            def expert_tile(r, a, i, e):
                add_b1(r + 1, 1 - a, e[1])
                add_b2(r, a, i, e[0])
                keep_gT(r + 1, 1 - a)

            dve.wait_ge(s_b1, 16)
            dve.wait_ge(s_we, (KC + HC + 1) * 16)
            load = experts_of(mybir.EngineType.DVE)
            add_b1(0, 0, load(0)[0])
            keep_gT(0, 0)
            pairwise(dve, expert_tile, ET - 2, load)
            e = load(ET // 2 - 1)
            add_b1(ET - 1, 1, e[1])
            add_b2(ET - 2, 0, ET // 2 - 1, e[0])
            keep_gT(ET - 1, 1)
            add_b2(ET - 1, 1, ET // 2 - 1, e[1])

            with did.loop(0, NT // MOVE, MOVE) as i:
                for m in range(MOVE):
                    t = i * MOVE + m
                    dve.wait_ge(s_res[m], (i + 1) * 16)
                    dve.wait_ge(s_fetch[m], (i + 1) * (K * 16))
                    did.did(v.scalar_tensor_tensor(res[:, m, :], fetched[:, m, 0, :], weight[:, 0, bass.ds(t, 1)],
                                                   res[:, m, :], ALU.mult, ALU.add))
                    did.wait()
                    v.scalar_tensor_tensor(res[:, m, :], fetched[:, m, 1, :], weight[:, 1, bass.ds(t, 1)],
                                           res[:, m, :], ALU.mult, ALU.add).then_inc(s_comb, 1)

        @block.tensor
        def _(pe):
            t = nc.tensor
            pe.wait_ge(s_const, NCONST)

            def rank(s):
                pe.wait_ge(s_hist, s + 1)
                pe.wait_ge(s_rank, s)
                t.matmul(ps_rank[0:P, 0:NB], below[:, :], hist[:, :], start=True, stop=True)
                t.matmul(ps_rank[0:P, NB:2 * NB], ones[:, :], hist[:, :], start=True, stop=True).then_inc(s_prefix, 1)

            def pair(g, k):
                pe.wait_ge(s_onehot, g + 1)
                pe.wait_ge(s_added, g + 1)
                for u in range(2):
                    for half in range(2):
                        o = u * AGG + half * (EA + 1)
                        for j in range(2):
                            for n, rows_of in enumerate((unit_hi[:, k], rest_hi[:, k % RING], rest_lo[:, k % RING])):
                                last = t.matmul(ps_g[k % RING][:, o:o + EA + 1],
                                                onehot[:, k % RING, 2 * u + j, half * P:half * P + 128],
                                                rows_of[:, 2 * u + j, 0:EA + 1],
                                                start=(j == 0 and n == 0), stop=(j == 1 and n == 2))
                last.then_inc(s_group, 1)

            def project(j, a, first=False):
                pe.wait_ge(s_xn, j + 1)
                pe.wait_ge(s_xtc, 2 * j)
                for c in range(KC):
                    last = t.transpose(ps_t[:, c * P:(c + 1) * P], xn[:, a, c * 128:(c + 1) * 128], ident[0:P, 0:P])
                last.then_inc(s_xt, 1)
                pe.wait_ge(s_xtc, 2 * j + 2)
                pe.wait_ge(s_kvn, j)
                for c in range(KC):
                    last = t.matmul(ps_kv[0:P, :], xnT_t[:, a, c, :], w_kv[:, c, :], start=(c == 0), stop=(c == KC - 1))
                last.then_inc(s_kvp, 1)

            def accumulate(j, a, start):
                pe.wait_ge(s_kvn, j + 1)
                for c in range(KC):
                    last = t.matmul(ps_vk[c], kvn[:, a, D + 128 * c:D + 128 * c + 128],
                                    kvn[:, a, 128 * c:128 * c + 128], start=start and c == 0, stop=False,
                                    skip_group_check=True)
                    for n in range(2):
                        last = t.matmul(ps_sums[:, n * KC + c:n * KC + c + 1],
                                        kvn[:, a, n * D + 128 * c:n * D + 128 * c + 128], ones[:, 0:1],
                                        start=False, stop=False, skip_group_check=True)
                last.then_inc(s_kvacc, 1)

            def mix2(j, a):
                pe.wait_ge(s_x2, j + 1)
                pe.wait_ge(s_mixed, j + 1)
                o = ps_kv[0:P, a * D:(a + 1) * D]
                for c in range(KC):
                    t.matmul(o, xnT_t[:, a, c, :], mix_w[:, c, :], start=(c == 0), stop=False)
                for r in range(2):
                    last = t.matmul(o, ones[0:1, :], bias_rows[0:1, r, :], start=False, stop=(r == 1))
                last.then_inc(s_mix, 1)

            def step(s, i, mix, groups, first=False):
                if mix == 1:
                    j = s * (2 * STEPS) + i * 2
                    todo = {0: lambda: project(j, 0), 5: lambda: project(j + 1, 1),
                            6: lambda: accumulate(j, 0, first), 10: lambda: accumulate(j + 1, 1, False)}
                elif mix == 2:
                    j = (s - SEGS // 2) * (2 * STEPS) + i * 2
                    todo = {1: lambda: mix2(j, 0), 6: lambda: mix2(j + 1, 1)}
                else:
                    todo = {}
                n = s * STEPS + i - BEHIND
                for k in range(GROUPS):
                    if groups:
                        pair(n * GROUPS + k, k)
                    if k in todo:
                        todo[k]()

            rank(0)
            pe.wait_ge(s_w, 22 * 16)
            for n in range(3):
                pe.wait_ge(s_wTc, n)
                for ci in range(KC):
                    for co in range(KC):
                        last = t.transpose(ps_t[:, ci * D + co * 128:ci * D + co * 128 + 128],
                                           raw[:, n, co, ci * 128:(ci + 1) * 128], ident[:, :])
                last.then_inc(s_wT, 1)
            for c in range(HC):
                o = ps_kv[:, c:c + 1]
                t.matmul(o, w1u[:, c * 128:(c + 1) * 128], u_col[:, :], start=True, stop=False)
                last = t.matmul(o, b1_row[0:1, c * 128:(c + 1) * 128], ones[0:1, 0:1], start=False, stop=True)
            last.then_inc(s_hb, 1)
            pe.wait_ge(s_wkv, 2)
            pe.wait_ge(s_wTc, 3)
            pe.wait_ge(s_hbc, 1)
            step(0, 0, 1, False, first=True)
            with pe.Fori(1, PREFIX_STEP) as i:
                step(0, i, 1, False)
            rank(1)
            with pe.Fori(PREFIX_STEP, STEPS) as i:
                step(0, i, 1, False)
            step(1, 0, 1, False)
            with pe.Fori(1, PREFIX_STEP) as i:
                step(1, i, 1, True)
            rank(2)
            with pe.Fori(PREFIX_STEP, STEPS) as i:
                step(1, i, 1, True)
            with pe.Fori(2, SEGS // 2) as s:
                with pe.Fori(0, PREFIX_STEP) as i:
                    step(s, i, 1, True)
                rank(s + 1)
                with pe.Fori(PREFIX_STEP, STEPS) as i:
                    step(s, i, 1, True)
            pe.wait_ge(s_kshift, 1)
            for c in range(KC):
                last = t.matmul(ps_t[:, c * 128:(c + 1) * 128], kvo[:, 0, c * 128:(c + 1) * 128], ident[:, :],
                                start=True, stop=True)
            last.then_inc(s_krow, 1)
            pe.wait_ge(s_kvsb, 4)
            for c in range(KC):
                t.matmul(ps_t[:, c * D:(c + 1) * D], kv_sb[:, c, :], w_oT[:, c, :], start=True, stop=True)\
                    .then_inc(s_kvo, 1)
            pe.wait_ge(s_kvoc, KC)
            pe.wait_ge(s_kvn, NT)
            for ci in range(KC):
                for c in range(KC):
                    last = t.matmul(ps_kv[:, ci * D:(ci + 1) * D], w_q[:, c, ci * 128:(ci + 1) * 128], kvo[:, c, :],
                                    start=(c == 0), stop=(c == KC - 1))
                last.then_inc(s_mixw, 1)
            pe.wait_ge(s_mixwc, KC)
            with pe.Fori(SEGS // 2, SEGS - 1) as s:
                with pe.Fori(0, PREFIX_STEP) as i:
                    step(s, i, 2, True)
                rank(s + 1)
                with pe.Fori(PREFIX_STEP, STEPS) as i:
                    step(s, i, 2, True)
            with pe.Fori(0, STEPS) as i:
                step(SEGS - 1, i, 2, True)
            with pe.Fori(0, BEHIND) as i:
                step(SEGS, i, 0, True)

            pe.wait_ge(s_gw, 4 * 16)
            for n in range(2):
                for c in range(KC):
                    last = t.matmul(ps_t[:, n * KC + c:n * KC + c + 1], gb_rows[0:1, n, c * 128:(c + 1) * 128],
                                    ones[0:1, 0:1], start=True, stop=True)
            last.then_inc(s_gb, 1)
            pe.wait_ge(s_gbc, 1)
            pe.wait_ge(s_mixed, NT + 1)
            pe.wait_ge(s_added, RING - 1 + SEGS * STEPS * GROUPS)

            def means_T(b):
                after(pe, s_aggtc, b)
                wait_apart(pe, s_aggn, b + 1)
                for a in range(2):
                    end = t.transpose(ps_rank[0:EA, a * P:(a + 1) * P], aggn[:, a, :], ident[0:P, 0:P])
                end.then_inc(s_aggt, 1)

            def hidden_T(b):
                pe.wait_ge(s_aggtc, b + 1)
                for hc in range(HC):
                    if hc % 2 == 0:
                        after(pe, s_relu, (b - 1) * HC + hc + 2)
                    o = ps_acc[hc // 2][:, (hc % 2) * BN:(hc % 2 + 1) * BN]
                    for c in range(KC):
                        t.matmul(o, w1x[:, c, hc * 128:(hc + 1) * 128], xnT[:, bass.ds(b * 2, 2), c, :],
                                 start=(c == 0), stop=False)
                    end = t.matmul(o, w1e[:, hc * 128:(hc + 1) * 128], aggT[:, :, :].rearrange("p t n -> p (t n)"),
                                   start=False, stop=True)
                    if hc % 2:
                        end.then_inc(s_h, 1)

            def network_out(b, a):
                pe.wait_ge(s_relu, (b + 1) * HC)
                after(pe, s_x1done, b)
                for q in range(2):
                    for hc in range(HC):
                        end = t.matmul(ps_g[0][0:P, q * D:(q + 1) * D], hT[:, a, hc, q, :], w2[:, hc, :],
                                       start=(hc == 0), stop=(hc == HC - 1))
                end.then_inc(s_o, 1)

            def y_T(b, a):
                after(pe, s_ytc, b * KC)
                wait_apart(pe, s_yn, b + 1)
                for q in range(2):
                    for c in range(KC):
                        end = t.transpose(ps_t[:, c * BN + q * P:c * BN + (q + 1) * P],
                                          y2[:, a, q, c * 128:(c + 1) * 128], ident[0:P, 0:P])
                end.then_inc(s_yt, 1)

            def router(b):
                after(pe, s_lgc, b)
                pe.wait_ge(s_ytc, (b + 1) * KC)
                for q in range(2):
                    o = ps_kv[0:P, q * NE:(q + 1) * NE]
                    for c in range(KC):
                        t.matmul(o, ynT[:, c, q, :], w_r[:, c, :], start=(c == 0), stop=False)
                    end = t.matmul(o, ones[0:1, :], br_row[:, :], start=False, stop=True)
                end.then_inc(s_lg, 1)

            def bucket(b, a, i):
                if not known_from(b, NB - 1):
                    hidden_T(b + 1)
                if not known_below(b, 2):
                    router(b - 2)
                network_out(b, a)
                if not known_from(b, NB - 2):
                    means_T(b + 2)
                if not known_below(b, 1):
                    y_T(b - 1, 1 - a)

            means_T(0)
            hidden_T(0)
            means_T(1)
            in_turn(pe, bucket)
            router(NB - 2)
            y_T(NB - 1, (NB - 1) % 2)
            router(NB - 1)

            pe.wait_ge(s_chist, 1)
            t.matmul(ps_rank[0:P, 0:NE], below[:, :], hist[:, 0:NE], start=True, stop=True)
            t.matmul(ps_rank[0:P, NE:2 * NE], ones[:, :], hist[:, 0:NE], start=True, stop=True).then_inc(s_cprefix, 1)

            def rows_T(r, a, i):
                pe.wait_ge(s_rowin[a], (i + 1) * 16)
                after(pe, s_ztc, r * KC)
                for c in range(KC):
                    last = t.transpose(ps_t[:, c * TR:(c + 1) * TR], row_in[:, a, c * 128:(c + 1) * 128], ident[:, :])
                last.then_inc(s_zt, 1)

            def hidden(r, a, e):
                pe.wait_ge(s_ztc, (r + 1) * KC)
                after(pe, s_ehb, r - 1)
                for c in range(KC):
                    last = t.matmul(ps_acc[a][:, :], zT[:, a, c, :], W1_all[:, bass.ds(e * (KC * HID) + c * HID, HID)],
                                    start=(c == 0), stop=(c == KC - 1))
                last.then_inc(s_eh, 1)

            def gelu_T(r, a):
                pe.wait_ge(s_gelu, r + 1)
                after(pe, s_gtc, r - 1)
                for c in range(HC):
                    last = t.transpose(ps_g[a][:, c * TR:(c + 1) * TR], hg[:, a, c * 128:(c + 1) * 128], ident[:, :])
                last.then_inc(s_gt, 1)

            def outputs(r, a, e):
                pe.wait_ge(s_gtc, r + 1)
                after(pe, s_eyb, r - 1)
                for c in range(HC):
                    last = t.matmul(ps_y[a][:, 0:D], hgT[:, a, c, :], W2_all[:, bass.ds(e * (HC * D) + c * D, D)],
                                    start=(c == 0), stop=(c == HC - 1))
                last.then_inc(s_ey, 1)

            def expert_tile(r, a, i, e):
                hidden(r + 1, 1 - a, e[1])
                outputs(r, a, e[0])
                rows_T(r + 2, a, i + 1)
                gelu_T(r + 1, 1 - a)

            pe.wait_ge(s_place, 1)
            pe.wait_ge(s_we, (KC + HC + 1) * 16)
            rows_T(0, 0, 0)
            rows_T(1, 1, 0)
            load = experts_of(mybir.EngineType.PE)
            hidden(0, 0, load(0)[0])
            gelu_T(0, 0)
            pairwise(pe, expert_tile, ET - 2, load)
            e = load(ET // 2 - 1)
            hidden(ET - 1, 1, e[1])
            outputs(ET - 2, 0, e[0])
            gelu_T(ET - 1, 1)
            outputs(ET - 1, 1, e[1])


_INS = ["x", "src", "edge_attr_64", "L0_gnn_u", "L0_gnn_W1", "L0_gnn_b1", "L0_gnn_W2", "L0_gnn_b2",
        "L0_mix_wq", "L0_mix_wk", "L0_mix_wv", "L0_mix_wo", "L0_mix_bo",
        "L0_mix_ln_k_g", "L0_mix_ln_k_b", "L0_mix_ln_v_g", "L0_mix_ln_v_b",
        "L0_ffn_gamma", "L0_ffn_beta", "L0_ffn_Wr", "L0_ffn_br", "L0_ffn_W1", "L0_ffn_b1", "L0_ffn_W2", "L0_ffn_b2"]


def kernel(**inputs):
    import numpy as _np
    import concourse.bacc as _bacc
    from concourse import mybir as _mybir
    from concourse.bass_utils import run_bass_kernel_spmd as _run

    nc = _bacc.Bacc("TRN2", target_bir_lowering=False, num_devices=1)
    arrays, args = {}, []
    for name in _INS:
        a = _np.ascontiguousarray(inputs[name])
        arrays[f"in_{name}_dram"] = a
        args.append(nc.dram_tensor(f"in_{name}_dram", a.shape, _mybir.dt.from_np(a.dtype), kind="ExternalInput").ap())
    args.append(nc.dram_tensor("out_0_dram", (N, D), F32, kind="ExternalOutput").ap())
    args.append(nc.dram_tensor("buckets", (SEGS * SEG_ROWS, ROW), F32, kind="Internal").ap())
    args.append(nc.dram_tensor("x1", (N, D), F32, kind="Internal").ap())
    args.append(nc.dram_tensor("sorted_y", (ET * TR, D), F32, kind="Internal").ap())
    args.append(nc.dram_tensor("expert_out", (ET * TR, D), F32, kind="Internal").ap())
    build(nc, *args)
    r = _run(nc, [arrays], core_ids=[0])
    return r.results[0]["out_0_dram"]
```

```python
from contextlib import ExitStack, contextmanager

import concourse.bass as bass
from concourse import mybir

ALU = mybir.AluOpType
ACT = mybir.ActivationFunctionType
AX_X = mybir.AxisListType.X
F32 = mybir.dt.float32
BF16 = mybir.dt.bfloat16
I32 = mybir.dt.int32

N = 6250
D = 256
EA = 64
HID = 512
HEADS, HD = 4, 64
NE = 8
EPS = 1e-5

P = 125
NT = N // P
KC = D // 128
HC = HID // 128

E = 206250
EC = E // P
SEGS = 10
SC = EC // SEGS
STEPS = 5
SLOTS = 3
CH = SC // (STEPS * SLOTS)
NB = 25
BN = N // NB
UR = 256
GROUPS = 11
NU = 2 * GROUPS * STEPS
assert (SC * P + NB * (UR - 1)) // UR <= NU
SEG_ROWS = NU * UR
ROW = EA + 2
AGG = 2 * (EA + 1)
RING = 4
LAG = RING - 2
assert GROUPS % RING == RING - 1
BEHIND = STEPS + 1
CREDIT = GROUPS
STEP_OFF = -(-2 * GROUPS // 4) * 4
PREFIX_STEP = 2
PREFIX = 1
OH = 256
QW = 6


K = 2
TR = 128
HALVES = 2
NTH = NT // HALVES
TP = (N // HALVES * K + NE * (TR - 1)) // TR // 2
TP += (N // HALVES * K + NE * (TR - 1)) // TR % 2
ETH = 2 * TP
ET = HALVES * ETH
MOVE = 5
MOVES = NTH // MOVE
assert MOVES * MOVE == NTH and 1 + MOVES * MOVE < TP
BIG = 3.0e38


class Steps:

    def __init__(self, eng, sem):
        self.eng, self.sem, self.base, self.k = eng, sem, 0, 0

    def did(self, ins):
        ins.then_inc(self.sem, 1)
        self.k += 1

    def wait(self):
        self.eng.wait_ge(self.sem, self.base + self.k)

    @contextmanager
    def loop(self, start, end, per):
        with self.eng.Fori(start, end) as i:
            base, k = self.base, self.k
            self.base, self.k = base + k + (i - start) * per, 0
            yield i
            assert self.k == per, (self.k, per)
            self.base, self.k = base, k + (end - start) * per


def build(nc, x, src, edge_attr, gnn_u, gnn_W1, gnn_b1, gnn_W2, gnn_b2,
          wq, wk, wv, wo, bo, k_g, k_b, v_g, v_b, gamma, beta, Wr, br, W1, b1, W2, b2,
          out, buckets, x1, sorted_y, expert_out):
    with ExitStack() as ctx:
        def sb(name, shape, dt=F32):
            return ctx.enter_context(nc.sbuf_tensor(name, shape, dt))

        def psum(name, shape, dt=F32):
            return ctx.enter_context(nc.psum_tensor(name, shape, dt))

        def sem(name):
            return ctx.enter_context(nc.semaphore(name))

        x_or_xnT = sb("x_or_xnT", [128, NT * D])
        xs = x_or_xnT[0:P, :].rearrange("p (j d) -> p j d", d=D)
        xnT = x_or_xnT[:, :].rearrange("p (j c n) -> p j c n", c=KC, n=128)[:, :, :, 0:P]
        agg = sb("agg", [P, NB + 1, AGG])
        arena = sb("arena", [128, 19500])
        arena2 = sb("arena2", [128, 8000])

        def carver(store, at=0):
            at = [at]
            return lambda shape, dt=F32: carve(store, at, shape, dt)

        def carve(store, at, shape, dt):
            size = 1
            for n in shape[1:]:
                size *= n
            words = size if dt != BF16 else (size + 1) // 2
            view = store[0:shape[0], at[0]:at[0] + words]
            at[0] += words
            assert at[0] <= store.shape[1], at[0]
            if dt != F32:
                view = view.bitcast(dt)[:, 0:size]
            names = " ".join("abcd"[:len(shape) - 1])
            return view.rearrange(f"p ({names}) -> p {names}",
                                  **{n: m for n, m in zip("abcd", shape[1:])}) if len(shape) > 2 else view

        part = carver(arena)
        part2 = carver(arena2)

        w_kv = part2([128, KC, 2 * D])
        w_q = part2([128, KC, D])
        w_oT = part2([128, KC, D])
        w1x = sb("w1x", [128, KC, HID])
        w1e = sb("w1e", [EA, HID])
        w1u = sb("w1u", [128, HID])
        w2 = sb("w2", [128, HC, D])
        u_col = sb("u_col", [128, 1])
        b1_row = sb("b1_row", [1, HID])
        h_bias = sb("h_bias", [128, HC])
        bias_rows = sb("bias_rows", [1, 2, D])
        k_rows = sb("k_rows", [128, 2, HD])
        kv_cols = sb("kv_cols", [128, 4])
        kv_sums = sb("kv_sums", [128, 2 * KC])
        k_shift = sb("k_shift", [128, KC + 1])
        mix_w = part2([128, KC, D])
        kv_sb = part2([128, KC, 128])
        kvo = part2([128, KC, D])
        ident = sb("ident", [128, 128])
        ones = sb("ones", [P, P])
        below = sb("below", [P, P])
        node_iota = sb("node_iota", [128, OH], BF16)
        bucket_iota = sb("bucket_iota", [P, NB], BF16)
        unit_start = sb("unit_start", [1, NU])
        seg_start = sb("seg_start", [P, SEGS])
        spare = sb("spare", [1, 32])
        eps_col = sb("eps_col", [P, 1])
        eps2_col = sb("eps2_col", [P, 1])
        zeros = sb("zeros", [128, SEG_ROWS * ROW // 128 // (STEPS * QW)])
        pos = part([P, EC], I32)
        local = part([P, EC], BF16)
        mask = part([P, NB, SC], BF16)
        count = part([P, NB, SC])
        filled = mask[:, :, :].rearrange("p b t -> p (b t)")[0:1, 0:NU * NB].rearrange("p (u b) -> p u b", b=NB)
        kq = sb("kq", [P, SC], I32)
        kf = sb("kf", [P, 4, SC])
        hist = sb("hist", [P, NB])
        rk = sb("rk", [P, 8, NB])
        rk_i = sb("rk_i", [P, NB], I32)
        ustart_f = sb("ustart_f", [1, NU])
        agg_off = sb("agg_off", [1, (SEGS * STEPS + 1) * STEP_OFF], I32)
        stage = part([P, SLOTS, CH, EA])
        rows = part([P, SLOTS, CH, ROW])
        rows_at = sb("rows_at", [P, SLOTS, CH], I32)
        unit = part([128, GROUPS, 4, ROW])
        unit_hi = unit.rearrange("p k j f -> p (k j f)").bitcast(BF16)\
            .rearrange("p (k j f h) -> p k j f h", k=GROUPS, j=4, h=2)[:, :, :, :, 1]
        rest = part([128, RING, 4, ROW])
        rest_hi = rest.rearrange("p k j f -> p (k j f)").bitcast(BF16)\
            .rearrange("p (k j f h) -> p k j f h", k=RING, j=4, h=2)[:, :, :, :, 1]
        rest_lo = part([128, RING, 4, ROW], BF16)
        onehot_words = part([128, RING * 4 * OH // 2])
        onehot = onehot_words.bitcast(BF16).rearrange("p (k j n) -> p k j n", k=RING, j=4)
        raw = onehot_words[:, 0:3 * KC * D].rearrange("p (n c d) -> p n c d", n=3, c=KC)
        xt = part2([P, 2, D])
        xn = part2([P, 2, D])
        xnT_t = part2([128, 2, KC, P])
        stats = sb("stats", [P, NT, 6])
        mv = sb("mv", [P, NT, 2])
        sd = sb("sd", [P, NT])
        rstd = sb("rstd", [P, NT])
        sq = part2([P, 2 * D])
        ss = sb("ss", [P, 8])
        hsd = sb("hsd", [P, 8])
        hrs = sb("hrs", [P, 8])
        kvn = part2([P, 2, 2 * D])
        csum = sb("csum", [128, KC, 8])

        part2 = carver(arena2)
        logits = part2([P, NT, NE])
        W1_all = arena[:, 0:NE * KC * HID]
        W2_all = arena[:, NE * KC * HID:NE * (KC * HID + HC * D)]
        x1t = part2([P, 2, 2, D])
        cnt = sb("cnt", [P, 2])
        rcnt = sb("rcnt", [P, 2])
        aggn = part2([P, 2, EA])
        aggT = part2([EA, 2, P])
        hT = part2([128, 2, HC, 2, P])
        st = sb("st", [P, 2, 6])
        mv2 = sb("mv2", [P, 2, 2])
        sd2 = sb("sd2", [P, 2])
        rs2 = sb("rs2", [P, 2])
        y2 = part2([P, 2, 2, D])
        ynT = part2([128, KC, 2, P])
        G_WORDS = NT * NE + 4 * D + 2 * EA + 2 * P + 2 * HC * 2 * P + 4 * D + KC * 2 * P
        w_r = sb("w_r", [128, KC, NE])
        br_row = sb("br_row", [1, NE])
        gb_rows = sb("gb_rows", [1, 2, D])
        gb_col = sb("gb_col", [128, 2, KC])

        part2h = [carver(arena2, G_WORDS), carver(arena2, NT * NE)]
        best = [part2h[h]([P, NE, K * NTH]) for h in range(HALVES)]
        at = [part2h[h]([P, NE, K * NTH]) for h in range(HALVES)]
        left = [part2h[h]([P, NTH, NE]) for h in range(HALVES)]
        tmp = [part2h[h]([P, NTH, NE]) for h in range(HALVES)]
        top = [part2h[h]([P, 2, 3, NTH]) for h in range(HALVES)]
        b1_rows = arena2[:, arena2.shape[1] - NE * HID:]
        assert NT * NE + 2 * NE * K * NTH + 2 * NTH * NE + 6 * NTH <= arena2.shape[1] - NE * HID
        b2_rows = arena[:, NE * (KC * HID + HC * D):NE * (KC * HID + HC * D) + NE * D]
        expert_iota = sb("expert_iota", [P, NE])
        tile_start = sb("tile_start", [1, ETH])
        place = kq[:, 0:NT * K].rearrange("p (t k) -> p t k", k=K)
        part4 = carver(kf[:, :, :].rearrange("p a t -> p (a t)"))
        weight = part4([P, HALVES, K, NTH])
        ended = part4([1, ETH, NE])
        expert_f = part4([1, ETH])
        experts3 = carver(stats[:, :, :].rearrange("p a t -> p (a t)"))([1, ET // 2, 4], I32)
        send = agg[:, :, :].rearrange("p b f -> p (b f)")[:, 0:MOVE * D].rearrange("p (m d) -> p m d", d=D)
        send_at = sb("send_at", [P, MOVE, K], I32)
        part3 = carver(x_or_xnT)
        row_in = part3([128, 2, D])
        zT = part3([128, 2, KC, TR])
        hb = part3([128, 2, HID])
        hg = part3([128, 2, HID])
        hgT = part3([128, 2, HC, TR])
        y_out = part3([128, 2, D])
        fetched = part3([P, MOVE, K, D])
        res = part3([P, MOVE, D])

        ps_rank = psum("ps_rank", [128, 512])
        ps_t = psum("ps_t", [128, 512])
        ps_kv = psum("ps_kv", [128, 512])
        ps_acc = [psum(f"ps_acc{c}", [128, 512]) for c in range(KC)]
        ps_vk = [ps_acc[0][:, 128 * c:128 * (c + 1)] for c in range(KC)]
        ps_sums = ps_acc[0][:, KC * 128:KC * 128 + 2 * KC]
        ps_y = (ps_kv, ps_rank)
        ps_g = [psum(f"ps_g{k}", [128, 512]) for k in range(RING - 1)] + [ps_acc[1]]

        s_src_loaded = sem("s_src_loaded")
        s_x_loaded = sem("s_x_loaded")
        s_weights_loaded = sem("s_weights_loaded")
        s_rows_cleared = sem("s_rows_cleared")
        s_chunk_loaded = [sem(f"s_chunk_loaded{k}") for k in range(SLOTS)]
        s_chunk_scattered = [sem(f"s_chunk_scattered{k}") for k in range(SLOTS)]
        s_features_copied = sem("s_features_copied")
        s_places_copied = sem("s_places_copied")
        s_constants = sem("s_constants")
        s_constant_parts = sem("s_constant_parts")
        s_unit_loaded = [sem(f"s_unit_loaded{k}") for k in range(GROUPS)]
        s_bucket_counts = sem("s_bucket_counts")
        s_lane_sums = sem("s_lane_sums")
        s_ranked = sem("s_ranked")
        s_onehots_made = sem("s_onehots_made")
        s_pair_multiplied = sem("s_pair_multiplied")
        s_rest_made = sem("s_rest_made")
        s_rest_lo_made = sem("s_rest_lo_made")
        s_pair_added = sem("s_pair_added")
        s_dve_steps = sem("s_dve_steps")
        s_variances = sem("s_variances")
        s_deviations = sem("s_deviations")
        s_weights_T = sem("s_weights_T")
        s_weights_T_kept = sem("s_weights_T_kept")
        s_kv_weights_centred = sem("s_kv_weights_centred")
        s_x_normalised = sem("s_x_normalised")
        s_xn_T = sem("s_xn_T")
        s_xn_T_kept = sem("s_xn_T_kept")
        s_kv_multiplied = sem("s_kv_multiplied")
        s_kv_squared = sem("s_kv_squared")
        s_kv_square_sums = sem("s_kv_square_sums")
        s_head_deviations = sem("s_head_deviations")
        s_kv_normalised = sem("s_kv_normalised")
        s_kv_accumulated = sem("s_kv_accumulated")
        s_kv_blocks = sem("s_kv_blocks")
        s_k_shifts = sem("s_k_shifts")
        s_k_shift_rows = sem("s_k_shift_rows")
        s_kv_wo = sem("s_kv_wo")
        s_kv_wo_kept = sem("s_kv_wo_kept")
        s_mix_weights = sem("s_mix_weights")
        s_mix_weights_kept = sem("s_mix_weights_kept")
        s_xn_T_again = sem("s_xn_T_again")
        s_mix_multiplied = sem("s_mix_multiplied")
        s_mix_added = sem("s_mix_added")
        s_hidden_bias = sem("s_hidden_bias")
        s_hidden_bias_kept = sem("s_hidden_bias_kept")
        s_router_weights_loaded = sem("s_router_weights_loaded")
        s_gamma_beta_cols = sem("s_gamma_beta_cols")
        s_gamma_beta_kept = sem("s_gamma_beta_kept")
        s_expert_weights_loaded = sem("s_expert_weights_loaded")
        s_stream_loaded = [sem(f"s_stream_loaded{a}") for a in range(2)]
        s_stream_stored = sem("s_stream_stored")
        s_means = sem("s_means")
        s_means_T = sem("s_means_T")
        s_means_T_kept = sem("s_means_T_kept")
        s_hidden_multiplied = sem("s_hidden_multiplied")
        s_hidden_relu = sem("s_hidden_relu")
        s_network_out = sem("s_network_out")
        s_stream_added = sem("s_stream_added")
        s_norm_variances = sem("s_norm_variances")
        s_norm_deviations = sem("s_norm_deviations")
        s_y_normalised = sem("s_y_normalised")
        s_y_kept = sem("s_y_kept")
        s_y_T = sem("s_y_T")
        s_y_T_scaled = sem("s_y_T_scaled")
        s_logits_multiplied = sem("s_logits_multiplied")
        s_logits_kept = sem("s_logits_kept")
        s_x_reloaded = [sem(f"s_x_reloaded{a}") for a in range(2)]
        s_mix_stored = sem("s_mix_stored")
        s_expert_rows_cleared = sem("s_expert_rows_cleared")
        s_b1_loaded = sem("s_b1_loaded")
        s_choice_counts = sem("s_choice_counts")
        s_choice_sums = sem("s_choice_sums")
        s_logit_differences = sem("s_logit_differences")
        s_logit_exps = sem("s_logit_exps")
        s_routed = sem("s_routed")
        s_rows_staged = sem("s_rows_staged")
        s_rows_sent = [sem(f"s_rows_sent{m}") for m in range(MOVE)]
        s_expert_rows_loaded = [sem(f"s_expert_rows_loaded{a}") for a in range(2)]
        s_z_T = sem("s_z_T")
        s_z_T_scaled = sem("s_z_T_scaled")
        s_expert_hidden = sem("s_expert_hidden")
        s_expert_hidden_biased = sem("s_expert_hidden_biased")
        s_gelu_done = sem("s_gelu_done")
        s_gelu_T = sem("s_gelu_T")
        s_gelu_T_kept = sem("s_gelu_T_kept")
        s_expert_multiplied = sem("s_expert_multiplied")
        s_expert_biased = sem("s_expert_biased")
        s_expert_stored = [sem(f"s_expert_stored{a}") for a in range(2)]
        s_places_back = sem("s_places_back")
        s_results_fetched = [sem(f"s_results_fetched{m}") for m in range(MOVE)]
        s_stream_reloaded = [sem(f"s_stream_reloaded{m}") for m in range(MOVE)]
        s_combined = sem("s_combined")
        s_out_stored = [sem(f"s_out_stored{m}") for m in range(MOVE)]

        ea_v = edge_attr.rearrange("(p t) f -> p (t f)", p=P)
        buck_fill = buckets.rearrange("(s p q) f -> s p (q f)", s=SEGS, p=128)\
            .rearrange("s p (q w) -> s p q w", q=STEPS * QW)
        buck_units = buckets.rearrange("(g u p j) f -> g p u (j f)", u=2, p=128, j=2)
        ZW = SEG_ROWS * ROW // 128 // (STEPS * QW)
        SORT_FILLS = (SEGS - 2) * (STEPS - 1)
        SW = ETH * D // SORT_FILLS
        assert SW * SORT_FILLS == ETH * D and SW <= ZW
        NCONST = 13

        block = ctx.enter_context(nc.Block())

        def wait_apart(eng, sem, value):
            if not isinstance(value, int):
                value = eng.to_reg(value)
            eng.wait_ge(s_constants, NCONST)
            eng.wait_ge(sem, value)

        def after(eng, sem, value):
            if not (isinstance(value, int) and value <= 0):
                eng.wait_ge(sem, value)

        def in_turn(eng, step, loop=None, between=lambda b, i: None):
            for b in range(2):
                step(b, b, 0)
            with (loop or eng.Fori)(1, 6) as i:
                for a in range(2):
                    step(2 * i + a, a, i)
            for b in range(12, 18):
                step(b, b % 2, b // 2)
                between(b, b // 2)
            with (loop or eng.Fori)(9, 11) as i:
                for a in range(2):
                    step(2 * i + a, a, i)
                between(None, i)
            for b in range(22, NB):
                step(b, b % 2, b // 2)
                between(b, b // 2)

        def known_below(b, n):
            return isinstance(b, int) and b < n

        def known_from(b, n):
            return isinstance(b, int) and b >= n

        def experts_of(kind):
            def load(i):
                _, e = nc.values_load_multi_w_load_instructions(
                    experts3[0:1, bass.ds(i, 1), :].rearrange("p i e -> p (i e)"), engines=(kind,), min_val=0,
                    max_val=NE - 1, skip_runtime_bounds_check_because="they are cut off at NE - 1")
                return e
            return load

        def tile_pairs(eng, h, step, load=lambda i: (None,) * 4, between=None, loop=None, amid=False):
            def pair(i, amid=None):
                e = load(i)
                for a in range(2):
                    step(2 * i + a, a, i, e[a:])
                    if a == 0 and amid:
                        amid()
            pair(h * TP)
            with (loop or eng.Fori)(0, MOVES) as g:
                for m in range(MOVE):
                    pair(h * TP + 1 + g * MOVE + m, (lambda: between(g, m)) if amid else None)
                    if between and amid is False:
                        between(g, m)
            for i in range(1 + NTH, TP - 1):
                pair(h * TP + i)

        @block.sync
        def _(sp):
            def load_chunk(k, col):
                src_cols = ea_v[:, bass.ds(col * EA, CH * EA)]
                dst = stage[:, k].rearrange("p c f -> p (c f)")
                sp.dma_start(dst[0:112, :], src_cols[0:112, :]).then_inc(s_chunk_loaded[k], 16)
                sp.dma_start(dst[112:P, :], src_cols[112:P, :]).then_inc(s_chunk_loaded[k], 16)

            sort_fill = [rows_h.rearrange("(p q) d -> p (q d)", p=128).rearrange("p (q w) -> p q w", w=SW)
                         for rows_h in sorted_y]

            def fill(s, q):
                sp.dma_start(buck_fill[bass.ds(s, 1), :, bass.ds(q * QW, QW), :].rearrange("s p q w -> (s p) q w"),
                             zeros[:, :].unsqueeze(1).to_broadcast([128, QW, ZW])).then_inc(s_rows_cleared, 16)

            def fill_sorted(q):
                for rows_h in sort_fill:
                    sp.dma_start(rows_h[:, bass.ds(q, 1), :].rearrange("p q w -> p (q w)"), zeros[:, 0:SW])\
                        .then_inc(s_expert_rows_cleared, 16)

            def load_unit(g, k):
                sp.wait_ge(s_pair_multiplied, g + 1)
                sp.dma_start(unit[:, k].rearrange("p (u j) f -> p u (j f)", u=2),
                             buck_units[bass.ds(g, 1)].rearrange("g p u q -> (g p) u q")).then_inc(s_unit_loaded[k], 16)

            sp.dma_start(pos[:, :], src.rearrange("(p t) -> p t", p=P)).then_inc(s_src_loaded, 16)
            for k in range(SLOTS):
                load_chunk(k, k * CH)
            sp.wait_ge(s_constants, 1)
            for q in range(STEPS):
                fill(0, q)
            for a in range(5):
                sp.dma_start(xs[:, 10 * a:10 * a + 10, :],
                             x.rearrange("(t p) d -> p t d", p=P)[:, 10 * a:10 * a + 10, :]).then_inc(s_x_loaded, 16)

            def load(dst, src_ap):
                sp.dma_start(dst, src_ap).then_inc(s_weights_loaded, 16)
            for n, w in enumerate((wk, wv, wo)):
                load(raw[:, n], w.rearrange("(c p) i -> p c i", p=128))
            load(w_q[:, :, :], wq.rearrange("(c p) i -> p c i", p=128))
            load(w1x[:, :, :], gnn_W1[0:D, :].rearrange("(c p) h -> p c h", p=128))
            load(w1e[:, :], gnn_W1[D:D + EA, :])
            load(w1u[:, :], gnn_W1[D + EA:, :])
            load(w2[:, :, :], gnn_W2.rearrange("(c p) d -> p c d", p=128))
            load(u_col[:, :], gnn_u[0, :].rearrange("(p a) -> p a", a=1))
            load(b1_row[:, :], gnn_b1.rearrange("(a d) -> a d", a=1))
            load(bias_rows[0:1, 0, :], bo.rearrange("(a d) -> a d", a=1))
            load(bias_rows[0:1, 1, :], gnn_b2.rearrange("(a d) -> a d", a=1))
            for n, row in enumerate((k_g, k_b)):
                load(k_rows[:, n, :], row.rearrange("(a d) -> a d", a=1).to_broadcast([128, HD]))
            for n, row in enumerate((k_g, k_b, v_g, v_b)):
                for h in range(2):
                    load(kv_cols[h * HD:(h + 1) * HD, n:n + 1], row.rearrange("(p a) -> p a", a=1))

            x_tiles = x.rearrange("(j p) d -> j p d", p=P)
            x1_tiles = x1.rearrange("(j p) d -> j p d", p=P)

            def load_g(dst, src_ap):
                sp.dma_start(dst, src_ap).then_inc(s_router_weights_loaded, 16)
            load_g(w_r[:, :, :], Wr.rearrange("(c p) e -> p c e", p=128))
            load_g(br_row[:, :], br.rearrange("(a e) -> a e", a=1))
            load_g(gb_rows[0:1, 0, :], gamma.rearrange("(a d) -> a d", a=1))
            load_g(gb_rows[0:1, 1, :], beta.rearrange("(a d) -> a d", a=1))

            def step(s, i, units, last=False, mix2=False):
                j = (s - SEGS // 2) * (2 * STEPS) + i * 2
                if mix2:
                    for a in range(2):
                        sp.wait_ge(s_mix_stored, (j + 1) * 16)
                        sp.dma_start(xt[:, a, :], x_tiles[bass.ds(j + a, 1)].rearrange("a p d -> (a p) d"))\
                            .then_inc(s_x_reloaded[a], 16)
                if units:
                    for k in range(GROUPS):
                        load_unit((s * STEPS + i - BEHIND) * GROUPS + k, k)
                if not last:
                    for k in range(SLOTS):
                        sp.wait_ge(s_features_copied, s * (STEPS * SLOTS) + i * SLOTS + k + 1)
                        load_chunk(k, s * SC + (i * SLOTS + SLOTS + k) * CH)
                if mix2:
                    for a in range(2):
                        sp.wait_ge(s_mix_added, j + a + 2)
                        sp.dma_start(x1_tiles[bass.ds(j + a, 1)].rearrange("a p d -> (a p) d"), xt[:, a, :])\
                            .then_inc(s_mix_stored, 16)

            def scattered(s):
                for k in range(SLOTS):
                    value = (s + 1) * (STEPS * CH * 16)
                    if isinstance(s, int):
                        sp.wait_ge(s_chunk_scattered[k], value)
                    else:
                        wait_apart(sp, s_chunk_scattered[k], value)

            with sp.Fori(0, STEPS) as i:
                step(0, i, False)
                sp.wait_ge(s_rows_cleared, STEPS * 16)
                fill(1, i)
            for first, end in ((1, 2), (2, SEGS // 2), (SEGS // 2, SEGS - 1)):
                with sp.Fori(first, end) as s:
                    step(s, 0, first > 1, mix2=first >= SEGS // 2)
                    sp.wait_ge(s_rows_cleared, (s + 1) * (STEPS * 16))
                    fill(s + 1, 0)
                    scattered(s - 1)
                    with sp.Fori(1, STEPS) as i:
                        step(s, i, True, mix2=first >= SEGS // 2)
                        fill(s + 1, i)
                        fill_sorted((s - 1) * (STEPS - 1) + i - 1)
            step(SEGS - 1, 0, True, mix2=True)
            scattered(SEGS - 2)
            with sp.Fori(1, STEPS - 1) as i:
                step(SEGS - 1, i, True, mix2=True)
            step(SEGS - 1, STEPS - 1, True, last=True, mix2=True)
            step(SEGS, 0, True, last=True)
            scattered(SEGS - 1)
            with sp.Fori(1, BEHIND) as i:
                step(SEGS, i, True, last=True)
            sp.wait_ge(s_mix_stored, (NT + 1) * 16)
            x1_pairs = x1.rearrange("(b t p) d -> b p t d", p=P, t=2)

            def load_x1(b, a):
                sp.dma_start(x1t[:, a], x1_pairs[bass.ds(b, 1)].rearrange("b p t d -> (b p) t d"))\
                    .then_inc(s_stream_loaded[a], 16)

            def store_x1(b, a):
                sp.wait_ge(s_stream_added, b + 1)
                sp.dma_start(x1_pairs[bass.ds(b, 1)].rearrange("b p t d -> (b p) t d"), x1t[:, a])\
                    .then_inc(s_stream_stored, 16)
                sp.wait_ge(s_stream_stored, (b + 1) * 16)
                wait_apart(sp, s_y_normalised, b + 1)

            load_x1(0, 0)
            load_x1(1, 1)
            sp.wait_ge(s_pair_added, RING - 1 + SEGS * STEPS * GROUPS)
            for c in range(KC):
                sp.dma_start(W1_all.rearrange("p (e c h) -> p e c h", c=KC, h=HID)[:, :, c, :],
                             W1.rearrange("e (c p) h -> p e c h", p=128)[:, :, c, :])\
                                 .then_inc(s_expert_weights_loaded, 16)
            for c in range(HC):
                sp.dma_start(W2_all.rearrange("p (e c d) -> p e c d", c=HC, d=D)[:, :, c, :],
                             W2.rearrange("e (c p) d -> p e c d", p=128)[:, :, c, :])\
                                 .then_inc(s_expert_weights_loaded, 16)
            sp.dma_start(b2_rows, b2.rearrange("(a e) d -> a (e d)", a=1).to_broadcast([128, NE * D]))\
                .then_inc(s_expert_weights_loaded, 16)
            with sp.Fori(0, NB // 2 - 1) as i:
                for a in range(2):
                    store_x1(2 * i + a, a)
                    load_x1(2 * i + a + 2, a)
            for a in range(2):
                store_x1(NB - 3 + a, a)
                if a == 0:
                    load_x1(NB - 1, 0)
            store_x1(NB - 1, 0)
            sp.wait_ge(s_logits_kept, NB)
            sp.dma_start(b1_rows, b1.rearrange("(a e) h -> a (e h)", a=1).to_broadcast([128, NE * HID]))\
                .then_inc(s_b1_loaded, 16)
            row_tiles = [rows_h.rearrange("(r p) d -> r p d", p=TR) for rows_h in sorted_y]
            out_tiles = [rows_h.rearrange("(r p) d -> r p d", p=TR) for rows_h in expert_out]
            out_nodes = out.rearrange("(j p) d -> j p d", p=P)

            def load_rows(h, r, a):
                sp.dma_start(row_in[:, a, :], row_tiles[h][bass.ds(r - h * ETH, 1)].rearrange("a p d -> (a p) d"))\
                    .then_inc(s_expert_rows_loaded[a], 16)

            def store_rows(h, r, a):
                sp.wait_ge(s_expert_biased, r + 1)
                sp.dma_start(out_tiles[h][bass.ds(r - h * ETH, 1)].rearrange("a p d -> (a p) d"), y_out[:, a, :])\
                    .then_inc(s_expert_stored[a], 16)

            def expert_rows(h):
                def step(r, a, i, e):
                    sp.wait_ge(s_z_T, r + 1)
                    load_rows(h, r + 2, a)
                    if not (isinstance(r, int) and r == h * ETH):
                        store_rows(h, r - 1, 1 - a)
                return step

            def load_res(i, m):
                sp.wait_ge(s_out_stored[m], (i + 1) * 16)
                sp.dma_start(res[:, m, :], x1_tiles[bass.ds(i * MOVE + m, 1)].rearrange("a p d -> (a p) d"))\
                    .then_inc(s_stream_reloaded[m], 16)

            def store_res(i, m):
                sp.wait_ge(s_combined, (i + 1) * MOVE + m + 1)
                sp.dma_start(out_nodes[bass.ds(i * MOVE + m, 1)].rearrange("a p d -> (a p) d"), res[:, m, :])\
                    .then_inc(s_out_stored[m], 16)

            def combine_first(g, m):
                load_res(g + (m > 0), (m - 1) % MOVE)
                store_res(g, m)

            for h in range(HALVES):
                for m in range(MOVE):
                    sp.wait_ge(s_rows_sent[m], (h + 1) * MOVES * K * 16)
                if h == 1:
                    for m in range(MOVE - 1):
                        load_res(0, m)
                for a in range(2):
                    if h:
                        sp.wait_ge(s_z_T, h * ETH)
                    load_rows(h, h * ETH + a, a)
                tile_pairs(sp, h, expert_rows(h), between=combine_first if h else None)
                for r in range(ETH - 3, ETH):
                    store_rows(h, h * ETH + r, r % 2)
            load_res(MOVES, MOVE - 1)
            for i in range(MOVES, 2 * MOVES):
                for m in range(MOVE):
                    store_res(i, m)
                if i < 2 * MOVES - 1:
                    for m in range(MOVE):
                        load_res(i + 1, m)
            for m in range(MOVE):
                sp.wait_ge(s_out_stored[m], (2 * MOVES + 1) * 16)

        @block.gpsimd
        def _(pool):
            pool.memset(zeros[:, :], 0.0).then_inc(s_constants, 1)
            for k, (free, n) in enumerate([(s_mix_stored, 16), (s_mix_added, 1), (s_kv_square_sums, 1),
                                           (s_mix_multiplied, 1), (s_xn_T, 1), (s_kv_accumulated, 1),
                                           (s_pair_added, RING - 1 - LAG), (s_combined, MOVE)] +
                                          [(s_out_stored[m], 16) for m in range(MOVE)]):
                pool.memset(spare[0:1, k:k + 1], 0.0).then_inc(free, n)
            pool.memset(ident[:, :], 0.0).then_inc(s_constant_parts, 1)
            pool.memset(below[:, :], 0.0).then_inc(s_constant_parts, 1)
            pool.memset(eps_col[:, :], EPS).then_inc(s_constants, 1)
            pool.memset(eps2_col[:, :], EPS * EPS).then_inc(s_constants, 1)
            pool.memset(ones[:, :], 1.0).then_inc(s_constants, 1)
            pool.memset(rows[:, :, :, :], 1.0).then_inc(s_constants, 1)
            pool.iota(node_iota[:, :], [[1, OH]], base=0, channel_multiplier=0,
                      allow_small_or_imprecise_dtypes=True).then_inc(s_constants, 1)
            pool.iota(bucket_iota[:, :], [[1, NB]], base=0, channel_multiplier=0,
                      allow_small_or_imprecise_dtypes=True).then_inc(s_constants, 1)
            pool.iota(unit_start[:, :], [[UR, NU]], base=0, channel_multiplier=0,
                      allow_small_or_imprecise_dtypes=True).then_inc(s_constants, 1)
            pool.iota(expert_iota[:, :], [[1, NE]], base=0, channel_multiplier=0,
                      allow_small_or_imprecise_dtypes=True).then_inc(s_constants, 1)
            pool.iota(tile_start[:, :], [[TR, ETH]], base=0, channel_multiplier=0,
                      allow_small_or_imprecise_dtypes=True).then_inc(s_constants, 1)
            pool.iota(rk_i[:, 0:SEGS], [[SEG_ROWS // 128, SEGS]], base=0, channel_multiplier=0)\
                .then_inc(s_constant_parts, 1)
            pool.wait_ge(s_constant_parts, 3)
            pool.affine_select(out=ident[:, :], in_=ident[:, :], compare_op=ALU.not_equal, fill=1.0,
                               base=0, pattern=[[-1, 128]], channel_multiplier=1).then_inc(s_constants, 1)
            pool.affine_select(out=below[:, :], in_=below[:, :], compare_op=ALU.is_ge, fill=1.0,
                               base=0, pattern=[[-1, P]], channel_multiplier=1).then_inc(s_constants, 1)
            pool.tensor_scalar(seg_start[:, :], rk_i[:, 0:SEGS], 128.0, 0.0, ALU.mult, ALU.add).then_inc(s_constants, 1)
            with pool.Fori(0, SEGS) as s:
                wait_apart(pool, s_rows_cleared, (s + 1) * (STEPS * 16))
                with pool.Fori(0, STEPS) as i:
                    for k in range(SLOTS):
                        c = s * (STEPS * SLOTS) + i * SLOTS + k
                        pool.wait_ge(s_features_copied, c + 1)
                        wait_apart(pool, s_places_copied, (c + 1) * 2)
                        for e in range(CH):
                            pool.indirect_dma_start(buckets[:, :], bass.IndirectOffsetOnAxis(rows_at[:, k, e:e + 1], 0),
                                                    rows[:, k, e, :], None).then_inc(s_chunk_scattered[k], 16)

            with pool.Fori(1, BEHIND) as i:
                n = (SEGS * STEPS - BEHIND) + i
                for k in range(GROUPS):
                    g = n * GROUPS + k
                    wait_apart(pool, s_unit_loaded[k], (n + 1) * 16)
                    wait_apart(pool, s_pair_multiplied, g + CREDIT - 2)
                    pool.tensor_tensor(rest[:, k % RING], unit[:, k], unit_hi[:, k], ALU.subtract)\
                        .then_inc(s_rest_made, 1)
                    wait_apart(pool, s_rest_made, (i - 1) * GROUPS + k + 1)
                    pool.tensor_tensor(rest_lo[:, k % RING], rest[:, k % RING], rest_hi[:, k % RING], ALU.subtract)\
                        .then_inc(s_rest_lo_made, 1)
            pool.wait_ge(s_expert_rows_cleared, SORT_FILLS * HALVES * 16)

            for h in range(HALVES):
                with pool.Fori(h * MOVES, (h + 1) * MOVES) as i:
                    for m in range(MOVE):
                        wait_apart(pool, s_rows_staged, (i * MOVE + m + 1) * 2)
                        for k in range(K):
                            pool.indirect_dma_start(sorted_y[h][:, :],
                                                    bass.IndirectOffsetOnAxis(send_at[:, m, k:k + 1], 0),
                                                    send[:, m, :], None).then_inc(s_rows_sent[m], 16)
            for h in range(HALVES):
                for a in range(2):
                    pool.wait_ge(s_expert_stored[a], (h + 1) * TP * 16)
                with pool.Fori(h * MOVES, (h + 1) * MOVES) as i:
                    for m in range(MOVE):
                        wait_apart(pool, s_places_back, i * MOVE + m + 1)
                        for k in range(K):
                            pool.indirect_dma_start(fetched[:, m, k, :], None, expert_out[h][:, :],
                                                    bass.IndirectOffsetOnAxis(send_at[:, m, k:k + 1], 0))\
                                .then_inc(s_results_fetched[m], 16)

        @block.scalar
        def _(act):
            act.wait_ge(s_constants, NCONST)

            def chunk(s, i, k):
                c = s * (STEPS * SLOTS) + i * SLOTS + k
                n = s * STEPS + i
                act.wait_ge(s_chunk_loaded[k], (n + 1) * 32)
                after(act, s_chunk_scattered[k], n * (CH * 16))
                nc.scalar.copy(rows[:, k, :, 0:EA], stage[:, k, :, :]).then_inc(s_features_copied, 1)
                col = s * SC + (i * SLOTS + k) * CH
                nc.scalar.copy(rows[:, k, :, EA + 1:ROW],
                               local[:, bass.ds(col, CH)].rearrange("p (c a) -> p c a", a=1))\
                                   .then_inc(s_places_copied, 1)
                nc.scalar.copy(rows_at[:, k, :], pos[:, bass.ds(col, CH)]).then_inc(s_places_copied, 1)

            def pass1(j, a):
                act.wait_ge(s_xn_T, j + 2)
                pt = ps_t[:, 0:KC * P].rearrange("p (c n) -> p c n", c=KC)
                nc.scalar.copy(xnT_t[:, a], pt).then_inc(s_xn_T_kept, 1)
                nc.scalar.copy(xnT[:, bass.ds(j, 1)].rearrange("p a c n -> p (a c) n"), pt).then_inc(s_xn_T_kept, 1)
                act.wait_ge(s_kv_multiplied, j + 1)
                act.wait_ge(s_kv_square_sums, j + 1)
                nc.scalar.activation(sq[:, :], ps_kv[0:P, :], ACT.Square).then_inc(s_kv_squared, 1)
                act.wait_ge(s_kv_square_sums, j + 2)
                nc.scalar.activation(hsd[:, :], ss[:, :], ACT.Sqrt, bias=eps_col[:, :], scale=1.0 / HD)\
                    .then_inc(s_head_deviations, 1)

            def pass2(j, a):
                act.wait_ge(s_mix_multiplied, j + 1)
                nc.scalar.copy(xnT_t[:, a], xnT[:, bass.ds(j, 1)].rearrange("p a c n -> p (a c) n"))\
                    .then_inc(s_xn_T_again, 1)

            def step(s, i, mix):
                for k in range(SLOTS):
                    chunk(s, i, k)
                for a in range(2):
                    if mix == 1:
                        pass1(s * (2 * STEPS) + i * 2 + a, a)
                    else:
                        pass2((s - SEGS // 2) * (2 * STEPS) + i * 2 + a, a)

            act.wait_ge(s_ranked, 1)
            for k in range(SLOTS):
                chunk(0, 0, k)
            for n in range(3):
                act.wait_ge(s_weights_T, n + 1)
                dst = (w_kv[:, :, 0:D], w_kv[:, :, D:2 * D], w_oT[:, :, :])[n]
                nc.scalar.copy(dst, ps_t[:, :].rearrange("p (c d) -> p c d", c=KC)).then_inc(s_weights_T_kept, 1)
            for k in range(SLOTS):
                chunk(0, 1, k)
            act.wait_ge(s_variances, 1)
            nc.scalar.activation(sd[:, :], mv[:, :, 1], ACT.Sqrt, bias=eps_col[:, :]).then_inc(s_deviations, 1)
            act.wait_ge(s_hidden_bias, 1)
            nc.scalar.activation(h_bias[:, :], ps_kv[:, 0:HC], ACT.Copy).then_inc(s_hidden_bias_kept, 1)
            for j in range(2):
                pass1(j, j)
            for k in range(SLOTS):
                chunk(0, 2, k)
            for j in range(2, 6):
                pass1(j, j % 2)
            with act.Fori(3, STEPS) as i:
                step(0, i, 1)
            with act.Fori(1, SEGS // 2) as s:
                act.wait_ge(s_ranked, s + 1)
                with act.Fori(0, STEPS) as i:
                    step(s, i, 1)
            act.wait_ge(s_ranked, SEGS // 2 + 1)
            for k in range(SLOTS):
                chunk(SEGS // 2, 0, k)
            for c in range(KC):
                act.wait_ge(s_kv_wo, KC)
                nc.scalar.copy(kvo[:, c, :], ps_t[:, c * D:(c + 1) * D]).then_inc(s_kv_wo_kept, 1)
            for c in range(KC):
                act.wait_ge(s_mix_weights, KC)
                nc.scalar.copy(mix_w[:, c, :], ps_kv[:, c * D:(c + 1) * D]).then_inc(s_mix_weights_kept, 1)
            for a in range(2):
                pass2(a, a)
            with act.Fori(1, STEPS) as i:
                step(SEGS // 2, i, 2)
            with act.Fori(SEGS // 2 + 1, SEGS) as s:
                act.wait_ge(s_ranked, s + 1)
                with act.Fori(0, STEPS) as i:
                    step(s, i, 2)
            act.wait_ge(s_gamma_beta_cols, 1)
            nc.scalar.copy(gb_col[:, :, :], ps_t[:, 0:2 * KC].rearrange("p (n c) -> p n c", n=2))\
                .then_inc(s_gamma_beta_kept, 1)

            def keep_agg(b):
                act.wait_ge(s_means_T, b + 1)
                nc.scalar.copy(aggT[:, :, :], ps_rank[0:EA, 0:2 * P].rearrange("p (t n) -> p t n", t=2))\
                    .then_inc(s_means_T_kept, 1)

            def relu(b, a):
                after(act, s_network_out, b - 1)
                for hc in range(HC):
                    if hc % 2 == 0:
                        act.wait_ge(s_hidden_multiplied, b * 2 + hc // 2 + 1)
                    nc.scalar.activation(hT[:, a, hc].rearrange("p t n -> p (t n)"),
                                         ps_acc[hc // 2][:, (hc % 2) * BN:(hc % 2 + 1) * BN], ACT.Relu,
                                         bias=h_bias[:, hc:hc + 1]).then_inc(s_hidden_relu, 1)

            def keep_y(b, a):
                act.wait_ge(s_y_normalised, b + 1)
                nc.scalar.copy(xs[:, bass.ds(b * 2, 2), :], y2[:, a]).then_inc(s_y_kept, 1)
                after(act, s_logits_multiplied, b)
                act.wait_ge(s_y_T, b + 1)
                for c in range(KC):
                    nc.scalar.activation(ynT[:, c].rearrange("p t n -> p (t n)"), ps_t[:, c * BN:(c + 1) * BN],
                                         ACT.Identity, scale=gb_col[:, 0, c:c + 1],
                                         bias=gb_col[:, 1, c:c + 1]).then_inc(s_y_T_scaled, 1)

            def keep_logits(b):
                act.wait_ge(s_logits_multiplied, b + 1)
                nc.scalar.copy(logits[:, bass.ds(b * 2, 2), :],
                               ps_kv[0:P, 0:2 * NE].rearrange("p (t e) -> p t e", t=2)).then_inc(s_logits_kept, 1)

            def bucket(b, a, i):
                if not known_from(b, NB - 1):
                    relu(b + 1, 1 - a)
                if not known_below(b, 2):
                    keep_logits(b - 2)
                if not known_from(b, NB - 2):
                    keep_agg(b + 2)
                if not known_below(b, 1):
                    keep_y(b - 1, 1 - a)
                act.wait_ge(s_norm_variances, b + 1)
                nc.scalar.activation(sd2[:, :], mv2[:, :, 1], ACT.Sqrt, bias=eps2_col[:, :], scale=1.0 + EPS)\
                    .then_inc(s_norm_deviations, 1)

            keep_agg(0)
            relu(0, 0)
            keep_agg(1)

            def weights(h):
                act.wait_ge(s_logit_differences, h + 1)
                nc.scalar.activation(top[h][:, 1, 1, :], top[h][:, 1, 0, :], ACT.Exp).then_inc(s_logit_exps, 1)

            def stage_rows(i, m):
                after(act, s_rows_sent[m], i * (K * 16))
                t = i * MOVE + m
                nc.scalar.copy(send[:, m, :], xs[:, bass.ds(t, 1), :].rearrange("p a d -> p (a d)"))\
                    .then_inc(s_rows_staged, 1)
                nc.scalar.copy(send_at[:, m, :],
                               place[:, bass.ds(t, 1), :].rearrange("p a k -> p (a k)")).then_inc(s_rows_staged, 1)

            def half_way(b, i):
                if b == 15:
                    weights(0)
                if b == 17:
                    act.wait_ge(s_routed, 1)
                if b in (17, None, 23, 24):
                    step = {17: 0, None: i - 8, 23: 3, 24: 4}[b]
                    for m in range(MOVE):
                        stage_rows(step, m)

            in_turn(act, bucket, between=half_way)
            keep_logits(NB - 2)
            keep_y(NB - 1, (NB - 1) % 2)
            keep_logits(NB - 1)
            weights(1)
            act.wait_ge(s_routed, 2)

            def scale_rows(r, a):
                act.wait_ge(s_z_T, r + 1)
                after(act, s_expert_hidden, r - 1)
                for c in range(KC):
                    nc.scalar.activation(zT[:, a, c, :], ps_t[:, c * TR:(c + 1) * TR], ACT.Identity,
                                         scale=gb_col[:, 0, c:c + 1], bias=gb_col[:, 1, c:c + 1])\
                                             .then_inc(s_z_T_scaled, 1)

            def gelu(r, a):
                act.wait_ge(s_expert_hidden_biased, r + 1)
                after(act, s_gelu_T, r - 1)
                nc.scalar.activation(hg[:, a, :], hb[:, a, :], ACT.Gelu).then_inc(s_gelu_done, 1)

            def expert_tile(r, a, i, e):
                scale_rows(r + 2, a)
                gelu(r + 1, 1 - a)

            def place_back(i, m):
                act.wait_ge(s_combined, i * MOVE + m + 1)
                nc.scalar.copy(send_at[:, m, :],
                               place[:, bass.ds(i * MOVE + m, 1), :].rearrange("p a k -> p (a k)"))\
                    .then_inc(s_places_back, 1)

            for h in range(HALVES):
                for m in range(MOVE):
                    act.wait_ge(s_rows_sent[m], (h + 1) * MOVES * K * 16)
                if h:
                    for m in range(MOVE):
                        place_back(0, m)
                scale_rows(h * ETH, 0)
                scale_rows(h * ETH + 1, 1)
                gelu(h * ETH, 0)
                tile_pairs(act, h, expert_tile,
                           between=(lambda g, m: stage_rows(g + MOVES, m)) if h == 0 else
                           (lambda g, m: place_back(g + 1, m)))
                gelu(h * ETH + ETH - 1, 1)
            for i in range(MOVES + 1, 2 * MOVES):
                for m in range(MOVE):
                    place_back(i, m)

        @block.vector
        def _(dve):
            did = Steps(dve, s_dve_steps)
            v = nc.vector

            def pause(slots):
                for _ in range(slots):
                    yield

            def rank_stages(s):
                cols = pos[:, bass.ds(s * SC, SC)]
                did.did(v.tensor_scalar(kq[:, :], cols, 1.0 / BN, None, ALU.mult))
                yield
                did.wait()
                did.did(v.scalar_tensor_tensor(kf[:, 0], kq[:, :], -float(BN), cols, ALU.mult, ALU.add))
                yield
                did.wait()
                did.did(v.tensor_scalar(kf[:, 1], kf[:, 0], 0.0, None, ALU.is_lt))
                yield
                did.wait()
                did.did(v.scalar_tensor_tensor(kf[:, 2], kf[:, 1], float(BN), kf[:, 0], ALU.mult, ALU.add))
                did.did(v.scalar_tensor_tensor(kf[:, 3], kf[:, 1], -1.0, kq[:, :], ALU.mult, ALU.add))
                yield
                did.wait()
                did.did(v.tensor_scalar(kf[:, 0], kf[:, 2], float(BN), None, ALU.is_ge))
                yield
                did.wait()
                did.did(v.scalar_tensor_tensor(local[:, bass.ds(s * SC, SC)], kf[:, 0], -float(BN), kf[:, 2],
                                               ALU.mult, ALU.add))
                did.did(v.tensor_tensor(kf[:, 1], kf[:, 3], kf[:, 0], ALU.add))
                yield
                did.wait()
                did.did(v.tensor_tensor(mask[:, :, :], kf[:, 1:2, :].to_broadcast([P, NB, SC]),
                                        bucket_iota[:, :].unsqueeze(2).to_broadcast([P, NB, SC]), ALU.is_equal))
                yield from pause(5)
                did.wait()
                flat = mask[:, :, :].rearrange("p b t -> p (b t)")
                did.did(v.tensor_tensor_scan(count[:, :, :].rearrange("p b t -> p (b t)"), flat, flat, 0.0,
                                             ALU.add, ALU.max))
                yield
                did.wait()
                up_to = count[:, :, SC - 1]
                did.did(v.tensor_copy(hist[:, 0:1], up_to[:, 0:1]))
                v.tensor_tensor(hist[:, 1:], up_to[:, 1:], up_to[:, 0:NB - 1], ALU.subtract)\
                    .then_inc(s_bucket_counts, 1)
                yield PREFIX
                dve.wait_ge(s_lane_sums, s + 1)
                lanes_before, total = ps_rank[0:P, 0:NB], ps_rank[0:P, NB:2 * NB]
                did.did(v.tensor_scalar(rk_i[:, :], total, float(UR - 1), None, ALU.add))
                did.did(v.scalar_tensor_tensor(rk[:, 3], hist[:, :], seg_start[:, bass.ds(s, 1)], up_to,
                                               ALU.add, ALU.subtract))
                yield
                did.wait()
                did.did(v.tensor_scalar(rk_i[:, :], rk_i[:, :], 8, 8, ALU.logical_shift_right, ALU.logical_shift_left))
                yield
                did.wait()
                did.did(v.tensor_copy(rk[:, 0], rk_i[:, :]))
                yield
                did.wait()
                did.did(v.tensor_tensor_scan(rk[:, 2], rk[:, 0], rk[:, 0], 0.0, ALU.add, ALU.max))
                did.did(v.scalar_tensor_tensor(rk[:, 4], lanes_before, -1.0, rk[:, 0], ALU.add, ALU.subtract))
                yield
                did.wait()
                did.did(v.tensor_tensor(rk[:, 5], rk[:, 2], rk[:, 3], ALU.add))
                yield
                did.wait()
                did.did(v.tensor_tensor(rk[:, 6], rk[:, 5], rk[:, 4], ALU.add))
                yield
                did.wait()
                did.did(v.tensor_tensor(count[:, :, :], count[:, :, :],
                                        rk[:, 6, :].unsqueeze(2).to_broadcast([P, NB, SC]), ALU.add))
                yield from pause(6)
                did.wait()
                did.did(v.tensor_tensor(count[:, :, :], count[:, :, :], mask[:, :, :], ALU.mult))
                yield from pause(5)
                wait_apart(dve, did.sem, did.base + did.k)
                with nc.allow_low_precision(reason="whole numbers below 2^24"):
                    v.tensor_reduce(pos[:, bass.ds(s * SC, SC)], count[:, :, :].rearrange("p b t -> p t b"),
                                    AX_X, ALU.add).then_inc(s_ranked, 1)
                yield from pause(6)
                did.did(v.tensor_tensor(filled[:, :, :], rk[0:1, 2:3, :].to_broadcast([1, NU, NB]),
                                        unit_start[:, :].unsqueeze(2).to_broadcast([1, NU, NB]), ALU.is_le))
                yield
                did.wait()
                did.did(v.tensor_reduce(ustart_f[:, :], filled[:, :, :], AX_X, ALU.add))
                yield
                did.wait()
                started = ustart_f[:, :].rearrange("p (i u) -> p i u", i=STEPS)
                late = 2 * LAG
                did.did(v.tensor_scalar(agg_off[:, bass.ds((s * STEPS + 1) * STEP_OFF, STEPS * STEP_OFF)]
                                        .rearrange("p (i u) -> p i u", i=STEPS)[:, :, 0:late],
                                        started[:, :, 2 * GROUPS - late:], float(AGG), None, ALU.mult))
                did.did(v.tensor_scalar(agg_off[:, bass.ds(s * (STEPS * STEP_OFF), STEPS * STEP_OFF)]
                                        .rearrange("p (i u) -> p i u", i=STEPS)[:, :, late:2 * GROUPS],
                                        started[:, :, 0:2 * GROUPS - late], float(AGG), None, ALU.mult))
                did.wait()
                if isinstance(s, int):
                    dve.wait_ge(s_ranked, s + 1)
                else:
                    wait_apart(dve, s_ranked, s + 1)

            def rank(s):
                for _ in rank_stages(s):
                    pass

            RANK = 25

            def pair(n, k, offs, rests=True):
                g = n * GROUPS + k
                dve.wait_ge(s_unit_loaded[k], (n + 1) * 16)
                dve.wait_ge(s_pair_multiplied, g + CREDIT - 2)
                if rests:
                    did.did(v.tensor_tensor(rest[:, k % RING], unit[:, k], unit_hi[:, k], ALU.subtract))
                for t in range(3):
                    v.tensor_scalar(onehot[:, k % RING, t, :], node_iota[:, :], unit[:, k, t, EA + 1:ROW], None,
                                    ALU.is_equal)
                add_unit(g - LAG, (k - LAG) % GROUPS, 0, offs[2 * k])
                end = v.tensor_scalar(onehot[:, k % RING, 3, :], node_iota[:, :], unit[:, k, 3, EA + 1:ROW], None,
                                      ALU.is_equal)
                did.wait()
                if rests:
                    end = v.tensor_tensor(rest_lo[:, k % RING], rest[:, k % RING], rest_hi[:, k % RING], ALU.subtract)
                end.then_inc(s_onehots_made, 1)
                add_unit(g - LAG, (k - LAG) % GROUPS, 1, offs[2 * k + 1])

            aggf = agg[:, :, :].rearrange("p b f -> p (b f)")

            def slots_of(n):
                _, offs = nc.values_load_multi_w_load_instructions(
                    agg_off[0:1, bass.ds(n * STEP_OFF, STEP_OFF)], engines=(mybir.EngineType.DVE,),
                    min_val=0, max_val=NB * AGG, skip_runtime_bounds_check_because="rank() writes only slots' offsets")
                return offs

            def add_unit(g, k, u, off):
                if u == 0:
                    dve.wait_ge(s_pair_multiplied, g + CREDIT + 1)
                    dve.wait_ge(s_pair_added, g + RING - 1)
                slot = aggf[:, bass.ds(off, AGG)]
                add = v.tensor_tensor(slot, slot, ps_g[k % RING][0:P, u * AGG:(u + 1) * AGG], ALU.add)
                if u == 0:
                    did.did(add)
                else:
                    add.then_inc(s_pair_added, 1)

            def mix_stages(j, a):
                def normalise():
                    dve.wait_ge(s_xn_T, j + 1)
                    v.tensor_scalar(xn[:, a], xs[:, bass.ds(j, 1), :].rearrange("p a d -> p (a d)"),
                                    mv[:, bass.ds(j, 1), 0], rstd[:, bass.ds(j, 1)],
                                    ALU.subtract, ALU.mult).then_inc(s_x_normalised, 1)

                def squares():
                    dve.wait_ge(s_kv_squared, j + 1)
                    v.tensor_reduce(ss[:, :], sq[:, :].rearrange("p (h d) -> p h d", d=HD), AX_X, ALU.add)\
                        .then_inc(s_kv_square_sums, 1)

                def kv():
                    dve.wait_ge(s_head_deviations, j + 1)
                    did.did(v.reciprocal(hrs[:, :], hsd[:, :]))
                    did.wait()
                    dve.wait_ge(s_kv_accumulated, j + 1)
                    dst = kvn[:, a].rearrange("p (h d) -> p h d", d=HD)
                    v.tensor_tensor(dst, ps_kv[0:P, :].rearrange("p (h d) -> p h d", d=HD),
                                    hrs[:, :].unsqueeze(2).to_broadcast([P, 8, HD]), ALU.mult)\
                                        .then_inc(s_kv_normalised, 1)

                return {0: normalise, 3: squares, 4: kv}

            def mix2(j, a, n):
                dve.wait_ge(s_mix_multiplied, j + 2)
                dve.wait_ge(s_x_reloaded[a], (n + 1) * 16)
                v.tensor_tensor(xt[:, a], xt[:, a], ps_kv[0:P, a * D:(a + 1) * D], ALU.add).then_inc(s_mix_added, 1)

            def step(s, i, mix, groups, ranking=None, rests=True):
                if mix == 1:
                    j = s * (2 * STEPS) + i * 2
                    todo = mix_stages(j, 0)
                    todo.update({k + 5: f for k, f in mix_stages(j + 1, 1).items()})
                elif mix == 2:
                    j = (s - SEGS // 2) * (2 * STEPS) + i * 2
                    n2 = (s - SEGS // 2) * STEPS + i
                    todo = {2: lambda: mix2(j, 0, n2), 7: lambda: mix2(j + 1, 1, n2)}
                else:
                    todo = {}
                n = s * STEPS + i - BEHIND
                for k in range(GROUPS):
                    if groups:
                        if k == 0:
                            offs = slots_of(n)
                        pair(n, k, offs, rests)
                    if k in todo:
                        todo[k]()
                    if ranking is not None:
                        ranking(i)

            def segment(s, mix, groups):
                stages = rank_stages(s + 1)
                at_prefix = []

                def ranking(i):
                    if at_prefix and i < PREFIX_STEP:
                        return
                    if next(stages, None) is PREFIX:
                        at_prefix.append(True)

                for i in range(STEPS):
                    step(s, i, mix, groups and not (isinstance(s, int) and s * STEPS + i < BEHIND), ranking)
                    if i == PREFIX_STEP - 1:
                        assert at_prefix
                assert next(stages, PREFIX + 1) == PREFIX + 1

            G_STEP = 2 * GROUPS
            M_STEP = 2

            did.did(v.memset(agg_off[:, :], NB * AGG))
            dve.wait_ge(s_constants, NCONST)
            dve.wait_ge(s_src_loaded, 16)
            rank(0)
            did.did(v.memset(agg[:, 0:1, :], 0.0))
            v.memset(agg[:, 1:, :], 0.0).then_inc(s_pair_multiplied, CREDIT)
            for k in range(GROUPS - LAG, GROUPS):
                did.did(v.memset(ps_g[k % RING][:, :], 0.0))
            dve.wait_ge(s_x_loaded, 80)
            with did.loop(0, NT, 1) as j:
                did.did(v.bn_stats(stats[:, bass.ds(j, 1), :].rearrange("p a d -> p (a d)"),
                                   xs[:, bass.ds(j, 1), :].rearrange("p a d -> p (a d)")))
            did.wait()
            did.did(v.tensor_tensor(mv[:, :, 0], stats[:, :, 1], stats[:, :, 4], ALU.add))
            did.did(v.tensor_tensor(mv[:, :, 1], stats[:, :, 1], stats[:, :, 4], ALU.subtract))
            did.did(v.tensor_tensor(rstd[:, :], stats[:, :, 2], stats[:, :, 5], ALU.add))
            did.wait()
            did.did(v.tensor_scalar(mv[:, :, 0], mv[:, :, 0], 0.5, None, ALU.mult))
            did.did(v.tensor_tensor(sd[:, :], mv[:, :, 1], mv[:, :, 1], ALU.mult))
            did.wait()
            did.did(v.tensor_scalar(sd[:, :], sd[:, :], 0.25, None, ALU.mult))
            did.wait()
            v.scalar_tensor_tensor(mv[:, :, 1], rstd[:, :], 1.0 / D, sd[:, :], ALU.mult, ALU.add)\
                .then_inc(s_variances, 1)
            dve.wait_ge(s_weights_T_kept, 2)
            for c in range(KC):
                wc = w_kv[:, c].rearrange("p (h d) -> p h d", d=HD)
                did.did(v.tensor_reduce(csum[:, c], wc, AX_X, ALU.add))
            did.wait()
            did.did(v.tensor_scalar(csum[:, :, :], csum[:, :, :], 1.0 / HD, None, ALU.mult))
            did.wait()
            for c in range(KC):
                wc = w_kv[:, c].rearrange("p (h d) -> p h d", d=HD)
                last = v.tensor_tensor(wc, wc, csum[:, c].unsqueeze(2).to_broadcast([128, 8, HD]), ALU.subtract)
                last.then_inc(s_kv_weights_centred, 1)
            dve.wait_ge(s_deviations, 1)
            did.did(v.reciprocal(rstd[:, :], sd[:, :]))
            did.wait()
            segment(0, 1, False)
            segment(1, 1, True)
            with did.loop(2, SEGS // 2, RANK + STEPS * (M_STEP + G_STEP)) as s:
                segment(s, 1, True)
            dve.wait_ge(s_kv_accumulated, NT + 1)
            did.did(v.memset(kv_sb[:, :, :], 0.0))
            did.wait()
            did.did(v.tensor_copy(kv_sums[:, :], ps_sums))
            did.did(v.tensor_scalar(k_shift[:, KC:], kv_cols[:, 1:2], float(N), None, ALU.mult))
            did.wait()
            for c in range(KC):
                did.did(v.scalar_tensor_tensor(k_shift[:, c:c + 1], kv_sums[:, c:c + 1], kv_cols[:, 0:1],
                                               k_shift[:, KC:], ALU.mult, ALU.add))
            did.wait()
            v.tensor_copy(kvo[:, 0, :].rearrange("p (c n) -> p c n", c=KC),
                          k_shift[:, 0:KC].unsqueeze(2).to_broadcast([128, KC, 128])).then_inc(s_k_shifts, 1)
            blocks = [(c, slice(HD * h, HD * h + HD)) for c in range(KC) for h in range(2)]
            for c, r in blocks:
                did.did(v.tensor_tensor(kv_sb[r, c, r], ps_vk[c][r, r], k_rows[r, 0, :], ALU.mult))
            did.wait()
            for c, r in blocks:
                did.did(v.scalar_tensor_tensor(kv_sb[r, c, r], k_rows[r, 1, :], kv_sums[r, KC + c:KC + c + 1],
                                               kv_sb[r, c, r], ALU.mult, ALU.add))
            did.wait()
            for c, r in blocks:
                did.did(v.tensor_scalar(kv_sb[r, c, r], kv_sb[r, c, r], kv_cols[r, 2:3], None, ALU.mult))
            did.wait()
            dve.wait_ge(s_k_shift_rows, 1)
            for c, r in blocks:
                did.did(v.scalar_tensor_tensor(kv_sb[r, c, r], ps_t[r, c * 128 + r.start:c * 128 + r.stop],
                                               kv_cols[r, 3:4], kv_sb[r, c, r], ALU.mult, ALU.add))
            did.wait()
            for c, r in blocks:
                v.tensor_scalar(kv_sb[r, c, r], kv_sb[r, c, r], 1.0 / N, None, ALU.mult).then_inc(s_kv_blocks, 1)
            with did.loop(SEGS // 2, SEGS - 1, RANK + STEPS * G_STEP) as s:
                segment(s, 2, True)
            with did.loop(0, STEPS, G_STEP) as i:
                step(SEGS - 1, i, 2, True)
            step(SEGS, 0, 0, True)
            with did.loop(1, BEHIND, GROUPS) as i:
                step(SEGS, i, 0, True, rests=False)
            offs = slots_of(SEGS * STEPS)
            for k in range(LAG):
                for u in range(2):
                    add_unit(SEGS * STEPS * GROUPS + k - LAG, GROUPS + k - LAG, u, offs[2 * k + u])
                    did.wait()
            dve.wait_ge(s_pair_added, RING - 1 + SEGS * STEPS * GROUPS)

            def network(b):
                sums = agg[:, bass.ds(b, 1), :].rearrange("p b (h f) -> p (b h) f", h=2)
                did.did(v.tensor_scalar(cnt[:, :], sums[:, :, EA], 1.0, None, ALU.max))
                did.wait()
                did.did(v.reciprocal(rcnt[:, :], cnt[:, :]))
                did.wait()
                after(dve, s_means_T, b)
                v.tensor_tensor(aggn[:, :, :], sums[:, :, 0:EA], rcnt[:, :].unsqueeze(2).to_broadcast([P, 2, EA]),
                                ALU.mult).then_inc(s_means, 1)

            def bucket(b, a, i):
                dve.wait_ge(s_stream_loaded[a], (i + 1) * 16)
                dve.wait_ge(s_network_out, b + 1)
                v.tensor_tensor(x1t[:, a], x1t[:, a], ps_g[0][0:P, :].rearrange("p (t d) -> p t d", t=2),
                                ALU.add).then_inc(s_stream_added, 1)
                dve.wait_ge(s_stream_added, b + 1)
                for q in range(2):
                    did.did(v.bn_stats(st[:, q, :], x1t[:, a, q, :]))
                wait_apart(dve, did.sem, did.base + did.k)
                did.did(v.bn_aggr(mv2[:, 0, :], st[:, 0, :]))
                v.bn_aggr(mv2[:, 1, :], st[:, 1, :]).then_inc(s_norm_variances, 1)
                if not known_from(b, NB - 3):
                    network(b + 3)
                dve.wait_ge(s_norm_variances, b + 1)
                dve.wait_ge(s_norm_deviations, b + 1)
                did.did(v.reciprocal(rs2[:, :], sd2[:, :]))
                did.wait()
                after(dve, s_y_T, b - 1)
                after(dve, s_y_kept, b - 1)
                for q in range(2):
                    end = v.tensor_scalar(y2[:, a, q, :], x1t[:, a, q, :], mv2[:, q, 0:1], rs2[:, q:q + 1],
                                          ALU.subtract, ALU.mult)
                end.then_inc(s_y_normalised, 1)

            for b in range(3):
                network(b)
            def route(h):
                dve.wait_ge(s_logits_kept, (NB // 2 + 1, NB)[h])
                if h:
                    dve.wait_ge(s_stream_stored, NB * 16)
                    dve.wait_ge(s_y_kept, NB)
                did.wait()
                experts = expert_iota[:, :].unsqueeze(1).to_broadcast([P, NTH, NE])
                for k in range(K):
                    vals = (logits[:, h * NTH:(h + 1) * NTH, :], left[h])[k]
                    did.did(v.tensor_reduce(top[h][:, k, 0, :], vals[:, :, :], AX_X, ALU.max))
                    did.wait()
                    did.did(v.tensor_tensor(tmp[h][:, :, :], vals[:, :, :],
                                            top[h][:, k, 0, :].unsqueeze(2).to_broadcast([P, NTH, NE]), ALU.is_equal))
                    did.wait()
                    did.did(v.scalar_tensor_tensor(tmp[h][:, :, :], tmp[h][:, :, :], -float(NE), experts, ALU.mult, ALU.add))
                    did.wait()
                    did.did(v.tensor_reduce(top[h][:, k, 1, :], tmp[h][:, :, :], AX_X, ALU.min))
                    did.wait()
                    did.did(v.tensor_scalar(top[h][:, k, 1, :], top[h][:, k, 1, :], float(NE), None, ALU.add))
                    did.wait()
                    did.did(v.tensor_tensor(best[h][:, :, k * NTH:(k + 1) * NTH].rearrange("p e t -> p t e"),
                                            top[h][:, k, 1, :].unsqueeze(2).to_broadcast([P, NTH, NE]), experts, ALU.is_equal))
                    did.wait()
                    if k == 0:
                        did.did(v.scalar_tensor_tensor(left[h][:, :, :],
                                                       best[h][:, :, 0:NTH].rearrange("p e t -> p t e"), -BIG,
                                                       logits[:, h * NTH:(h + 1) * NTH, :], ALU.mult, ALU.add))
                        did.wait()
                v.tensor_tensor(top[h][:, 1, 0, :], top[h][:, 1, 0, :], top[h][:, 0, 0, :], ALU.subtract)\
                    .then_inc(s_logit_differences, 1)
                v.tensor_reduce(hist[:, 0:NE], best[h][:, :, :], AX_X, ALU.add).then_inc(s_choice_counts, 1)
                flat = best[h][:, :, :].rearrange("p e t -> p (e t)")
                did.did(v.tensor_tensor_scan(at[h][:, :, :].rearrange("p e t -> p (e t)"), flat, flat, 0.0, ALU.add, ALU.max))
                yield
                dve.wait_ge(s_logit_exps, h + 1)
                did.did(v.tensor_scalar(top[h][:, 0, 2, :], top[h][:, 1, 1, :], 1.0, None, ALU.add))
                did.wait()
                did.did(v.reciprocal(weight[:, h, 0, :], top[h][:, 0, 2, :]))
                did.wait()
                did.did(v.tensor_tensor(weight[:, h, 1, :], weight[:, h, 0, :], top[h][:, 1, 1, :], ALU.mult))
                did.did(v.memset(experts3[:, h * TP:(h + 1) * TP, :], 0))
                dve.wait_ge(s_choice_counts, h + 1)
                dve.wait_ge(s_choice_sums, h + 1)
                lanes_before, total = ps_g[2][0:P, 0:NE], ps_g[2][0:P, NE:2 * NE]
                did.did(v.tensor_scalar(rk_i[:, 0:NE], total, float(TR - 1), None, ALU.add))
                did.wait()
                did.did(v.tensor_scalar(rk_i[:, 0:NE], rk_i[:, 0:NE], 7, 7, ALU.logical_shift_right, ALU.logical_shift_left))
                did.wait()
                did.did(v.tensor_copy(rk[:, 0, 0:NE], rk_i[:, 0:NE]))
                did.did(v.tensor_tensor_scan(rk[:, 1, 0:NE], hist[:, 0:NE], hist[:, 0:NE], 0.0, ALU.add, ALU.max))
                did.wait()
                did.did(v.tensor_tensor_scan(rk[:, 2, 0:NE], rk[:, 0, 0:NE], rk[:, 0, 0:NE], 0.0, ALU.add, ALU.max))
                did.did(v.tensor_tensor(rk[:, 3, 0:NE], hist[:, 0:NE], rk[:, 1, 0:NE], ALU.subtract))
                did.did(v.scalar_tensor_tensor(rk[:, 4, 0:NE], lanes_before, -1.0, rk[:, 0, 0:NE], ALU.add, ALU.subtract))
                did.wait()
                did.did(v.tensor_tensor(rk[:, 5, 0:NE], rk[:, 2, 0:NE], rk[:, 3, 0:NE], ALU.add))
                did.did(v.tensor_tensor(ended[:, :, :], rk[0:1, 2:3, 0:NE].to_broadcast([1, ETH, NE]),
                                        tile_start[:, :].unsqueeze(2).to_broadcast([1, ETH, NE]), ALU.is_le))
                did.wait()
                did.did(v.tensor_tensor(rk[:, 6, 0:NE], rk[:, 5, 0:NE], rk[:, 4, 0:NE], ALU.add))
                did.did(v.tensor_reduce(expert_f[:, :], ended[:, :, :], AX_X, ALU.add))
                did.wait()
                pairs_f = expert_f[:, :].rearrange("p (i a) -> p i a", a=2)
                did.did(v.tensor_scalar(experts3[:, h * TP:(h + 1) * TP, 0:2], pairs_f, float(NE - 1), None, ALU.min))
                did.did(v.tensor_scalar(experts3[:, h * TP:(h + 1) * TP - 1, 2:3], pairs_f[:, 1:, 0:1], float(NE - 1), None, ALU.min))
                did.did(v.tensor_tensor(at[h][:, :, :], at[h][:, :, :],
                                        rk[:, 6, 0:NE].unsqueeze(2).to_broadcast([P, NE, K * NTH]), ALU.add))
                did.wait()
                did.did(v.tensor_tensor(at[h][:, :, :], at[h][:, :, :], best[h][:, :, :], ALU.mult))
                did.wait()
                with nc.allow_low_precision(reason="whole numbers below 2^24"):
                    for k in range(K):
                        end = v.tensor_reduce(place[:, h * NTH:(h + 1) * NTH, k],
                                              at[h][:, :, k * NTH:(k + 1) * NTH].rearrange("p e t -> p t e"),
                                              AX_X, ALU.add)
                end.then_inc(s_routed, 1)

            routing = route(0)

            def half_way(b, i):
                if b in (14, 15):
                    next(routing, None)

            in_turn(dve, bucket, lambda start, end: did.loop(start, end, 2 * (4 + 2)), between=half_way)
            did.wait()
            for _ in route(1):
                pass

            def add_b1(r, a, e):
                dve.wait_ge(s_expert_hidden, r + 1)
                after(dve, s_gelu_done, r - 1)
                v.tensor_tensor(hb[:, a, :], ps_acc[a][:, :], b1_rows[:, bass.ds(e * HID, HID)], ALU.add)\
                    .then_inc(s_expert_hidden_biased, 1)

            def keep_gT(r, a):
                dve.wait_ge(s_gelu_T, r + 1)
                after(dve, s_expert_multiplied, r - 1)
                v.tensor_copy(hgT[:, a].rearrange("p c n -> p (c n)"), ps_g[a][:, :]).then_inc(s_gelu_T_kept, 1)

            def add_b2(r, a, i, e):
                dve.wait_ge(s_expert_multiplied, r + 1)
                after(dve, s_expert_stored[a], i * 16)
                v.tensor_tensor(y_out[:, a, :], ps_y[a][:, 0:D], b2_rows[:, bass.ds(e * D, D)], ALU.add)\
                    .then_inc(s_expert_biased, 1)

            def expert_tile(r, a, i, e):
                add_b1(r + 1, 1 - a, e[1])
                add_b2(r, a, i, e[0])
                keep_gT(r + 1, 1 - a)

            dve.wait_ge(s_b1_loaded, 16)
            dve.wait_ge(s_expert_weights_loaded, (KC + HC + 1) * 16)

            def combine(h, i, m):
                t = i * MOVE + m
                dve.wait_ge(s_stream_reloaded[m], (i + 1) * 16)
                dve.wait_ge(s_results_fetched[m], (i + 1) * (K * 16))
                did.did(v.scalar_tensor_tensor(res[:, m, :], fetched[:, m, 0, :],
                                               weight[:, h, 0, bass.ds(t - h * NTH, 1)],
                                               res[:, m, :], ALU.mult, ALU.add))
                did.wait()
                v.scalar_tensor_tensor(res[:, m, :], fetched[:, m, 1, :], weight[:, h, 1, bass.ds(t - h * NTH, 1)],
                                       res[:, m, :], ALU.mult, ALU.add).then_inc(s_combined, 1)

            load = experts_of(mybir.EngineType.DVE)
            for h in range(HALVES):
                first = h * ETH
                add_b1(first, 0, load(h * TP)[0])
                keep_gT(first, 0)
                tile_pairs(dve, h, expert_tile, load, between=(lambda g, m: combine(0, g, m)) if h else None, amid=bool(h),
                           loop=lambda start, end: did.loop(start, end, MOVE * h))
                e = load(h * TP + TP - 1)
                add_b1(first + ETH - 1, 1, e[1])
                add_b2(first + ETH - 2, 0, (h + 1) * TP - 1, e[0])
                keep_gT(first + ETH - 1, 1)
                add_b2(first + ETH - 1, 1, (h + 1) * TP - 1, e[1])
            with did.loop(MOVES, 2 * MOVES, MOVE) as i:
                for m in range(MOVE):
                    combine(1, i, m)

        @block.tensor
        def _(pe):
            t = nc.tensor
            pe.wait_ge(s_constants, NCONST)

            def rank(s):
                pe.wait_ge(s_bucket_counts, s + 1)
                after(pe, s_ranked, s)
                t.matmul(ps_rank[0:P, 0:NB], below[:, :], hist[:, :], start=True, stop=True)
                t.matmul(ps_rank[0:P, NB:2 * NB], ones[:, :], hist[:, :], start=True, stop=True)\
                    .then_inc(s_lane_sums, 1)

            def pair(g, k, rests=None):
                pe.wait_ge(s_onehots_made, g + 1)
                if rests is not None:
                    pe.wait_ge(s_rest_lo_made, rests + 1)
                pe.wait_ge(s_pair_added, g + 1)
                for u in range(2):
                    for half in range(2):
                        o = u * AGG + half * (EA + 1)
                        for j in range(2):
                            for n, rows_of in enumerate((unit_hi[:, k], rest_hi[:, k % RING], rest_lo[:, k % RING])):
                                last = t.matmul(ps_g[k % RING][:, o:o + EA + 1],
                                                onehot[:, k % RING, 2 * u + j, half * P:half * P + 128],
                                                rows_of[:, 2 * u + j, 0:EA + 1],
                                                start=(j == 0 and n == 0), stop=(j == 1 and n == 2))
                last.then_inc(s_pair_multiplied, 1)

            def project(j, a):
                pe.wait_ge(s_x_normalised, j + 1)
                after(pe, s_xn_T_kept, 2 * j)
                for c in range(KC):
                    last = t.transpose(ps_t[:, c * P:(c + 1) * P], xn[:, a, c * 128:(c + 1) * 128], ident[0:P, 0:P])
                last.then_inc(s_xn_T, 1)
                pe.wait_ge(s_xn_T_kept, 2 * j + 2)
                after(pe, s_kv_normalised, j)
                for c in range(KC):
                    last = t.matmul(ps_kv[0:P, :], xnT_t[:, a, c, :], w_kv[:, c, :], start=(c == 0), stop=(c == KC - 1))
                last.then_inc(s_kv_multiplied, 1)

            def accumulate(j, a, start):
                pe.wait_ge(s_kv_normalised, j + 1)
                for c in range(KC):
                    last = t.matmul(ps_vk[c], kvn[:, a, D + 128 * c:D + 128 * c + 128],
                                    kvn[:, a, 128 * c:128 * c + 128], start=start and c == 0, stop=False,
                                    skip_group_check=True)
                    for n in range(2):
                        last = t.matmul(ps_sums[:, n * KC + c:n * KC + c + 1],
                                        kvn[:, a, n * D + 128 * c:n * D + 128 * c + 128], ones[:, 0:1],
                                        start=False, stop=False, skip_group_check=True)
                last.then_inc(s_kv_accumulated, 1)

            def mix2(j, a):
                pe.wait_ge(s_xn_T_again, j + 1)
                pe.wait_ge(s_mix_added, j + 1)
                o = ps_kv[0:P, a * D:(a + 1) * D]
                for c in range(KC):
                    t.matmul(o, xnT_t[:, a, c, :], mix_w[:, c, :], start=(c == 0), stop=False)
                for r in range(2):
                    last = t.matmul(o, ones[0:1, :], bias_rows[0:1, r, :], start=False, stop=(r == 1))
                last.then_inc(s_mix_multiplied, 1)

            def step(s, i, mix, groups, first=False, rests=False):
                if mix == 1:
                    j = s * (2 * STEPS) + i * 2
                    todo = {0: lambda: project(j, 0), 5: lambda: project(j + 1, 1),
                            6: lambda: accumulate(j, 0, first), 10: lambda: accumulate(j + 1, 1, False)}
                elif mix == 2:
                    j = (s - SEGS // 2) * (2 * STEPS) + i * 2
                    todo = {1: lambda: mix2(j, 0), 6: lambda: mix2(j + 1, 1)}
                else:
                    todo = {}
                n = s * STEPS + i - BEHIND
                for k in range(GROUPS):
                    if groups:
                        pair(n * GROUPS + k, k, (i - 1) * GROUPS + k if rests else None)
                    if k in todo:
                        todo[k]()

            rank(0)
            pe.wait_ge(s_weights_loaded, 22 * 16)
            for n in range(3):
                after(pe, s_weights_T_kept, n)
                for ci in range(KC):
                    for co in range(KC):
                        last = t.transpose(ps_t[:, ci * D + co * 128:ci * D + co * 128 + 128],
                                           raw[:, n, co, ci * 128:(ci + 1) * 128], ident[:, :])
                last.then_inc(s_weights_T, 1)
            for c in range(HC):
                o = ps_kv[:, c:c + 1]
                t.matmul(o, w1u[:, c * 128:(c + 1) * 128], u_col[:, :], start=True, stop=False)
                last = t.matmul(o, b1_row[0:1, c * 128:(c + 1) * 128], ones[0:1, 0:1], start=False, stop=True)
            last.then_inc(s_hidden_bias, 1)
            pe.wait_ge(s_kv_weights_centred, 2)
            pe.wait_ge(s_weights_T_kept, 3)
            pe.wait_ge(s_hidden_bias_kept, 1)
            step(0, 0, 1, False, first=True)
            with pe.Fori(1, PREFIX_STEP) as i:
                step(0, i, 1, False)
            rank(1)
            with pe.Fori(PREFIX_STEP, STEPS) as i:
                step(0, i, 1, False)
            step(1, 0, 1, False)
            with pe.Fori(1, PREFIX_STEP) as i:
                step(1, i, 1, True)
            rank(2)
            with pe.Fori(PREFIX_STEP, STEPS) as i:
                step(1, i, 1, True)
            with pe.Fori(2, SEGS // 2) as s:
                with pe.Fori(0, PREFIX_STEP) as i:
                    step(s, i, 1, True)
                rank(s + 1)
                with pe.Fori(PREFIX_STEP, STEPS) as i:
                    step(s, i, 1, True)
            pe.wait_ge(s_k_shifts, 1)
            for c in range(KC):
                last = t.matmul(ps_t[:, c * 128:(c + 1) * 128], kvo[:, 0, c * 128:(c + 1) * 128], ident[:, :],
                                start=True, stop=True)
            last.then_inc(s_k_shift_rows, 1)
            pe.wait_ge(s_kv_blocks, 4)
            for c in range(KC):
                t.matmul(ps_t[:, c * D:(c + 1) * D], kv_sb[:, c, :], w_oT[:, c, :], start=True, stop=True)\
                    .then_inc(s_kv_wo, 1)
            pe.wait_ge(s_kv_wo_kept, KC)
            pe.wait_ge(s_kv_normalised, NT)
            for ci in range(KC):
                for c in range(KC):
                    last = t.matmul(ps_kv[:, ci * D:(ci + 1) * D], w_q[:, c, ci * 128:(ci + 1) * 128], kvo[:, c, :],
                                    start=(c == 0), stop=(c == KC - 1))
                last.then_inc(s_mix_weights, 1)
            pe.wait_ge(s_mix_weights_kept, KC)
            with pe.Fori(SEGS // 2, SEGS - 1) as s:
                with pe.Fori(0, PREFIX_STEP) as i:
                    step(s, i, 2, True)
                rank(s + 1)
                with pe.Fori(PREFIX_STEP, STEPS) as i:
                    step(s, i, 2, True)
            with pe.Fori(0, STEPS) as i:
                step(SEGS - 1, i, 2, True)
            step(SEGS, 0, 0, True)
            with pe.Fori(1, BEHIND) as i:
                step(SEGS, i, 0, True, rests=True)

            pe.wait_ge(s_router_weights_loaded, 4 * 16)
            for n in range(2):
                for c in range(KC):
                    last = t.matmul(ps_t[:, n * KC + c:n * KC + c + 1], gb_rows[0:1, n, c * 128:(c + 1) * 128],
                                    ones[0:1, 0:1], start=True, stop=True)
            last.then_inc(s_gamma_beta_cols, 1)
            pe.wait_ge(s_gamma_beta_kept, 1)
            pe.wait_ge(s_mix_added, NT + 1)
            pe.wait_ge(s_pair_added, RING - 1 + SEGS * STEPS * GROUPS)

            def means_T(b):
                after(pe, s_means_T_kept, b)
                wait_apart(pe, s_means, b + 1)
                for a in range(2):
                    end = t.transpose(ps_rank[0:EA, a * P:(a + 1) * P], aggn[:, a, :], ident[0:P, 0:P])
                end.then_inc(s_means_T, 1)

            def hidden_T(b):
                pe.wait_ge(s_means_T_kept, b + 1)
                for hc in range(HC):
                    if hc % 2 == 0:
                        after(pe, s_hidden_relu, (b - 1) * HC + hc + 2)
                    o = ps_acc[hc // 2][:, (hc % 2) * BN:(hc % 2 + 1) * BN]
                    for c in range(KC):
                        t.matmul(o, w1x[:, c, hc * 128:(hc + 1) * 128], xnT[:, bass.ds(b * 2, 2), c, :],
                                 start=(c == 0), stop=False)
                    end = t.matmul(o, w1e[:, hc * 128:(hc + 1) * 128], aggT[:, :, :].rearrange("p t n -> p (t n)"),
                                   start=False, stop=True)
                    if hc % 2:
                        end.then_inc(s_hidden_multiplied, 1)

            def network_out(b, a):
                pe.wait_ge(s_hidden_relu, (b + 1) * HC)
                after(pe, s_stream_added, b)
                for q in range(2):
                    for hc in range(HC):
                        end = t.matmul(ps_g[0][0:P, q * D:(q + 1) * D], hT[:, a, hc, q, :], w2[:, hc, :],
                                       start=(hc == 0), stop=(hc == HC - 1))
                end.then_inc(s_network_out, 1)

            def y_T(b, a):
                after(pe, s_y_T_scaled, b * KC)
                wait_apart(pe, s_y_normalised, b + 1)
                for q in range(2):
                    for c in range(KC):
                        end = t.transpose(ps_t[:, c * BN + q * P:c * BN + (q + 1) * P],
                                          y2[:, a, q, c * 128:(c + 1) * 128], ident[0:P, 0:P])
                end.then_inc(s_y_T, 1)

            def router(b):
                after(pe, s_logits_kept, b)
                pe.wait_ge(s_y_T_scaled, (b + 1) * KC)
                for q in range(2):
                    o = ps_kv[0:P, q * NE:(q + 1) * NE]
                    for c in range(KC):
                        t.matmul(o, ynT[:, c, q, :], w_r[:, c, :], start=(c == 0), stop=False)
                    end = t.matmul(o, ones[0:1, :], br_row[:, :], start=False, stop=True)
                end.then_inc(s_logits_multiplied, 1)

            def bucket(b, a, i):
                if not known_from(b, NB - 1):
                    hidden_T(b + 1)
                if not known_below(b, 2):
                    router(b - 2)
                network_out(b, a)
                if not known_from(b, NB - 2):
                    means_T(b + 2)
                if not known_below(b, 1):
                    y_T(b - 1, 1 - a)

            means_T(0)
            hidden_T(0)
            means_T(1)

            def choices(h):
                pe.wait_ge(s_choice_counts, h + 1)
                t.matmul(ps_g[2][0:P, 0:NE], below[:, :], hist[:, 0:NE], start=True, stop=True)
                t.matmul(ps_g[2][0:P, NE:2 * NE], ones[:, :], hist[:, 0:NE], start=True, stop=True)\
                    .then_inc(s_choice_sums, 1)

            in_turn(pe, bucket, between=lambda b, i: choices(0) if b == 15 else None)
            router(NB - 2)
            y_T(NB - 1, (NB - 1) % 2)
            router(NB - 1)

            choices(1)

            def rows_T(r, a, i):
                pe.wait_ge(s_expert_rows_loaded[a], (i + 1) * 16)
                after(pe, s_z_T_scaled, r * KC)
                for c in range(KC):
                    last = t.transpose(ps_t[:, c * TR:(c + 1) * TR], row_in[:, a, c * 128:(c + 1) * 128], ident[:, :])
                last.then_inc(s_z_T, 1)

            def hidden(r, a, e):
                pe.wait_ge(s_z_T_scaled, (r + 1) * KC)
                after(pe, s_expert_hidden_biased, r - 1)
                for c in range(KC):
                    last = t.matmul(ps_acc[a][:, :], zT[:, a, c, :], W1_all[:, bass.ds(e * (KC * HID) + c * HID, HID)],
                                    start=(c == 0), stop=(c == KC - 1))
                last.then_inc(s_expert_hidden, 1)

            def gelu_T(r, a):
                pe.wait_ge(s_gelu_done, r + 1)
                after(pe, s_gelu_T_kept, r - 1)
                for c in range(HC):
                    last = t.transpose(ps_g[a][:, c * TR:(c + 1) * TR], hg[:, a, c * 128:(c + 1) * 128], ident[:, :])
                last.then_inc(s_gelu_T, 1)

            def outputs(r, a, e):
                pe.wait_ge(s_gelu_T_kept, r + 1)
                after(pe, s_expert_biased, r - 1)
                for c in range(HC):
                    last = t.matmul(ps_y[a][:, 0:D], hgT[:, a, c, :], W2_all[:, bass.ds(e * (HC * D) + c * D, D)],
                                    start=(c == 0), stop=(c == HC - 1))
                last.then_inc(s_expert_multiplied, 1)

            def expert_tile(r, a, i, e):
                hidden(r + 1, 1 - a, e[1])
                rows_T(r + 2, a, i + 1)
                outputs(r, a, e[0])
                gelu_T(r + 1, 1 - a)

            pe.wait_ge(s_routed, 2)
            pe.wait_ge(s_expert_weights_loaded, (KC + HC + 1) * 16)
            load = experts_of(mybir.EngineType.PE)
            for h in range(HALVES):
                first = h * ETH
                rows_T(first, 0, h * TP)
                rows_T(first + 1, 1, h * TP)
                hidden(first, 0, load(h * TP)[0])
                gelu_T(first, 0)
                tile_pairs(pe, h, expert_tile, load)
                e = load(h * TP + TP - 1)
                hidden(first + ETH - 1, 1, e[1])
                outputs(first + ETH - 2, 0, e[0])
                gelu_T(first + ETH - 1, 1)
                outputs(first + ETH - 1, 1, e[1])


_INS = ["x", "src", "edge_attr_64", "L0_gnn_u", "L0_gnn_W1", "L0_gnn_b1", "L0_gnn_W2", "L0_gnn_b2",
        "L0_mix_wq", "L0_mix_wk", "L0_mix_wv", "L0_mix_wo", "L0_mix_bo",
        "L0_mix_ln_k_g", "L0_mix_ln_k_b", "L0_mix_ln_v_g", "L0_mix_ln_v_b",
        "L0_ffn_gamma", "L0_ffn_beta", "L0_ffn_Wr", "L0_ffn_br", "L0_ffn_W1", "L0_ffn_b1", "L0_ffn_W2", "L0_ffn_b2"]


def kernel(**inputs):
    import numpy as _np
    import concourse.bacc as _bacc
    from concourse import mybir as _mybir
    from concourse.bass_utils import run_bass_kernel_spmd as _run

    nc = _bacc.Bacc("TRN2", target_bir_lowering=False, num_devices=1)
    arrays, args = {}, []
    for name in _INS:
        a = _np.ascontiguousarray(inputs[name])
        arrays[f"in_{name}_dram"] = a
        args.append(nc.dram_tensor(f"in_{name}_dram", a.shape, _mybir.dt.from_np(a.dtype), kind="ExternalInput").ap())
    args.append(nc.dram_tensor("out_0_dram", (N, D), F32, kind="ExternalOutput").ap())
    args.append(nc.dram_tensor("buckets", (SEGS * SEG_ROWS, ROW), F32, kind="Internal").ap())
    args.append(nc.dram_tensor("x1", (N, D), F32, kind="Internal").ap())
    for name in ("sorted_y", "expert_out"):
        args.append([nc.dram_tensor(f"{name}{h}", (ETH * TR, D), F32, kind="Internal").ap() for h in range(HALVES)])
    build(nc, *args)
    r = _run(nc, [arrays], core_ids=[0])
    return r.results[0]["out_0_dram"]
```
